# Optimizing a Trainium2 kernel written in Bass

```python
import numpy as np
import jax
import jax.numpy as jnp

def _softmax(x, axis=-1):
    return jax.nn.softmax(x, axis=axis)

def _gelu(x):
    return jax.nn.gelu(x, approximate=True)

def _silu(x):
    return jax.nn.silu(x)

def _sigmoid(x):
    return jax.nn.sigmoid(x)

def _layernorm(x, axis=-1, eps=1e-05):
    m = jnp.mean(x, axis=axis, keepdims=True)
    v = jnp.var(x, axis=axis, keepdims=True)
    return (x - m) / jnp.sqrt(v + eps)

def _scatter_add(tgt, idx, src, axis=0):
    return tgt.at[idx].add(src)

def _segment_sum(src, seg, n):
    return jax.ops.segment_sum(src, seg, n)
kernel_name = 'mk_seq_preln_d2_jaxref_r4_75cbcf'

def setup_inputs(seed: int=0):
    np.random.seed(seed)
    _w = jnp.asarray

    def _L0_attn_setup():
        import jax, jax.numpy as jnp
        import numpy as np
        B, L = (4, 512)
        D_MODEL, D_STATE, D_CONV, EXPAND = (256, 16, 4, 2)
        D_INNER = D_MODEL * EXPAND

        def _silu(v):
            return v * jax.nn.sigmoid(v)
        key = jax.random.key(seed)
        ks = jax.random.split(key, 6)
        x = jax.random.normal(ks[0], (B, L, D_MODEL), dtype=jnp.float32)
        W_in = jax.random.normal(ks[1], (D_MODEL, 2 * D_INNER), dtype=jnp.float32) / np.sqrt(D_MODEL)
        conv_w = jax.random.normal(ks[2], (D_INNER, D_CONV), dtype=jnp.float32) / np.sqrt(D_CONV)
        conv_b = jax.random.normal(ks[3], (D_INNER,), dtype=jnp.float32) * 0.02
        W_x = jax.random.normal(ks[4], (D_INNER, 2 * D_STATE + 1), dtype=jnp.float32) / np.sqrt(D_INNER)
        A_log = jnp.log(jnp.arange(1, D_STATE + 1, dtype=jnp.float32))
        D_param = jnp.ones((D_INNER,), dtype=jnp.float32)
        W_out = jax.random.normal(ks[5], (D_INNER, D_MODEL), dtype=jnp.float32) / np.sqrt(D_INNER)
        return {'x': x, 'W_in': W_in, 'conv_w': conv_w, 'conv_b': conv_b, 'W_x': W_x, 'A_log': A_log, 'D_param': D_param, 'W_out': W_out}
    _L0_attn_in = _L0_attn_setup()

    def _L0_ffn_setup():
        import jax, jax.numpy as jnp
        import numpy as np
        DM, NE, ES, ESZ = (256, 16, 4, 64)
        BATCH, SEQ = (8, 512)
        key = jax.random.key(seed)
        k = jax.random.split(key, 5)
        scale = 0.02
        return {'x': jax.random.normal(k[0], (BATCH, SEQ, DM), dtype=jnp.float32), 'controller': jax.random.normal(k[1], (DM, NE, ES), dtype=jnp.float32) * scale, 'f1': jax.random.normal(k[2], (DM, NE, ES, ESZ), dtype=jnp.float32) * scale, 'f2': jax.random.normal(k[3], (NE, ES, ESZ, DM), dtype=jnp.float32) * scale, 'bias': jax.random.normal(k[4], (NE, ES, ESZ), dtype=jnp.float32) * scale}
    _L0_ffn_in = _L0_ffn_setup()

    def _L1_attn_setup():
        import jax, jax.numpy as jnp
        import numpy as np
        import math
        HIDDEN = 256
        HEADS = 16
        HEAD_DIM = HIDDEN // HEADS
        NUM_FEATURES = 64
        B, N = (4, 1024)

        def _feature_map(x, rf):
            proj = jnp.einsum('bhnd,fd->bhnf', x, rf) / jnp.sqrt(jnp.float32(NUM_FEATURES))
            norm = jnp.linalg.norm(x, axis=-1, keepdims=True)
            return jnp.exp(proj - norm)
        key = jax.random.key(seed)
        ks = jax.random.split(key, 5)
        x = jax.random.normal(ks[0], (B, N, HIDDEN), dtype=jnp.float32)
        w_qkv = jax.random.normal(ks[1], (3 * HIDDEN, HIDDEN), dtype=jnp.float32) / math.sqrt(HIDDEN)
        w_out = jax.random.normal(ks[2], (HIDDEN, HIDDEN), dtype=jnp.float32) / math.sqrt(HIDDEN)
        b_out = jnp.zeros((HIDDEN,), dtype=jnp.float32)
        random_features = jax.random.normal(ks[3], (NUM_FEATURES, HEAD_DIM), dtype=jnp.float32)
        return {'x': x, 'w_qkv': w_qkv, 'w_out': w_out, 'b_out': b_out, 'random_features': random_features}
    _L1_attn_in = _L1_attn_setup()

    def _L1_ffn_setup():
        import jax, jax.numpy as jnp
        import numpy as np
        B, S, H, E = (4, 512, 256, 8)
        key = jax.random.key(seed)
        k1, k2, k3 = jax.random.split(key, 3)
        scale_w = 1.0 / np.sqrt(H)
        return {'x': jax.random.normal(k1, (B, S, H), dtype=jnp.float32), 'router_w': jax.random.normal(k2, (H, E), dtype=jnp.float32) * scale_w, 'router_b': jnp.zeros((E,), dtype=jnp.float32), 'expert_w': jax.random.normal(k3, (E, H, H), dtype=jnp.float32) * scale_w, 'expert_b': jnp.zeros((E, H), dtype=jnp.float32)}
    _L1_ffn_in = _L1_ffn_setup()
    _d = {'L0_attn_x': _L0_attn_in['x'], 'L0_attn_W_in': _L0_attn_in['W_in'], 'L0_attn_conv_w': _L0_attn_in['conv_w'], 'L0_attn_conv_b': _L0_attn_in['conv_b'], 'L0_attn_W_x': _L0_attn_in['W_x'], 'L0_attn_A_log': _L0_attn_in['A_log'], 'L0_attn_D_param': _L0_attn_in['D_param'], 'L0_attn_W_out': _L0_attn_in['W_out'], 'L0_ffn_controller': _L0_ffn_in['controller'], 'L0_ffn_f1': _L0_ffn_in['f1'], 'L0_ffn_f2': _L0_ffn_in['f2'], 'L0_ffn_bias': _L0_ffn_in['bias'], 'L1_attn_w_qkv': _L1_attn_in['w_qkv'], 'L1_attn_w_out': _L1_attn_in['w_out'], 'L1_attn_b_out': _L1_attn_in['b_out'], 'L1_attn_random_features': _L1_attn_in['random_features'], 'L1_ffn_router_w': _L1_ffn_in['router_w'], 'L1_ffn_router_b': _L1_ffn_in['router_b'], 'L1_ffn_expert_w': _L1_ffn_in['expert_w'], 'L1_ffn_expert_b': _L1_ffn_in['expert_b']}
    _x0 = _d['L0_attn_x']
    _d['L0_attn_x'] = jax.random.normal(jax.random.fold_in(jax.random.key(seed), 1), (4, 1024, 256), dtype=_x0.dtype)
    del _x0
    return _d

def reference(L0_attn_x, L0_attn_W_in, L0_attn_conv_w, L0_attn_conv_b, L0_attn_W_x, L0_attn_A_log, L0_attn_D_param, L0_attn_W_out, L0_ffn_controller, L0_ffn_f1, L0_ffn_f2, L0_ffn_bias, L1_attn_w_qkv, L1_attn_w_out, L1_attn_b_out, L1_attn_random_features, L1_ffn_router_w, L1_ffn_router_b, L1_ffn_expert_w, L1_ffn_expert_b):

    def _L0_attn_ref(x, W_in, conv_w, conv_b, W_x, A_log, D_param, W_out):
        import jax, jax.numpy as jnp
        import numpy as np
        B, L = (4, 512)
        D_MODEL, D_STATE, D_CONV, EXPAND = (256, 16, 4, 2)
        D_INNER = D_MODEL * EXPAND

        def _silu(v):
            return v * jax.nn.sigmoid(v)
        b, l, _ = x.shape
        xz = x @ W_in
        x_ssm, z = jnp.split(xz, 2, axis=-1)
        xp = jnp.pad(x_ssm, ((0, 0), (D_CONV - 1, 0), (0, 0)))
        xc = conv_b
        for k in range(D_CONV):
            xc = xc + xp[:, k:k + l, :] * conv_w[:, k]
        xc = _silu(xc)
        x_dbl = xc @ W_x
        delta = jax.nn.softplus(x_dbl[..., :1])
        B_mat = x_dbl[..., 1:1 + D_STATE]
        C_mat = x_dbl[..., 1 + D_STATE:]
        A = -jnp.exp(A_log)
        A_bar = jnp.exp(delta * A)
        B_bar = delta * B_mat

        def step(h, inp):
            a, bb, xt, ct = inp
            h = a[:, None, :] * h + bb[:, None, :] * xt[:, :, None]
            y = jnp.einsum('bdn,bn->bd', h, ct)
            return (h, y)
        h0 = jnp.zeros((b, D_INNER, D_STATE), dtype=x.dtype)
        seq = (jnp.swapaxes(A_bar, 0, 1), jnp.swapaxes(B_bar, 0, 1), jnp.swapaxes(xc, 0, 1), jnp.swapaxes(C_mat, 0, 1))
        _, ys = jax.lax.scan(step, h0, seq)
        y = jnp.swapaxes(ys, 0, 1)
        y = y + xc * D_param
        y = y * _silu(z)
        return y @ W_out

    def _L0_ffn_ref(x, controller, f1, f2, bias):
        import jax, jax.numpy as jnp
        import numpy as np
        DM, NE, ES, ESZ = (256, 16, 4, 64)
        BATCH, SEQ = (8, 512)
        ne = controller.shape[1]
        d = x.shape[-1]
        grouped = x.reshape(x.shape[:-2] + (-1, ne, d))
        logits = jnp.einsum('...btd,des->...btes', grouped, controller)
        tie = jnp.linspace(0.0, 1e-06, ne, dtype=logits.dtype).reshape(ne, 1, 1)
        logits = logits + tie
        perm = (logits == jnp.max(logits, axis=-3, keepdims=True)).astype(x.dtype)
        sel = jnp.einsum('...btd,...btes->...besd', grouped, perm)
        inner = jax.nn.relu(jnp.einsum('...besd,desf->...besf', sel, f1) + bias)
        inter = jnp.einsum('...besf,esfd->...besd', inner, f2)
        out = jnp.einsum('...besd,...btes->...btd', inter, perm)
        return out.reshape(x.shape)

    def _L1_attn_ref(x, w_qkv, w_out, b_out, random_features):
        import jax, jax.numpy as jnp
        import numpy as np
        import math
        HIDDEN = 256
        HEADS = 16
        HEAD_DIM = HIDDEN // HEADS
        NUM_FEATURES = 64
        B, N = (4, 1024)

        def _feature_map(x, rf):
            proj = jnp.einsum('bhnd,fd->bhnf', x, rf) / jnp.sqrt(jnp.float32(NUM_FEATURES))
            norm = jnp.linalg.norm(x, axis=-1, keepdims=True)
            return jnp.exp(proj - norm)
        b, n, _ = x.shape
        qkv = jnp.einsum('bnh,oh->bno', x, w_qkv)
        qkv = qkv.reshape(b, n, 3, HEADS, HEAD_DIM)
        qkv = jnp.transpose(qkv, (2, 0, 3, 1, 4))
        q, k, v = (qkv[0], qkv[1], qkv[2])
        q_prime = _feature_map(q, random_features)
        k_prime = _feature_map(k, random_features)
        kv = jnp.einsum('bhnf,bhnd->bhfd', k_prime, v)
        normalizer = jnp.einsum('bhnf,bhf->bhn', q_prime, k_prime.sum(axis=2))
        out = jnp.einsum('bhnf,bhfd->bhnd', q_prime, kv)
        out = out / (normalizer[..., None] + 1e-06)
        out = jnp.transpose(out, (0, 2, 1, 3)).reshape(b, n, HIDDEN)
        return jnp.einsum('bnh,oh->bno', out, w_out) + b_out

    def _L1_ffn_ref(x, router_w, router_b, expert_w, expert_b):
        import jax, jax.numpy as jnp
        import numpy as np
        B, S, H, E = (4, 512, 256, 8)
        b, s, h = x.shape
        xt = x.reshape(b * s, h)
        logits = xt @ router_w + router_b
        probs = jax.nn.softmax(logits, axis=-1)
        gate = jnp.max(probs, axis=-1)
        idx = jnp.argmax(probs, axis=-1)
        out_all = jnp.einsum('th,ehd->ted', xt, expert_w) + expert_b[None, :, :]
        e_out = jnp.take_along_axis(out_all, idx[:, None, None], axis=1)[:, 0, :]
        y = gate[:, None] * e_out
        return y.reshape(b, s, h)
    x = L0_attn_x
    x = x + _L0_attn_ref(_layernorm(x, axis=-1), L0_attn_W_in, L0_attn_conv_w, L0_attn_conv_b, L0_attn_W_x, L0_attn_A_log, L0_attn_D_param, L0_attn_W_out)
    x = x + _L0_ffn_ref(_layernorm(x, axis=-1), L0_ffn_controller, L0_ffn_f1, L0_ffn_f2, L0_ffn_bias)
    x = x + _L1_attn_ref(_layernorm(x, axis=-1), L1_attn_w_qkv, L1_attn_w_out, L1_attn_b_out, L1_attn_random_features)
    x = x + _L1_ffn_ref(_layernorm(x, axis=-1), L1_ffn_router_w, L1_ffn_router_b, L1_ffn_expert_w, L1_ffn_expert_b)
    return x

_drawn_inputs = setup_inputs


def setup_inputs(seed=0):
    import zlib

    import numpy as np

    out = dict(_drawn_inputs(seed))
    spreads = {'L0_attn_D_param': (1.0, 0.2),
     'L1_attn_b_out': (0.0, 0.1),
     'L1_ffn_router_b': (0.0, 0.1),
     'L1_ffn_expert_b': (0.0, 0.1)}
    factors = {'L0_ffn_bias': 3.349, 'L1_attn_random_features': 3.561}
    for name, (base, spread) in spreads.items():
        noise = np.random.default_rng([zlib.crc32(name.encode()), seed]).standard_normal(out[name].shape)
        drawn = base * np.exp(spread * noise) if base else spread * noise
        out[name] = jnp.asarray(drawn.astype(out[name].dtype))
    for name, factor in factors.items():
        out[name] = (out[name] * factor).astype(out[name].dtype)
    return out
```

```python
from contextlib import ExitStack

import concourse.bass as bass
import numpy as np
from concourse import mybir

ALU = mybir.AluOpType
ACT = mybir.ActivationFunctionType
AX = mybir.AxisListType
F32 = mybir.dt.float32
ds = bass.ds

P = 128
B, L, D = 4, 1024, 256
TOKENS = B * L
CHUNKS = TOKENS // P
TILE = 4
TW = TILE * P
TILES = CHUNKS // TILE
KD = D // P
HALVES = L // TW
EPS = 1e-5
DI, NS, TAPS = 512, 16, 4
KI = DI // P
Q = 16
NB = P // Q
XD = 1 + 2 * NS
GRP = 16
ES, FF = 64, 64
GC = P // GRP
GROUPS = TOKENS // GRP
PAIRS = ES // 2
HEADS, HD, NF = 16, 16, 64
HP = HEADS // 2
HEADS_OF = [range(0, 6), range(6, 12), range(12, 16)]
NORM_ROW = [96, 96, 64]
VW = HD + 1
NE = 8


def shape_constants():
    p = np.arange(P)
    parts = {
        "ident": np.eye(P),
        "sel_delta": np.repeat((p == 0)[:, None], P, 1),
        "sel_b": (p[:, None] == 1 + p[None, :] % NS),
        "sel_c": (p[:, None] == 1 + NS + p[None, :] % NS),
        "place_n": np.repeat((p[:, None] % Q) == np.arange(Q)[None, :], NS, 1),
        "place": (p[:, None] % Q) == np.arange(Q)[None, :],
        "same_block": (p[:, None] // Q) == (p[None, :] // Q),
        "earlier_block": (p[:, None] // Q) < (p[None, :] // Q),
        "own_block_causal": ((p[:, None] // Q) == (p[None, :] // Q)) & (p[None, :] >= p[:, None]),
        "ref_of": (p[:, None] // NS - 1) == np.arange(NB)[None, :],
        "block_of_state": (p[:, None] // NS) == (p[None, :] // Q),
        "scan_keep": np.repeat((np.arange(TW) % P != 0)[None, :], P, 0),
        "tie": np.repeat(np.linspace(0.0, 1e-6, GRP, dtype=np.float32)[None, :], P, 0),
        "group_of": (p[:, None] // GRP) == np.arange(GC)[None, :],
        "parity": (p[:, None] // ES) == ((p[None, :] // GRP) % 2),
        "eps": np.full((P, 1), EPS),
        "head_of": (p[:, None] // HD) == np.arange(6)[None, :],
        "minus_half": np.full((P, 1), -0.5),
        "rank": np.repeat(np.arange(NE, 0, -1)[None, :], P, 0),
    }
    at, n = {}, 0
    for k, v in parts.items():
        at[k] = (n, n + v.shape[1])
        n += v.shape[1]
    return np.concatenate([v.astype(np.float32) for v in parts.values()], 1), at


PRIME = 16


class Signal:

    def __init__(self, sem, per):
        self.sem, self.per = sem, per

    def inc(self, instruction):
        instruction.then_inc(self.sem, 1)

    def at(self, i, n):
        return i * self.per + n + PRIME


def build(nc, a, out, consts, at, scratch, phases):
    with ExitStack() as ctx:
        kept = dict(
            X=ctx.enter_context(nc.sbuf_tensor("X", [P, CHUNKS, D], F32)),
            C=ctx.enter_context(nc.sbuf_tensor("consts", [P, consts.shape[1]], F32)),
            ps=ctx.enter_context(nc.psum_tensor("ps", [P, 8, 512], F32)),
            mv=ctx.enter_context(nc.sbuf_tensor("mean_var", [P, TILE, 2], F32)),
            st=ctx.enter_context(nc.sbuf_tensor("stats", [P, TILE, 6], F32)),
            carrier=ctx.enter_context(nc.sbuf_tensor("carrier", [P, 1], F32)),
            ve=ctx.enter_context(nc.sbuf_tensor("var_eps", [P, TILE], F32)),
            rstd=ctx.enter_context(nc.sbuf_tensor("rstd", [P, TILE], F32)),
            xn=ctx.enter_context(nc.sbuf_tensor("xn", [P, TILE, D], F32)),
            xnT=ctx.enter_context(nc.sbuf_tensor("xnT", [P, KD, TW], F32)),
        )

        def const(name, rows=P):
            lo, hi = at[name]
            return kept["C"][0:rows, lo:hi]

        mamba(nc, a, consts, kept, const)
        if phases >= 2:
            sparse_ffn(nc, a, kept, const, scratch)
        if phases >= 3:
            attention(nc, a, kept, const)
        if phases >= 4:
            experts(nc, a, kept, const)
        stored = ctx.enter_context(nc.semaphore("stored"))
        with nc.Block() as block:

            @block.sync
            def _(sp):
                o = out.rearrange("b (c p) d -> p (b c) d", p=P)
                for i in range(TILES):
                    sp.dma_start(o[:, TILE * i:TILE * (i + 1)],
                                 kept["X"][:, TILE * i:TILE * (i + 1)]).then_inc(stored, 16)
                sp.wait_ge(stored, 16 * TILES)


def prime(eng, S, *norms):
    for s in [*S.values(), *(x for n in norms for x in (n.stats, n.mv, n.ve, n.rstd, n.xn, n.turned, n.xnT))]:
        eng.sem_inc(s.sem, PRIME)


class Norm:

    def __init__(self, name, sem, kept, const):
        self.k, self.const = kept, const
        self.stats = Signal(sem(f"{name}_stats"), TILE)
        self.mv = Signal(sem(f"{name}_mean_var"), TILE)
        self.ve = Signal(sem(f"{name}_var_eps"), 1)
        self.rstd = Signal(sem(f"{name}_rstd"), 1)
        self.xn = Signal(sem(f"{name}_xn"), TILE)
        self.turned = Signal(sem(f"{name}_xn_turned"), KD)
        self.xnT = Signal(sem(f"{name}_xnT"), KD)

    def vector_stats(self, dve, i):
        k = self.k
        for c in range(TILE):
            self.stats.inc(dve.bn_stats(k["st"][:, c:c + 1, :], k["X"][:, ds(i * TILE + c, 1), :]))
        dve.wait_ge(self.stats.sem, self.stats.at(i, TILE))
        dve.wait_ge(self.ve.sem, self.ve.at(i, 0))
        dve.wait_ge(self.xn.sem, self.xn.at(i, 0))
        dve.tensor_copy(k["carrier"][:, :], k["st"][:, 0, 0:1])
        for c in range(TILE):
            self.mv.inc(dve.bn_aggr(k["mv"][:, c, :], k["st"][:, c, :]))

    def gpsimd_rstd(self, pool, i):
        k = self.k
        pool.wait_ge(self.mv.sem, self.mv.at(i, TILE))
        pool.wait_ge(self.xn.sem, self.xn.at(i, 0))
        self.ve.inc(pool.tensor_tensor(k["ve"][:, :], k["mv"][:, :, 1],
                                       self.const("eps").to_broadcast([P, TILE]), ALU.add))
        pool.wait_ge(self.ve.sem, self.ve.at(i, 1))
        self.rstd.inc(pool.tensor_tensor(k["rstd"][:, :], k["ve"][:, :],
                                         self.const("minus_half").to_broadcast([P, TILE]), ALU.pow))

    def vector_apply(self, dve, i):
        k = self.k
        dve.wait_ge(self.rstd.sem, self.rstd.at(i, 1))
        dve.wait_ge(self.turned.sem, self.turned.at(i, 0))
        for c in range(TILE):
            self.xn.inc(dve.tensor_scalar(k["xn"][:, c:c + 1, :], k["X"][:, ds(i * TILE + c, 1), :],
                                          k["mv"][:, c, 0:1], k["rstd"][:, c:c + 1],
                                          ALU.subtract, ALU.mult))

    def tensor_turn(self, pe, i, banks):
        k = self.k
        pe.wait_ge(self.xn.sem, self.xn.at(i, TILE))
        pe.wait_ge(self.xnT.sem, self.xnT.at(i, 0))
        for d in range(KD):
            for c in range(TILE):
                t = pe.transpose(k["ps"][:, banks + d, c * P:(c + 1) * P],
                                 k["xn"][:, c, d * P:(d + 1) * P], self.const("ident"))
            self.turned.inc(t)

    def scalar_copy(self, act, i, banks):
        k = self.k
        for d in range(KD):
            act.wait_ge(self.turned.sem, self.turned.at(i, d + 1))
            self.xnT.inc(act.copy(k["xnT"][:, d, :], k["ps"][:, banks + d, :]))


def mamba(nc, a, consts, kept, const):
    sems = []
    with ExitStack() as ctx:
        def sb(name, shape):
            return ctx.enter_context(nc.sbuf_tensor(name, shape, F32))

        def sem(name):
            sems.append(nc.alloc_semaphore(name))
            return sems[-1]

        X, ps = kept["X"], kept["ps"]
        w_in = sb("w_in", [P, KD, 2 * DI])
        w_x = sb("w_x", [P, KI, XD])
        w_out = sb("w_out", [P, KI, D])
        conv_w = sb("conv_w", [P, KI, TAPS])
        conv_b = sb("conv_b", [P, KI])
        d_skip = sb("d_skip", [P, KI])
        a_col = sb("a_col", [P, 1])
        a_neg = sb("a_neg", [P, 1])
        a_row = sb("a_row", [P, NS])
        xpad = sb("xpad", [P, KI, TAPS - 1 + TW])
        acc = sb("acc", [P, KI, TW])
        xcT = sb("xcT", [P, KI, TW])
        zs = sb("zs", [P, KI, TW])
        xd = sb("xd", [XD, TW])
        soft = sb("soft", [P, TW])
        delta = sb("delta", [P, TW])
        run = sb("run", [P, TW])
        bd = sb("bd", [P, TW])
        refs8 = sb("refs8", [P, TILE, NB])
        ref = sb("ref", [P, TILE])
        a2 = sb("a2", [P, TW])
        a1 = sb("a1", [P, TW])
        f2 = sb("f2", [P, TW])
        f1p = sb("f1p", [P, TW])
        f1 = sb("f1", [P, TW])
        TOKC = TILE * (XD + 32 + 32)
        tok = sb("tok", [P, TOKC])
        tok_x = tok[:, 0:TILE * XD].rearrange("p (c k) -> p c k", c=TILE)
        tok_d = tok[:, TILE * XD:TILE * (XD + 32)].rearrange("p (c k) -> p c k", c=TILE)
        tok_b = tok[:, TILE * (XD + 32):TOKC].rearrange("p (c k) -> p c k", c=TILE)
        cm = sb("cm", [P, TILE, Q * NS + Q])
        a3 = sb("a3", [P, TILE, Q])
        big = sb("big", [P, TILE, Q * NS])
        md = sb("md", [P, TILE, Q])
        mdx = sb("mdx", [P, TILE, P])
        mt = sb("mt", [P, TILE, P])
        wd = sb("wd", [P, TILE])
        w2a = sb("w2a", [P, TILE, NS])
        w2 = sb("w2", [P, TILE, NS])
        xtok = sb("xtok", [P, TILE, DI])
        h = sb("h", [NS, 2, DI])
        y = sb("y", [P, KI, TW])

        x_in, w_loaded = sem("x_in"), sem("w_loaded")
        a_abs, a_ready = sem("a_abs"), sem("a_ready")
        nrm = Norm("m", sem, kept, const)
        S = {}
        for name, per in dict(xz=2 * KI, xpad=KI, zs=KI, cleared=1, conv=TAPS * KI, hist=1, xc=KI, xdT=1,
                              xd=1, rep=3, soft=3, delta=1, run=1, bd=1, refs8=1, ref=1, a2=TILE,
                              a1=TILE, e2=1, e1=1, f2=1, f1p=1, f1=1, tokp=1, tok=1, cm=2, crep=1,
                              a3=TILE, ah=1, eh=1, g1=1, g2=1, md=1, mdx=1, off=1, mt0=1, mt=1, wd=1,
                              w2a=1, w2e=1, w2=1, xtp=TILE, xt=TILE, y=TILE, hc=TILE, h=TILE,
                              ys=KI, yg=1, o=2, res=2).items():
            S[name] = Signal(sem(f"m_{name}"), per)

        def done(eng, name, i, n=None):
            s = S[name]
            eng.wait_ge(s.sem, s.at(i, s.per if n is None else n))

        with nc.Block() as block:

            @block.sync
            def _(sp):
                xin = a["L0_attn_x"].rearrange("b (c p) d -> p (b c) d", p=P)
                sp.dma_start(kept["C"][:, :], consts).then_inc(w_loaded, 16)
                for t in range(TILES):
                    sp.dma_start(X[:, TILE * t:TILE * (t + 1)], xin[:, TILE * t:TILE * (t + 1)]).then_inc(x_in, 16)
                for dst, src in (
                    (w_in[:, :, :], a["L0_attn_W_in"].rearrange("(k p) n -> p k n", p=P)),
                    (w_x[:, :, :], a["L0_attn_W_x"].rearrange("(k p) n -> p k n", p=P)),
                    (w_out[:, :, :], a["L0_attn_W_out"].rearrange("(k p) n -> p k n", p=P)),
                    (conv_w[:, :, :], a["L0_attn_conv_w"].rearrange("(k p) n -> p k n", p=P)),
                    (conv_b[:, :], a["conv_b_cols"]),
                    (d_skip[:, :], a["d_cols"]),
                    (a_row[:, :], a["L0_attn_A_log"].rearrange("(o n) -> o n", o=1).to_broadcast([P, NS])),
                ):
                    sp.dma_start(dst, src).then_inc(w_loaded, 16)
                for b in range(NB):
                    sp.dma_start(a_col[b * NS:(b + 1) * NS, :],
                                 a["L0_attn_A_log"].rearrange("(n o) -> n o", o=1)).then_inc(w_loaded, 16)
                prime(sp, {k: v for k, v in S.items() if k != "cleared"}, nrm)

            W_LOADS = 16 * (8 + NB)

            @block.gpsimd
            def _(pool):
                pool.wait_ge(w_loaded, W_LOADS)
                with pool.Fori(0, TILES) as i:
                    nrm.gpsimd_rstd(pool, i)
                    done(pool, "tok", i)
                    done(pool, "crep", i, 0)
                    for v in range(1):
                        S["cm"].inc(pool.tensor_tensor(
                            cm[:, :, 0:Q * NS].rearrange("p c (t n) -> p c t n", n=NS),
                            tok_x[:, :, 1 + NS:XD].unsqueeze(2).to_broadcast([P, TILE, Q, NS]),
                            const("place_n").rearrange("p (t n) -> p t n", n=NS).unsqueeze(1).to_broadcast([P, TILE, Q, NS]),
                            ALU.mult))
                    S["cm"].inc(pool.tensor_tensor(
                        cm[:, :, Q * NS:], tok_d[:, :, 0:1].to_broadcast([P, TILE, Q]),
                        const("place").unsqueeze(1).to_broadcast([P, TILE, Q]), ALU.mult))

            @block.scalar
            def _(act):
                act.wait_ge(w_loaded, W_LOADS)
                act.activation(a_col[:, :], a_col[:, :], ACT.Exp).then_inc(a_abs, 1)
                act.activation(a_row[:, :], a_row[:, :], ACT.Exp).then_inc(a_abs, 1)
                act.wait_ge(a_abs, 2)
                act.mul(a_neg[:, :], a_col[:, :], -1.0).then_inc(a_ready, 1)
                act.mul(a_row[:, :], a_row[:, :], -1.0).then_inc(a_ready, 1)
                act.wait_ge(a_ready, 2)
                with act.Fori(0, TILES) as i:
                    nrm.scalar_copy(act, i, 0)
                    for m in range(2 * KI):
                        done(act, "xz", i, m + 1)
                        if m < KI:
                            if m == 0:
                                done(act, "hist", i, 0)
                                act.wait_ge(S["cleared"].sem, 1 + i)
                            S["xpad"].inc(act.copy(xpad[:, m, TAPS - 1:], ps[:, 2 + m % 2, :]))
                        else:
                            if m == KI:
                                done(act, "yg", i, 0)
                            S["zs"].inc(act.activation(zs[:, m - KI, :], ps[:, 2 + m % 2, :], ACT.Silu))
                    done(act, "y", i, 0)
                    for m in range(KI):
                        done(act, "conv", i, KI * (TAPS - 1) + m + 1)
                        S["xc"].inc(act.activation(xcT[:, m, :], acc[:, m, :], ACT.Silu))
                    done(act, "xdT", i)
                    done(act, "tokp", i, 0)
                    done(act, "rep", i, 0)
                    S["xd"].inc(act.copy(xd[:, :], ps[0:XD, 4, :]))
                    done(act, "rep", i, 1)
                    done(act, "delta", i, 0)
                    S["soft"].inc(act.activation(soft[:, :], ps[:, 5, :], ACT.Abs))
                    done(act, "soft", i, 1)
                    S["soft"].inc(act.activation(soft[:, :], soft[:, :], ACT.Exp, scale=-1.0))
                    done(act, "soft", i, 2)
                    S["soft"].inc(act.activation(soft[:, :], soft[:, :], ACT.Ln, bias=1.0))
                    done(act, "tokp", i)
                    done(act, "w2", i, 0)
                    done(act, "cm", i, 0)
                    done(act, "g2", i, 0)
                    S["tok"].inc(act.copy(tok[:, :], ps[:, 4, 0:TOKC]))
                    done(act, "a2", i)
                    S["e2"].inc(act.activation(a2[:, :], a2[:, :], ACT.Exp, scale=a_col[:, :]))
                    done(act, "a1", i)
                    S["e1"].inc(act.activation(a1[:, :], a1[:, :], ACT.Exp, scale=a_neg[:, :]))
                    for c in range(TILE):
                        done(act, "xtp", i, c + 1)
                        S["xt"].inc(act.copy(xtok[:, c, :], ps[:, 6 + c % 2, :]))
                    done(act, "ah", i)
                    S["eh"].inc(act.activation(big[:, :, :], big[:, :, :], ACT.Exp))
                    done(act, "w2a", i)
                    S["w2e"].inc(act.activation(w2a[:, :, :], w2a[:, :, :], ACT.Exp))

            @block.vector
            def _(dve):
                hist = xpad[:, :, 0:TAPS - 1]
                dve.memset(hist, 0.0).then_inc(S["cleared"].sem, 1)
                dve.wait_ge(w_loaded, W_LOADS)
                dve.wait_ge(a_ready, 2)
                dve.wait_ge(x_in, 16 * TILES)
                with dve.Fori(0, B) as b:
                    for half in range(HALVES):
                        i = b * HALVES + half
                        nrm.vector_stats(dve, i)
                        nrm.vector_apply(dve, i)
                        done(dve, "xc", i, 0)
                        for k in range(TAPS):
                            for m in range(KI):
                                if k == 0:
                                    done(dve, "xpad", i, m + 1)
                                    ins = dve.tensor_scalar(acc[:, m, :], xpad[:, m, TAPS - 1:], conv_w[:, m, TAPS - 1:],
                                                            conv_b[:, m:m + 1], ALU.mult, ALU.add)
                                else:
                                    done(dve, "conv", i, KI * (k - 1) + m + 1)
                                    ins = dve.scalar_tensor_tensor(acc[:, m, :], xpad[:, m, k - 1:k - 1 + TW],
                                                                   conv_w[:, m, k - 1:k], acc[:, m, :],
                                                                   ALU.mult, ALU.add)
                                S["conv"].inc(ins)
                        done(dve, "conv", i)
                        if half < HALVES - 1:
                            S["hist"].inc(dve.tensor_copy(hist, xpad[:, :, TW:]))
                        else:
                            S["hist"].inc(dve.memset(hist, 0.0))
                        done(dve, "hist", i)
                        dve.sem_inc(S["cleared"].sem, 1)
                        done(dve, "soft", i)
                        done(dve, "run", i, 0)
                        done(dve, "bd", i, 0)
                        S["delta"].inc(dve.scalar_tensor_tensor(delta[:, :], ps[:, 5, :], 0.0, soft[:, :],
                                                                ALU.max, ALU.add))
                        done(dve, "delta", i)
                        done(dve, "wd", i, 0)
                        done(dve, "tokp", i, 0)
                        S["run"].inc(dve.tensor_tensor_scan(run[:, :], const("scan_keep"), delta[:, :], 0.0,
                                                            ALU.mult, ALU.add))
                        done(dve, "rep", i, 2)
                        S["bd"].inc(dve.tensor_tensor(bd[:, :], delta[:, :], ps[:, 6, :], ALU.mult))
                        done(dve, "run", i)
                        S["refs8"].inc(dve.tensor_tensor(
                            refs8[:, :, :], run[:, :].rearrange("p (c b q) -> p c b q", c=TILE, q=Q)[:, :, :, Q - 1],
                            const("ref_of").unsqueeze(1).to_broadcast([P, TILE, NB]), ALU.mult))
                        done(dve, "refs8", i)
                        S["ref"].inc(dve.tensor_reduce(ref[:, :], refs8[:, :, :], AX.X, ALU.add))
                        done(dve, "ref", i)
                        for c in range(TILE):
                            S["a2"].inc(dve.tensor_scalar(a2[:, c * P:(c + 1) * P], run[:, c * P:(c + 1) * P],
                                                          ref[:, c:c + 1], 0.0, ALU.subtract, ALU.min))
                        done(dve, "h", i, 0)
                        for c in range(TILE):
                            S["a1"].inc(dve.tensor_scalar(a1[:, c * P:(c + 1) * P], run[:, c * P:(c + 1) * P],
                                                          ref[:, c:c + 1], 0.0, ALU.subtract, ALU.max))
                        done(dve, "e2", i)
                        done(dve, "bd", i)
                        done(dve, "off", i, 0)
                        S["f2"].inc(dve.tensor_tensor(f2[:, :], a2[:, :], bd[:, :], ALU.mult))
                        done(dve, "e1", i)
                        done(dve, "rep", i, 3)
                        done(dve, "y", i, 0)
                        S["f1p"].inc(dve.tensor_tensor(f1p[:, :], a1[:, :], ps[:, 7, :], ALU.mult))
                        done(dve, "f1p", i)
                        S["f1"].inc(dve.tensor_tensor(
                            f1[:, :].rearrange("p (c t) -> p c t", c=TILE), f1p[:, :].rearrange("p (c t) -> p c t", c=TILE),
                            const("block_of_state").unsqueeze(1).to_broadcast([P, TILE, P]), ALU.mult))
                        done(dve, "tok", i)
                        S["wd"].inc(dve.tensor_tensor(
                            wd[:, :], run[:, :].rearrange("p (c t) -> p c t", c=TILE)[:, :, P - 1],
                            tok_d[:, :, 0], ALU.subtract))
                        done(dve, "wd", i)
                        S["w2a"].inc(dve.tensor_tensor(
                            w2a[:, :, :], wd[:, :].unsqueeze(2).to_broadcast([P, TILE, NS]),
                            a_row[:, :].unsqueeze(1).to_broadcast([P, TILE, NS]), ALU.mult))
                        done(dve, "crep", i)
                        for c in range(TILE):
                            S["a3"].inc(dve.tensor_scalar(a3[:, c, :], ps[:, c, Q * NS:Q * NS + Q],
                                                          tok_d[:, c, 0:1], 0.0, ALU.subtract, ALU.max))
                        done(dve, "a3", i)
                        S["ah"].inc(dve.tensor_tensor(
                            big[:, :, :].rearrange("p c (t n) -> p (c t) n", n=NS),
                            a3[:, :, :].rearrange("p c t -> p (c t)").unsqueeze(2).to_broadcast([P, TILE * Q, NS]),
                            a_row[:, :].unsqueeze(1).to_broadcast([P, TILE * Q, NS]), ALU.mult))
                        done(dve, "w2e", i)
                        done(dve, "hc", i, 0)
                        S["w2"].inc(dve.tensor_tensor(w2[:, :, :], w2a[:, :, :], tok_b[:, :, 0:NS], ALU.mult))
                        done(dve, "eh", i)
                        S["g1"].inc(dve.tensor_tensor(big[:, :, :], big[:, :, :], ps[:, 0:TILE, 0:Q * NS], ALU.mult))
                        done(dve, "g1", i)
                        S["g2"].inc(dve.tensor_tensor(
                            big[:, :, :].rearrange("p c (t n) -> p c t n", n=NS),
                            big[:, :, :].rearrange("p c (t n) -> p c t n", n=NS),
                            tok_b[:, :, 0:NS].unsqueeze(2).to_broadcast([P, TILE, Q, NS]), ALU.mult))
                        done(dve, "g2", i)
                        S["md"].inc(dve.tensor_reduce(md[:, :, :], big[:, :, :].rearrange("p c (t n) -> p c t n", n=NS),
                                                      AX.X, ALU.add))
                        done(dve, "md", i)
                        S["mdx"].inc(dve.tensor_tensor(
                            mdx[:, :, :].rearrange("p c (b t) -> p c b t", t=Q),
                            md[:, :, :].unsqueeze(2).to_broadcast([P, TILE, NB, Q]),
                            const("own_block_causal").rearrange("p (b t) -> p b t", t=Q).unsqueeze(1).to_broadcast([P, TILE, NB, Q]),
                            ALU.mult))
                        done(dve, "off", i)
                        done(dve, "y", i, 0)
                        S["mt0"].inc(dve.tensor_tensor(
                            mt[:, :, :], ps[:, 5, :].rearrange("p (c t) -> p c t", c=TILE),
                            const("earlier_block").unsqueeze(1).to_broadcast([P, TILE, P]), ALU.mult))
                        done(dve, "mt0", i)
                        done(dve, "mdx", i)
                        S["mt"].inc(dve.tensor_tensor(mt[:, :, :], mt[:, :, :], mdx[:, :, :], ALU.add))
                        for c in range(TILE):
                            done(dve, "hc", i, c + 1)
                            done(dve, "y", i, c)
                            if c or half:
                                S["h"].inc(dve.scalar_tensor_tensor(
                                    h[:, (c + 1) % 2, :], h[:, c % 2, :], a1[0:NS, (c + 1) * P - 1:(c + 1) * P],
                                    ps[0:NS, 4, :], ALU.mult, ALU.add))
                            else:
                                S["h"].inc(dve.tensor_copy(h[:, 1, :], ps[0:NS, 4, :]))
                            done(dve, "h", i, c + 1)
                        done(dve, "y", i)
                        for m in range(KI):
                            S["ys"].inc(dve.scalar_tensor_tensor(
                                y[:, m, :].rearrange("p (c t) -> p c t", c=TILE),
                                xcT[:, m, :].rearrange("p (c t) -> p c t", c=TILE), d_skip[:, m:m + 1],
                                ps[:, 0:TILE, m * P:(m + 1) * P], ALU.mult, ALU.add))
                        done(dve, "ys", i)
                        S["yg"].inc(dve.tensor_tensor(y[:, :, :], y[:, :, :], zs[:, :, :], ALU.mult))
                        for j in range(2):
                            done(dve, "o", i, j + 1)
                            xs = X[:, ds(i * TILE + 2 * j, 2), :]
                            S["res"].inc(dve.tensor_tensor(xs, xs, ps[:, 6 + j, :].rearrange("p (c d) -> p c d", c=2), ALU.add))
                        done(dve, "res", i)

            @block.tensor
            def _(pe):
                pe.wait_ge(w_loaded, W_LOADS)
                with pe.Fori(0, B) as b:
                    for half in range(HALVES):
                        i = b * HALVES + half
                        done(pe, "ys", i, 0)
                        nrm.tensor_turn(pe, i, 0)
                        done_xnT = nrm.xnT
                        pe.wait_ge(done_xnT.sem, done_xnT.at(i, KD))
                        for m in range(2 * KI):
                            if m >= 2:
                                done(pe, "xpad", i, min(m - 1, KI))
                                if m - 1 > KI:
                                    done(pe, "zs", i, m - 1 - KI)
                            for k in range(KD):
                                t = pe.matmul(ps[:, 2 + m % 2, :], w_in[:, k, m * P:(m + 1) * P],
                                              kept["xnT"][:, k, :], start=(k == 0), stop=(k == KD - 1))
                            S["xz"].inc(t)
                        done(pe, "xc", i)
                        done(pe, "h", i, 0)
                        for m in range(KI):
                            t = pe.matmul(ps[0:XD, 4, :], w_x[:, m, :], xcT[:, m, :], start=(m == 0), stop=(m == KI - 1))
                        S["xdT"].inc(t)
                        done(pe, "xd", i)
                        done(pe, "mt0", i, 0)
                        done(pe, "res", i, 0)
                        for j, name in enumerate(("sel_delta", "sel_b", "sel_c")):
                            S["rep"].inc(pe.matmul(ps[:, 5 + j, :], const(name, XD), xd[:, :], start=True, stop=True))
                        for c in range(TILE):
                            pe.transpose(ps[:, 4, c * XD:(c + 1) * XD], xd[:, c * P:(c + 1) * P], const("ident", XD)[:, 0:XD])
                        done(pe, "run", i)
                        done(pe, "bd", i)
                        for j, src in enumerate((run, bd)):
                            for c in range(TILE):
                                o = TILE * (XD + 32 * j) + 32 * c
                                t = pe.matmul(ps[:, 4, o:o + 32], src[:, c * P:(c + 1) * P], const("ident")[:, 0:32],
                                              start=True, stop=True)
                        S["tokp"].inc(t)
                        done(pe, "f1", i)
                        for c in range(TILE):
                            t = pe.matmul(ps[:, 5, c * P:(c + 1) * P], f2[:, c * P:(c + 1) * P],
                                          f1[:, c * P:(c + 1) * P], start=True, stop=True)
                        S["off"].inc(t)
                        for c in range(TILE):
                            if c >= 2:
                                done(pe, "xt", i, c - 1)
                            for m in range(KI):
                                t = pe.transpose(ps[:, 6 + c % 2, m * P:(m + 1) * P], xcT[:, m, c * P:(c + 1) * P], const("ident"))
                            S["xtp"].inc(t)
                        done(pe, "cm", i)
                        done(pe, "zs", i)
                        for c in range(TILE):
                            t = pe.matmul(ps[:, c, 0:Q * NS + Q], const("same_block"), cm[:, c, :], start=True, stop=True)
                        S["crep"].inc(t)
                        done(pe, "xt", i)
                        done(pe, "w2", i)
                        done(pe, "tok", i)
                        done(pe, "mt", i)
                        for c in range(TILE):
                            if c:
                                done(pe, "h", i, c)
                            first = half == 0 and c == 0
                            S["hc"].inc(pe.matmul(ps[0:NS, 4, :], w2[:, c, :], xtok[:, c, :], start=True, stop=True))
                            for m in range(KI):
                                t = pe.matmul(ps[:, c, m * P:(m + 1) * P], xtok[:, c, m * P:(m + 1) * P],
                                              mt[:, c, :], start=True, stop=first)
                                if not first:
                                    t = pe.matmul(ps[:, c, m * P:(m + 1) * P], h[:, c % 2, m * P:(m + 1) * P],
                                                  f1p[0:NS, c * P:(c + 1) * P], start=False, stop=True)
                            S["y"].inc(t)
                        done(pe, "yg", i)
                        for c in range(TILE):
                            for m in range(KI):
                                t = pe.matmul(ps[:, 6 + c // 2, (c % 2) * D:(c % 2 + 1) * D], y[:, m, c * P:(c + 1) * P],
                                              w_out[:, m, :], start=(m == 0), stop=(m == KI - 1))
                            if c % 2:
                                S["o"].inc(t)

    nc.clear_and_free_semaphores(sems)
    nc.all_engine_barrier()


def sparse_ffn(nc, a, kept, const, scratch):
    X, ps = kept["X"], kept["ps"]
    with ExitStack() as ctx:
        def sb(name, shape, dt=F32):
            return ctx.enter_context(nc.sbuf_tensor(name, shape, dt))

        def sem(name):
            return ctx.enter_context(nc.semaphore(name))

        picks = sb("picks", [P, TOKENS], mybir.dt.bfloat16)
        with ExitStack() as sel_ctx:
            selT = sel_ctx.enter_context(nc.sbuf_tensor("selT", [P, KD, ES, GROUPS], F32))
            pick_tokens(nc, a, kept, const, picks, selT)
            apply_experts(nc, a, kept, const, selT, scratch)
        scatter_tokens(nc, a, kept, picks, scratch)


def signals(sem, prefix, **per):
    return {name: Signal(sem(f"{prefix}_{name}"), n) for name, n in per.items()}


def waiter(S):
    def done(eng, name, i, n=None):
        s = S[name]
        eng.wait_ge(s.sem, s.at(i, s.per if n is None else n))
    return done


def pick_tokens(nc, a, kept, const, picks, selT):
    X, ps = kept["X"], kept["ps"]
    with ExitStack() as ctx:
        def sb(name, shape, dt=F32):
            return ctx.enter_context(nc.sbuf_tensor(name, shape, dt))

        def sem(name):
            return ctx.enter_context(nc.semaphore(name))

        ctrl = sb("ctrl", [P, KD, 2 * ES])
        lg = sb("logits", [P, TW])
        gmax = sb("gmax", [P, TW // GRP])
        one = sb("one_hot", [P, TW])
        spread = sb("spread", [P, TILE, GC, ES])
        loaded = sem("p_loaded")
        nrm = Norm("p", sem, kept, const)
        S = signals(sem, "p", lgp=1, lg=1, gmax=1, one=1, picks=1, turned=1, spread=1, gath=KD * TILE, sel=KD * TILE)
        done = waiter(S)
        with nc.Block() as block:

            @block.sync
            def _(sp):
                sp.dma_start(ctrl[:, :, :], a["ctrl_twice"].rearrange("(k p) n -> p k n", p=P)).then_inc(loaded, 16)
                prime(sp, S, nrm)

            @block.gpsimd
            def _(pool):
                with pool.Fori(0, TILES) as i:
                    nrm.gpsimd_rstd(pool, i)

            @block.scalar
            def _(act):
                with act.Fori(0, TILES) as i:
                    nrm.scalar_copy(act, i, 0)
                    for c in range(TILE):
                        for k in range(KD):
                            n = KD * c + k
                            done(act, "gath", i, n + 1)
                            S["sel"].inc(act.copy(
                                selT[:, k, :, ds((i * TILE + c) * GC, GC)].rearrange("p e g -> p g e"),
                                ps[:, 4 + n % 4, :].rearrange("p (g e) -> p g e", g=GC)))

            @block.vector
            def _(dve):
                with dve.Fori(0, TILES) as i:
                    nrm.vector_stats(dve, i)
                    done(dve, "gath", i, 0)
                    nrm.vector_apply(dve, i)
                    done(dve, "lgp", i)
                    groups = lambda t: t.rearrange("p (g t) -> p g t", t=GRP)
                    S["lg"].inc(dve.tensor_tensor(groups(lg[:, :]), groups(ps[:, 2, :]),
                                                  const("tie").unsqueeze(1).to_broadcast([P, TW // GRP, GRP]), ALU.add))
                    done(dve, "lg", i)
                    S["gmax"].inc(dve.tensor_reduce(gmax[:, :], groups(lg[:, :]), AX.X, ALU.max))
                    done(dve, "gmax", i)
                    S["one"].inc(dve.tensor_tensor(groups(one[:, :]), groups(lg[:, :]),
                                                   gmax[:, :].unsqueeze(2).to_broadcast([P, TW // GRP, GRP]), ALU.is_equal))
                    done(dve, "one", i)
                    S["picks"].inc(dve.tensor_tensor(
                        picks[:, ds(i * TW, TW)].rearrange("p (c t) -> p c t", c=TILE),
                        one[:, :].rearrange("p (c t) -> p c t", c=TILE),
                        const("parity").unsqueeze(1).to_broadcast([P, TILE, P]), ALU.mult))
                    done(dve, "turned", i)
                    S["spread"].inc(dve.tensor_tensor(
                        spread[:, :, :, :],
                        ps[:, 3, :].rearrange("p (c e) -> p c e", c=TILE)[:, :, 0:ES].unsqueeze(2).to_broadcast([P, TILE, GC, ES]),
                        const("group_of").unsqueeze(1).unsqueeze(3).to_broadcast([P, TILE, GC, ES]), ALU.mult))

            @block.tensor
            def _(pe):
                pe.wait_ge(loaded, 16)
                with pe.Fori(0, TILES) as i:
                    nrm.tensor_turn(pe, i, 0)
                    pe.wait_ge(nrm.xnT.sem, nrm.xnT.at(i, KD))
                    done(pe, "lg", i, 0)
                    for k in range(KD):
                        t = pe.matmul(ps[:, 2, :], ctrl[:, k, :], kept["xnT"][:, k, :], start=(k == 0), stop=(k == KD - 1))
                    S["lgp"].inc(t)
                    done(pe, "one", i)
                    done(pe, "spread", i, 0)
                    for c in range(TILE):
                        t = pe.transpose(ps[:, 3, c * P:(c + 1) * P], one[:, c * P:(c + 1) * P], const("ident"))
                    S["turned"].inc(t)
                    done(pe, "spread", i)
                    for c in range(TILE):
                        for k in range(KD):
                            n = KD * c + k
                            if n < 4:
                                done(pe, "sel", i, 0)
                            else:
                                done(pe, "sel", i, n - 3)
                            S["gath"].inc(pe.matmul(ps[:, 4 + n % 4, :], kept["xn"][:, c, k * P:(k + 1) * P],
                                                    spread[:, c, :, :].rearrange("p g e -> p (g e)"), start=True, stop=True))


def apply_experts(nc, a, kept, const, selT, scratch):
    ps, xn, xnT = kept["ps"], kept["xn"], kept["xnT"]
    SLOTS = 4
    with ExitStack() as ctx:
        def sb(name, shape, dt=F32):
            return ctx.enter_context(nc.sbuf_tensor(name, shape, dt))

        def sem(name):
            return ctx.enter_context(nc.semaphore(name))

        f1 = sb("f1w", [P, KD, SLOTS, 2 * FF])
        f2 = sb("f2w", [P, SLOTS, D])
        bias = sb("ffn_bias", [P, PAIRS])
        inter = sb("inter_sb", [P, 2, 2, 2, D])
        loaded = sem("e_loaded")
        f1_in = [sem(f"e_f1_in{u}") for u in range(SLOTS)]
        f2_in = [sem(f"e_f2_in{u}") for u in range(SLOTS)]
        stored = [sem(f"e_stored{u}") for u in range(2)]
        S = signals(sem, "e", innp=SLOTS, inner=2 * SLOTS, outp=SLOTS, low=SLOTS, high=SLOTS)
        done = waiter(S)
        f1_d = a["L0_ffn_f1"].rearrange("(k p) e s f -> p k (e s f)", p=P)
        f2_d = a["L0_ffn_f2"].rearrange("e s f d -> (e s f) d")
        out_d = scratch.rearrange("(h g) e d -> g h (e d)", g=P)

        def stored_before(eng, i, v):
            eng.wait_ge(stored[v % 2], PRIME + 16 * (2 * i + v // 2))

        with nc.Block() as block:

            @block.gpsimd
            def _(pool):
                pool.dma_start(bias[:, :], a["ffn_bias_cols"]).then_inc(loaded, 16)
                with pool.Fori(0, PAIRS // SLOTS) as i:
                    for u in range(SLOTS):
                        pair = i * SLOTS + u
                        done(pool, "innp", i, u + 1 - SLOTS)
                        pool.dma_start(f1[:, :, u, :], f1_d[:, :, ds(pair * P, P)]).then_inc(f1_in[u], 16)
                        done(pool, "outp", i, u + 1 - SLOTS)
                        pool.dma_start(f2[:, u, :], f2_d[ds(pair * P, P), :]).then_inc(f2_in[u], 16)

            @block.tensor
            def _(pe):
                def second(i, u, n):
                    done(pe, "inner", i, 2 * n + 2)
                    done(pe, "low", i, n - 1)
                    done(pe, "high", i, n - 1)
                    pe.wait_ge(f2_in[u], 16 * (i + 1) if n >= 0 else 16 * i)
                    for g in range(2):
                        for e in range(2):
                            t = pe.matmul(ps[:, 2 + 2 * (u % 2) + e, g * D:(g + 1) * D],
                                          xn[e * FF:(e + 1) * FF, u, g * P:(g + 1) * P],
                                          f2[e * FF:(e + 1) * FF, u, :], start=True, stop=True)
                    S["outp"].inc(t)

                with pe.Fori(0, PAIRS // SLOTS) as i:
                    for u in range(SLOTS):
                        pe.wait_ge(f1_in[u], 16 * (i + 1))
                        done(pe, "inner", i, 2 * (u - 1))
                        for e in range(2):
                            for k in range(KD):
                                t = pe.matmul(ps[:, u % 2, e * GROUPS:(e + 1) * GROUPS], f1[:, k, u, :],
                                              selT[:, k, ds((i * SLOTS + u) * 2 + e, 1), :].rearrange("p o g -> p (o g)"),
                                              start=(k == 0), stop=(k == KD - 1))
                        S["innp"].inc(t)
                        if u:
                            second(i, u - 1, u - 1)
                    second(i, SLOTS - 1, SLOTS - 1)

            @block.scalar
            def _(act):
                act.wait_ge(loaded, 16)
                with act.Fori(0, PAIRS // SLOTS) as i:
                    for u in range(SLOTS + 1):
                        if u < SLOTS:
                            done(act, "innp", i, u + 1)
                            done(act, "outp", i, u + 1 - SLOTS)
                            for e in range(2):
                                r = slice(e * FF, (e + 1) * FF)
                                S["inner"].inc(act.activation(xn[r, u, :], ps[r, u % 2, e * GROUPS:(e + 1) * GROUPS],
                                                              ACT.Relu, bias=bias[r, ds(i * SLOTS + u, 1)]))
                        if u:
                            v = u - 1
                            done(act, "outp", i, v + 1)
                            stored_before(act, i, v)
                            S["high"].inc(act.copy(inter[:, v % 2, :, 1, :],
                                                   ps[:, 3 + 2 * (v % 2), :].rearrange("p (g d) -> p g d", g=2)))

            @block.vector
            def _(dve):
                with dve.Fori(0, PAIRS // SLOTS) as i:
                    for v in range(SLOTS):
                        done(dve, "outp", i, v + 1)
                        stored_before(dve, i, v)
                        S["low"].inc(dve.tensor_copy(inter[:, v % 2, :, 0, :],
                                                     ps[:, 2 + 2 * (v % 2), :].rearrange("p (g d) -> p g d", g=2)))

            @block.sync
            def _(sp):
                prime(sp, S)
                for s in stored:
                    sp.sem_inc(s, PRIME)
                with sp.Fori(0, PAIRS // SLOTS) as i:
                    for v in range(SLOTS):
                        done(sp, "low", i, v + 1)
                        done(sp, "high", i, v + 1)
                        sp.dma_start(out_d[:, :, ds((i * SLOTS + v) * 2 * D, 2 * D)],
                                     inter[:, v % 2, :, :, :].rearrange("p g e d -> p g (e d)")).then_inc(stored[v % 2], 16)
                for s in stored:
                    sp.wait_ge(s, PRIME + 16 * PAIRS // 2)


def scatter_tokens(nc, a, kept, picks, scratch):
    X, ps = kept["X"], kept["ps"]
    GP = GC // 2
    with ExitStack() as ctx:
        def sb(name, shape, dt=F32):
            return ctx.enter_context(nc.sbuf_tensor(name, shape, dt))

        def sem(name):
            return ctx.enter_context(nc.semaphore(name))

        inter = sb("inter_in", [P, 2, TILE, GP, D])
        hot = sb("hot", [P, 2, TW])
        read = [sem(f"s_read{u}") for u in range(2 * TILE)]
        S = signals(sem, "s", hot=2, added=2 * TILE, res=2 * TILE)
        done = waiter(S)
        src = scratch.rearrange("(c q r) e d -> c (r e) q d", q=GP, r=2)
        with nc.Block() as block:

            @block.sync
            def _(sp):
                prime(sp, S)
                with sp.Fori(0, TILES // 2) as i:
                    for u in range(2 * TILE):
                        done(sp, "added", i, u + 1 - 2 * TILE)
                        sp.dma_start(inter[:, u // TILE, u % TILE, :, :],
                                     src[ds(i * 2 * TILE + u, 1)].rearrange("o p q d -> p (o q) d")).then_inc(read[u], 16)

            @block.scalar
            def _(act):
                with act.Fori(0, TILES // 2) as i:
                    for t in range(2):
                        done(act, "added", i, TILE * (t - 1))
                        S["hot"].inc(act.copy(hot[:, t, :], picks[:, ds((2 * i + t) * TW, TW)]))

            @block.tensor
            def _(pe):
                with pe.Fori(0, TILES // 2) as i:
                    for u in range(2 * TILE):
                        t, c = u // TILE, u % TILE
                        done(pe, "hot", i, t + 1)
                        done(pe, "res", i, u - 7)
                        pe.wait_ge(read[u], 16 * (i + 1))
                        for q in range(GP):
                            m = pe.matmul(ps[32 * q:32 * (q + 1), u, 0:D], hot[:, t, c * P + 32 * q:c * P + 32 * (q + 1)],
                                          inter[:, t, c, q, :], start=True, stop=True)
                        S["added"].inc(m)

            @block.vector
            def _(dve):
                with dve.Fori(0, TILES // 2) as i:
                    for u in range(2 * TILE):
                        done(dve, "added", i, u + 1)
                        xs = X[:, ds(i * 2 * TILE + u, 1), :]
                        S["res"].inc(dve.tensor_tensor(xs, xs, ps[:, u, 0:D].unsqueeze(1), ALU.add))
                    done(dve, "res", i)

def attention(nc, a, kept, const):
    X, ps, xnT = kept["X"], kept["ps"], kept["xnT"]
    NJ = len(HEADS_OF)
    rows = [NORM_ROW[j] + len(HEADS_OF[j]) for j in range(NJ)]
    with ExitStack() as ctx:
        def sb(name, shape, dt=F32):
            return ctx.enter_context(nc.sbuf_tensor(name, shape, dt))

        def sem(name):
            return ctx.enter_context(nc.semaphore(name))

        wqkv = sb("wqkv", [P, KD, 3 * D])
        wo = sb("wo", [P, KD, D])
        rfb = sb("rfb", [P, NJ * 6 * NF])
        b_out = sb("b_out", [P, D])
        kT = sb("kT", [P, NJ, TW])
        qT = sb("qT", [P, NJ, HALVES, TW])
        sq = sb("sq", [P, 2 * NJ, TW])
        v = sb("v", [P, TILE, HEADS, VW])
        kp = sb("kp", [P, TILE, HEADS * NF])
        kv = sb("kv", [P, HP, 2 * VW])
        qp = sb("qp", [P, HP, TW])
        den = sb("den", [P, TILE, HEADS])
        rec = sb("rec", [P, TILE, HEADS])
        o = sb("o", [P, TILE, D])
        oT = sb("oT", [P, KD, TW])
        loaded, cleared = sem("a_loaded"), sem("a_cleared")
        nrm = Norm("a", sem, kept, const)
        S = signals(sem, "a", qk=2 * NJ, sq=2 * NJ, copy=2 * NJ, nsq=2 * NJ, norm=2 * NJ,
                    vp=2, v=2, kpp=TILE, kp=TILE, kvp=TILE,
                    qpp=HP, qp=HP, op=1, den=2, rec=1, o=2, turned=KD, oT=KD, yp=2, res=2, bias=1)
        S2 = signals(sem, "a", kv=2)
        done = waiter({**S, **S2})

        def square_sums(pe, i, n):
            j = n % NJ
            if n == 0:
                done(pe, "sq", i)
            S["nsq"].inc(pe.matmul(ps[NORM_ROW[j]:rows[j], proj_bank(n), :], const("head_of")[0:NORM_ROW[j], 0:len(HEADS_OF[j])],
                                   sq[0:NORM_ROW[j], n, :], start=True, stop=True))

        proj_bank = lambda n: 2 + n if n < 5 else 1

        with nc.Block() as block:

            @block.sync
            def _(sp):
                for dst, src in ((wqkv[:, :, :], a["w_qkv_T"].rearrange("(k p) n -> p k n", p=P)),
                                 (wo[:, :, :], a["w_out_T"].rearrange("(k p) n -> p k n", p=P)),
                                 (rfb[:, :], a["rf_blocks"]),
                                 (b_out[:, :], a["L1_attn_b_out"].rearrange("(o n) -> o n", o=1).to_broadcast([P, D]))):
                    sp.dma_start(dst, src).then_inc(loaded, 16)
                prime(sp, {**S, **S2}, nrm)

            @block.gpsimd
            def _(pool):
                pool.memset(kv[:, :, :], 0.0).then_inc(cleared, 1)
                pool.memset(v[:, :, :, HD:], 1.0).then_inc(cleared, 1)
                pool.wait_ge(loaded, 64)
                with pool.Fori(0, B) as b:
                    for half in range(HALVES):
                        nrm.gpsimd_rstd(pool, b * HALVES + half)
                    for half in range(HALVES):
                        i = b * HALVES + half
                        done(pool, "res", i)
                        xs = X[:, ds(i * TILE, TILE), :]
                        S["bias"].inc(pool.tensor_tensor(xs, xs, b_out[:, :].unsqueeze(1).to_broadcast([P, TILE, D]), ALU.add))
                    done(pool, "bias", b * HALVES + HALVES - 1)

            @block.scalar
            def _(act):
                with act.Fori(0, B) as b:
                    for half in range(HALVES):
                        i = b * HALVES + half
                        nrm.scalar_copy(act, i, 0)
                        for n in range(2 * NJ):
                            j = n % NJ
                            done(act, "qk", i, n + 1)
                            if n == 0:
                                done(act, "nsq", i, 0)
                            S["sq"].inc(act.activation(sq[0:NORM_ROW[j], n, :], ps[0:NORM_ROW[j], proj_bank(n), :], ACT.Square))
                        for n in range(2 * NJ):
                            j = n % NJ
                            r = slice(NORM_ROW[j], rows[j])
                            done(act, "nsq", i, n + 1)
                            if n == 0:
                                done(act, "kpp", i, 0)
                            if n == NJ and half == 0:
                                done(act, "qpp", i, 0)
                            dst = kT[r, j, :] if n < NJ else qT[r, j, half, :]
                            S["norm"].inc(act.activation(dst, ps[r, proj_bank(n), :], ACT.Sqrt))
                        for c in range(TILE):
                            done(act, "kpp", i, c + 1)
                            if c == 0:
                                done(act, "kvp", i, 0)
                            S["kp"].inc(act.activation(kp[:, c, :].rearrange("p (u n) -> p u n", u=2),
                                                       ps[:, 2 + 2 * (c % 2):4 + 2 * (c % 2), :], ACT.Exp, scale=NF ** -0.5))
                    for half in range(HALVES):
                        i = b * HALVES + half
                        for p in range(HP):
                            done(act, "qpp", i, p + 1)
                            if p == 0:
                                done(act, "op", i, 0)
                            S["qp"].inc(act.activation(qp[:, p, :], ps[:, 2 + p % 4, :], ACT.Exp, scale=NF ** -0.5))
                        for k in range(KD):
                            done(act, "turned", i, k + 1)
                            if k == 0:
                                done(act, "yp", i, 0)
                            S["oT"].inc(act.copy(oT[:, k, :], ps[:, 2 + k, :]))

            @block.vector
            def _(dve):
                dve.wait_ge(cleared, 2)
                with dve.Fori(0, B) as b:
                    for half in range(HALVES):
                        i = b * HALVES + half
                        nrm.vector_stats(dve, i)
                        nrm.vector_apply(dve, i)
                        for n in range(2 * NJ):
                            j = n % NJ
                            done(dve, "sq", i, n + 1)
                            if n == 0:
                                done(dve, "kpp", i, 0)
                            if n == NJ and half == 0:
                                done(dve, "qpp", i, 0)
                            dst = kT[0:NORM_ROW[j], j, :] if n < NJ else qT[0:NORM_ROW[j], j, half, :]
                            S["copy"].inc(dve.tensor_copy(dst, ps[0:NORM_ROW[j], proj_bank(n), :]))
                        for u in range(2):
                            done(dve, "vp", i, u + 1)
                            if u == 0:
                                done(dve, "kvp", i, 0)
                            S["v"].inc(dve.tensor_copy(
                                v[:, 2 * u:2 * u + 2, :, 0:HD],
                                ps[:, 6, :].rearrange("p (c h d) -> p c h d", c=2, d=HD)))
                    done(dve, "kvp", b * HALVES + HALVES - 1)
                    done(dve, "op", b * HALVES, 0)
                    for e in range(2):
                        r = slice(e * NF, (e + 1) * NF)
                        S2["kv"].inc(dve.tensor_copy(
                            kv[r, :, e * VW:(e + 1) * VW],
                            ps[r, 7, 0:HP * 2 * VW].rearrange("p (a w) -> p a w", w=2 * VW)[:, :, e * VW:(e + 1) * VW]))
                    for half in range(HALVES):
                        i = b * HALVES + half
                        done(dve, "op", i)
                        heads = lambda u: ps[:, 6 * u:6 * u + 2, 0:HEADS * VW].rearrange("p c (h w) -> p c h w", w=VW)
                        for u in range(2):
                            S["den"].inc(dve.tensor_scalar(den[:, 2 * u:2 * u + 2, :], heads(u)[:, :, :, HD], 1e-6, None, ALU.add))
                        done(dve, "den", i)
                        S["rec"].inc(dve.reciprocal(rec[:, :, :], den[:, :, :]))
                        done(dve, "rec", i)
                        done(dve, "turned", i, 0)
                        for u in range(2):
                            S["o"].inc(dve.tensor_tensor(
                                o[:, 2 * u:2 * u + 2, :].rearrange("p c (h d) -> p c h d", d=HD), heads(u)[:, :, :, 0:HD],
                                rec[:, 2 * u:2 * u + 2, :].unsqueeze(3).to_broadcast([P, 2, HEADS, HD]), ALU.mult))
                        for u in range(2):
                            done(dve, "yp", i, u + 1)
                            xs = X[:, ds(i * TILE + 2 * u, 2), :]
                            S["res"].inc(dve.tensor_tensor(xs, xs, ps[:, 4 + u, :].rearrange("p (c d) -> p c d", c=2), ALU.add))

            @block.tensor
            def _(pe):
                pe.wait_ge(loaded, 64)
                with pe.Fori(0, B) as b:
                    for half in range(HALVES):
                        i = b * HALVES + half
                        if half == 0:
                            done(pe, "o", i, 0)
                            done(pe, "res", i, 0)
                        nrm.tensor_turn(pe, i, 0)
                        pe.wait_ge(nrm.xnT.sem, nrm.xnT.at(i, KD))
                        done(pe, "kp", i, 0)
                        done(pe, "v", i, 0)
                        for n in range(2 * NJ):
                            j = n % NJ
                            w = (D if n < NJ else 0) + HEADS_OF[j][0] * HD
                            for k in range(KD):
                                t = pe.matmul(ps[0:NORM_ROW[j], proj_bank(n), :], wqkv[:, k, w:w + NORM_ROW[j]],
                                              xnT[:, k, :], start=(k == 0), stop=(k == KD - 1))
                            S["qk"].inc(t)
                        for n in range(2 * NJ):
                            square_sums(pe, i, n)
                        done(pe, "norm", i)
                        done(pe, "copy", i)
                        for c in range(TILE):
                            if c == 2:
                                done(pe, "v", i, 1)
                            for k in range(KD):
                                t = pe.matmul(ps[:, 6, (c % 2) * D:(c % 2 + 1) * D], xnT[:, k, c * P:(c + 1) * P],
                                              wqkv[:, k, 2 * D:3 * D], start=(k == 0), stop=(k == KD - 1))
                            if c % 2:
                                S["vp"].inc(t)
                            if c >= 2:
                                done(pe, "kp", i, c - 1)
                            at = 0
                            for j in range(NJ):
                                left, src = len(HEADS_OF[j]) * NF, j * 6 * NF
                                while left:
                                    n = min(left, 512 - at % 512)
                                    t = pe.matmul(ps[:, 2 + 2 * (c % 2) + at // 512, at % 512:at % 512 + n],
                                                  kT[0:rows[j], j, c * P:(c + 1) * P], rfb[0:rows[j], src:src + n],
                                                  start=True, stop=True)
                                    at, src, left = at + n, src + n, left - n
                            S["kpp"].inc(t)
                        done(pe, "v", i)
                        if half == 0:
                            done(pe, "o", i, 0)
                        for c in range(TILE):
                            done(pe, "kp", i, c + 1)
                            for p in range(HP):
                                first = half == 0 and c == 0
                                t = pe.matmul(ps[:, 7, p * 2 * VW:(p + 1) * 2 * VW], kp[:, c, p * P:(p + 1) * P],
                                              v[:, c, 2 * p:2 * p + 2, :].rearrange("p h w -> p (h w)"),
                                              start=first and p == 0, stop=half == HALVES - 1 and c == TILE - 1,
                                              skip_group_check=True)
                            S["kvp"].inc(t)
                    done(pe, "kv", b)
                    for half in range(HALVES):
                        i = b * HALVES + half
                        done(pe, "oT", i, 0)
                        done(pe, "res", i, 0)
                        for p in range(HP):
                            if p >= 4:
                                done(pe, "qp", i, p - 3)
                            j, src = p // 3, (p // 3) * 6 * NF + (p % 3) * P
                            S["qpp"].inc(pe.matmul(ps[:, 2 + p % 4, :], rfb[0:rows[j], src:src + P],
                                                   qT[0:rows[j], j, half, :], start=True, stop=True))
                        done(pe, "qp", i)
                        done(pe, "o", i, 0)
                        for c in range(TILE):
                            for p in range(HP):
                                t = pe.matmul(ps[:, (0, 1, 6, 7)[c], p * 2 * VW:(p + 1) * 2 * VW],
                                              qp[:, p, c * P:(c + 1) * P], kv[:, p, :], start=True, stop=True)
                        S["op"].inc(t)
                        done(pe, "o", i)
                        for k in range(KD):
                            for c in range(TILE):
                                t = pe.transpose(ps[:, 2 + k, c * P:(c + 1) * P], o[:, c, k * P:(k + 1) * P], const("ident"))
                            S["turned"].inc(t)
                        done(pe, "oT", i)
                        for c in range(TILE):
                            for k in range(KD):
                                t = pe.matmul(ps[:, 4 + c // 2, (c % 2) * D:(c % 2 + 1) * D], oT[:, k, c * P:(c + 1) * P],
                                              wo[:, k, :], start=(k == 0), stop=(k == KD - 1))
                            if c % 2:
                                S["yp"].inc(t)


def experts(nc, a, kept, const):
    X, ps, xnT = kept["X"], kept["ps"], kept["xnT"]
    with ExitStack() as ctx:
        def sb(name, shape, dt=F32):
            return ctx.enter_context(nc.sbuf_tensor(name, shape, dt))

        def sem(name):
            return ctx.enter_context(nc.semaphore(name))

        ew = sb("ew", [P, KD, NE, D])
        eb = sb("eb", [NE, D])
        rw = sb("rw", [P, KD, NE])
        rb = sb("rb", [P, NE])
        lg = sb("router_logits", [P, TILE, NE])
        z = sb("z", [P, TILE, NE])
        top = sb("top", [P, TILE])
        total = sb("total", [P, TILE])
        gate = sb("gate", [P, TILE])
        one = sb("one", [P, TILE, NE])
        best = sb("best", [P, TILE])
        g = sb("g", [P, TILE, NE])
        gT = sb("gT", [NE, TW])
        loaded = sem("x_loaded")
        nrm = Norm("x", sem, kept, const)
        S = signals(sem, "x", lgp=1, lg=1, top=1, z=1, ez=1, total=1, gate=1, one=1, ranked=1, best=1, first=1,
                    g=1, gTp=1, gT=1, biasp=TILE, bias=TILE, yp=TILE * NE // 2, acc=TILE * NE)
        done = waiter(S)
        with nc.Block() as block:

            @block.sync
            def _(sp):
                for dst, src in ((rw[:, :, :], a["L1_ffn_router_w"].rearrange("(k p) e -> p k e", p=P)),
                                 (rb[:, :], a["L1_ffn_router_b"].rearrange("(o n) -> o n", o=1).to_broadcast([P, NE])),
                                 (eb[:, :], a["L1_ffn_expert_b"]),
                                 (ew[:, 0, :, :], a["L1_ffn_expert_w"].rearrange("e (k p) d -> k p e d", p=P)[0]),
                                 (ew[:, 1, :, :], a["L1_ffn_expert_w"].rearrange("e (k p) d -> k p e d", p=P)[1])):
                    sp.dma_start(dst, src).then_inc(loaded, 16)
                prime(sp, S, nrm)

            @block.gpsimd
            def _(pool):
                with pool.Fori(0, TILES) as i:
                    nrm.gpsimd_rstd(pool, i)

            @block.scalar
            def _(act):
                with act.Fori(0, TILES) as i:
                    nrm.scalar_copy(act, i, 0)
                    done(act, "z", i)
                    S["ez"].inc(act.activation(z[:, :, :], z[:, :, :], ACT.Exp))
                    done(act, "gTp", i)
                    done(act, "biasp", i, 0)
                    S["gT"].inc(act.copy(gT[:, :], ps[0:NE, 3, :]))

            @block.vector
            def _(dve):
                dve.wait_ge(loaded, 80)
                wide = lambda t: t[:, :].unsqueeze(2).to_broadcast([P, TILE, NE])
                with dve.Fori(0, TILES) as i:
                    nrm.vector_stats(dve, i)
                    nrm.vector_apply(dve, i)
                    done(dve, "lgp", i)
                    S["lg"].inc(dve.tensor_tensor(lg[:, :, :], ps[:, 2, 0:TILE * NE].rearrange("p (c e) -> p c e", e=NE),
                                                  rb[:, :].unsqueeze(1).to_broadcast([P, TILE, NE]), ALU.add))
                    done(dve, "lg", i)
                    S["top"].inc(dve.tensor_reduce(top[:, :], lg[:, :, :], AX.X, ALU.max))
                    done(dve, "top", i)
                    S["z"].inc(dve.tensor_tensor(z[:, :, :], lg[:, :, :], wide(top), ALU.subtract))
                    S["one"].inc(dve.tensor_tensor(one[:, :, :], lg[:, :, :], wide(top), ALU.is_equal))
                    done(dve, "one", i)
                    S["ranked"].inc(dve.tensor_tensor(one[:, :, :], one[:, :, :],
                                                      const("rank").unsqueeze(1).to_broadcast([P, TILE, NE]), ALU.mult))
                    done(dve, "ranked", i)
                    S["best"].inc(dve.tensor_reduce(best[:, :], one[:, :, :], AX.X, ALU.max))
                    done(dve, "best", i)
                    S["first"].inc(dve.tensor_tensor(one[:, :, :], one[:, :, :], wide(best), ALU.is_equal))
                    done(dve, "ez", i)
                    S["total"].inc(dve.tensor_reduce(total[:, :], z[:, :, :], AX.X, ALU.add))
                    done(dve, "total", i)
                    S["gate"].inc(dve.reciprocal(gate[:, :], total[:, :]))
                    done(dve, "gate", i)
                    done(dve, "first", i)
                    S["g"].inc(dve.tensor_tensor(g[:, :, :], one[:, :, :], wide(gate), ALU.mult))
                    done(dve, "g", i)
                    n = 0
                    for c in range(TILE):
                        xs = X[:, ds(i * TILE + c, 1), :]
                        for q in range(NE // 2):
                            done(dve, "yp", i, c * NE // 2 + q + 1)
                            for e in range(2):
                                if n:
                                    done(dve, "acc", i, n)
                                n += 1
                                S["acc"].inc(dve.scalar_tensor_tensor(
                                    xs, ps[:, 4 + q, e * D:(e + 1) * D].unsqueeze(1), g[:, c, 2 * q + e:2 * q + e + 1], xs,
                                    ALU.mult, ALU.add))
                        done(dve, "biasp", i, c + 1)
                        done(dve, "acc", i, n)
                        S["bias"].inc(dve.tensor_tensor(xs, xs, ps[:, 2, D:2 * D].unsqueeze(1), ALU.add))

            @block.tensor
            def _(pe):
                pe.wait_ge(loaded, 80)
                with pe.Fori(0, TILES) as i:
                    nrm.tensor_turn(pe, i, 0)
                    pe.wait_ge(nrm.xnT.sem, nrm.xnT.at(i, KD))
                    done(pe, "bias", i, 0)
                    for c in range(TILE):
                        for k in range(KD):
                            t = pe.matmul(ps[:, 2, c * NE:(c + 1) * NE], xnT[:, k, c * P:(c + 1) * P], rw[:, k, :],
                                          start=(k == 0), stop=(k == KD - 1))
                    S["lgp"].inc(t)
                    for c in range(TILE):
                        for q in range(NE // 2):
                            done(pe, "acc", i, (c - 1) * NE + 2 * q + 2)
                            for k in range(KD):
                                t = pe.matmul(ps[:, 4 + q, :], xnT[:, k, c * P:(c + 1) * P],
                                              ew[:, k, 2 * q:2 * q + 2, :].rearrange("p e d -> p (e d)"),
                                              start=(k == 0), stop=(k == KD - 1))
                            S["yp"].inc(t)
                        if c == 0:
                            done(pe, "g", i)
                            done(pe, "gT", i, 0)
                            for d in range(TILE):
                                t = pe.transpose(ps[0:NE, 3, d * P:(d + 1) * P], g[:, d, :], const("ident"))
                            S["gTp"].inc(t)
                            done(pe, "gT", i)
                        done(pe, "bias", i, c)
                        S["biasp"].inc(pe.matmul(ps[:, 2, D:2 * D], gT[:, c * P:(c + 1) * P], eb[:, :], start=True, stop=True))


PHASES = 4
_INS = ['L0_attn_x', 'L0_attn_W_in', 'L0_attn_conv_w', 'L0_attn_W_x', 'L0_attn_A_log', 'L0_attn_W_out',
        'L0_ffn_f1', 'L0_ffn_f2', 'L1_attn_b_out', 'L1_ffn_router_w', 'L1_ffn_router_b', 'L1_ffn_expert_w',
        'L1_ffn_expert_b']


def laid_out(inputs):
    w_qkv = np.asarray(inputs["L1_attn_w_qkv"])
    rf = np.asarray(inputs["L1_attn_random_features"])
    rfb = np.zeros((P, 3 * 6 * NF), np.float32)
    for j, heads in enumerate(HEADS_OF):
        for n, _ in enumerate(heads):
            c = (j * 6 + n) * NF
            rfb[n * HD:(n + 1) * HD, c:c + NF] = rf.T
            rfb[NORM_ROW[j] + n, c:c + NF] = -float(NF) ** 0.5
    ctrl = np.asarray(inputs["L0_ffn_controller"]).reshape(D, ES)
    return {
        "conv_b_cols": np.asarray(inputs["L0_attn_conv_b"]).reshape(KI, P).T,
        "d_cols": np.asarray(inputs["L0_attn_D_param"]).reshape(KI, P).T,
        "ctrl_twice": np.concatenate([ctrl, ctrl], 1),
        "ffn_bias_cols": np.asarray(inputs["L0_ffn_bias"]).reshape(PAIRS, P).T,
        "w_qkv_T": w_qkv.T,
        "w_out_T": np.asarray(inputs["L1_attn_w_out"]).T,
        "rf_blocks": rfb,
    }


def kernel(**inputs):
    import numpy as _np
    import concourse.bacc as _bacc
    from concourse import mybir as _mybir
    from concourse.bass_utils import run_bass_kernel_spmd as _run

    nc = _bacc.Bacc("TRN2", target_bir_lowering=False, num_devices=1)
    arrays, a = {}, {}
    consts, at = shape_constants()
    given = {n: inputs[n] for n in _INS}
    for name, v in {**given, **laid_out(inputs), "consts": consts}.items():
        v = _np.ascontiguousarray(v)
        arrays[f"in_{name}"] = v
        a[name] = nc.dram_tensor(f"in_{name}", v.shape, _mybir.dt.from_np(v.dtype), kind="ExternalInput").ap()
    out = nc.dram_tensor("out", (B, L, D), F32, kind="ExternalOutput").ap()
    scratch = nc.dram_tensor("inter", (GROUPS, ES, D), F32, kind="Internal").ap()
    build(nc, a, out, a["consts"], at, scratch, PHASES)
    r = _run(nc, [arrays], core_ids=[0])
    return r.results[0]["out"]
```

```python
from contextlib import ExitStack

import concourse.bass as bass
import numpy as np
from concourse import mybir

ALU = mybir.AluOpType
ACT = mybir.ActivationFunctionType
AX = mybir.AxisListType
F32 = mybir.dt.float32
F32R = mybir.dt.float32r
ds = bass.ds

P = 128
B, L, D = 4, 1024, 256
TOKENS = B * L
CHUNKS = TOKENS // P
TILE = 4
TW = TILE * P
TILES = CHUNKS // TILE
KD = D // P
HALVES = L // TW
EPS = 1e-5
DI, NS, TAPS = 512, 16, 4
KI = DI // P
Q = 16
NB = P // Q
XD = 1 + 2 * NS
GRP = 16
ES, FF = 64, 64
GC = P // GRP
GROUPS = TOKENS // GRP
PAIRS = ES // 2
HEADS, HD, NF = 16, 16, 64
HP = HEADS // 2
HEADS_OF = [range(0, 6), range(6, 12), range(12, 16)]
NORM_ROW = [96, 96, 64]
NE = 8


def shape_constants():
    p = np.arange(P)
    parts = {
        "ident": np.eye(P),
        "sel_delta": np.repeat((p == 0)[:, None], P, 1),
        "sel_b": (p[:, None] == 1 + p[None, :] % NS),
        "sel_c": (p[:, None] == 1 + NS + p[None, :] % NS),
        "place_n": np.repeat((p[:, None] % Q) == np.arange(Q)[None, :], NS, 1),
        "place": (p[:, None] % Q) == np.arange(Q)[None, :],
        "same_block": (p[:, None] // Q) == (p[None, :] // Q),
        "earlier_block": (p[:, None] // Q) < (p[None, :] // Q),
        "own_block_causal": ((p[:, None] // Q) == (p[None, :] // Q)) & (p[None, :] >= p[:, None]),
        "ref_of": (p[:, None] // NS - 1) == np.arange(NB)[None, :],
        "block_of_state": (p[:, None] // NS) == (p[None, :] // Q),
        "scan_keep": np.repeat((np.arange(TW) % P != 0)[None, :], P, 0),
        "tie": np.repeat(np.linspace(0.0, 1e-6, GRP, dtype=np.float32)[None, :], P, 0),
        "group_of": (p[:, None] // GRP) == np.arange(GC)[None, :],
        "parity": (p[:, None] // ES) == ((p[None, :] // GRP) % 2),
        "eps": np.full((P, 1), EPS),
        "head_of": (p[:, None] // HD) == np.arange(6)[None, :],
        "minus_half": np.full((P, 1), -0.5),
        "rank": np.repeat(np.arange(NE, 0, -1)[None, :], P, 0),
    }
    at, n = {}, 0
    for k, v in parts.items():
        at[k] = (n, n + v.shape[1])
        n += v.shape[1]
    return np.concatenate([v.astype(np.float32) for v in parts.values()], 1), at


PRIME = 16


class Signal:

    def __init__(self, sem, per):
        self.sem, self.per = sem, per

    def inc(self, instruction):
        instruction.then_inc(self.sem, 1)

    def at(self, i, n):
        return i * self.per + n + PRIME


def build(nc, a, out, consts, at, scratch, phases):
    with ExitStack() as ctx:
        kept = dict(
            X=ctx.enter_context(nc.sbuf_tensor("X", [P, CHUNKS, D], F32)),
            C=ctx.enter_context(nc.sbuf_tensor("consts", [P, consts.shape[1]], F32)),
            ps=ctx.enter_context(nc.psum_tensor("ps", [P, 8, 512], F32)),
            mv=ctx.enter_context(nc.sbuf_tensor("mean_var", [P, TILE, 2], F32)),
            st=ctx.enter_context(nc.sbuf_tensor("stats", [P, TILE, 6], F32)),
            carrier=ctx.enter_context(nc.sbuf_tensor("carrier", [P, 1], F32)),
            ve=ctx.enter_context(nc.sbuf_tensor("var_eps", [P, TILE], F32)),
            rstd=ctx.enter_context(nc.sbuf_tensor("rstd", [P, TILE], F32)),
            xn=ctx.enter_context(nc.sbuf_tensor("xn", [P, TILE, D], F32)),
            xnT=ctx.enter_context(nc.sbuf_tensor("xnT", [P, KD, TW], F32)),
        )

        def const(name, rows=P):
            lo, hi = at[name]
            return kept["C"][0:rows, lo:hi]

        mamba(nc, a, consts, kept, const)
        if phases >= 2:
            sparse_ffn(nc, a, kept, const, scratch)
        if phases >= 3:
            nxt = dict(
                w_hi=ctx.enter_context(nc.sbuf_tensor("ew_hi", [P, KD, NE, D], F32R)),
                w_lo=ctx.enter_context(nc.sbuf_tensor("ew_lo", [P, KD, NE, D], F32R)),
                rw=ctx.enter_context(nc.sbuf_tensor("rw", [P, KD, NE], F32)),
                rb=ctx.enter_context(nc.sbuf_tensor("rb", [P, NE], F32)),
                eb=ctx.enter_context(nc.sbuf_tensor("eb", [NE, D], F32)),
            )
            attention(nc, a, kept, const, nxt)
        if phases >= 4:
            experts(nc, a, kept, const, nxt, out)
            return
        stored = ctx.enter_context(nc.semaphore("stored"))
        with nc.Block() as block:

            @block.sync
            def _(sp):
                o = out.rearrange("b (c p) d -> p (b c) d", p=P)
                for i in range(TILES):
                    sp.dma_start(o[:, TILE * i:TILE * (i + 1)],
                                 kept["X"][:, TILE * i:TILE * (i + 1)]).then_inc(stored, 16)
                sp.wait_ge(stored, 16 * TILES)


def prime(eng, S, *norms):
    for s in [*S.values(), *(x for n in norms for x in (n.stats, n.mv, n.ve, n.rstd, n.xn, n.turned, n.xnT))]:
        eng.sem_inc(s.sem, PRIME)


class Norm:

    def __init__(self, name, sem, kept, const):
        self.k, self.const = kept, const
        self.stats = Signal(sem(f"{name}_stats"), TILE)
        self.mv = Signal(sem(f"{name}_mean_var"), TILE)
        self.ve = Signal(sem(f"{name}_var_eps"), 1)
        self.rstd = Signal(sem(f"{name}_rstd"), 1)
        self.xn = Signal(sem(f"{name}_xn"), TILE)
        self.turned = Signal(sem(f"{name}_xn_turned"), KD)
        self.xnT = Signal(sem(f"{name}_xnT"), KD)

    def vector_stats(self, dve, i):
        k = self.k
        for c in range(TILE):
            self.stats.inc(dve.bn_stats(k["st"][:, c:c + 1, :], k["X"][:, ds(i * TILE + c, 1), :]))
        dve.wait_ge(self.stats.sem, self.stats.at(i, TILE))
        dve.wait_ge(self.ve.sem, self.ve.at(i, 0))
        dve.wait_ge(self.xn.sem, self.xn.at(i, 0))
        dve.tensor_copy(k["carrier"][:, :], k["st"][:, 0, 0:1])
        for c in range(TILE):
            self.mv.inc(dve.bn_aggr(k["mv"][:, c, :], k["st"][:, c, :]))

    def gpsimd_rstd(self, pool, i):
        k = self.k
        pool.wait_ge(self.mv.sem, self.mv.at(i, TILE))
        pool.wait_ge(self.xn.sem, self.xn.at(i, 0))
        self.ve.inc(pool.tensor_tensor(k["ve"][:, :], k["mv"][:, :, 1],
                                       self.const("eps").to_broadcast([P, TILE]), ALU.add))
        pool.wait_ge(self.ve.sem, self.ve.at(i, 1))
        self.rstd.inc(pool.tensor_tensor(k["rstd"][:, :], k["ve"][:, :],
                                         self.const("minus_half").to_broadcast([P, TILE]), ALU.pow))

    def vector_apply(self, dve, i):
        k = self.k
        dve.wait_ge(self.rstd.sem, self.rstd.at(i, 1))
        dve.wait_ge(self.turned.sem, self.turned.at(i, 0))
        for c in range(TILE):
            self.xn.inc(dve.tensor_scalar(k["xn"][:, c:c + 1, :], k["X"][:, ds(i * TILE + c, 1), :],
                                          k["mv"][:, c, 0:1], k["rstd"][:, c:c + 1],
                                          ALU.subtract, ALU.mult))

    def tensor_turn(self, pe, i, banks):
        k = self.k
        pe.wait_ge(self.xn.sem, self.xn.at(i, TILE))
        pe.wait_ge(self.xnT.sem, self.xnT.at(i, 0))
        for d in range(KD):
            for c in range(TILE):
                t = pe.transpose(k["ps"][:, banks + d, c * P:(c + 1) * P],
                                 k["xn"][:, c, d * P:(d + 1) * P], self.const("ident"))
            self.turned.inc(t)

    def scalar_copy(self, act, i, banks):
        k = self.k
        for d in range(KD):
            act.wait_ge(self.turned.sem, self.turned.at(i, d + 1))
            self.xnT.inc(act.copy(k["xnT"][:, d, :], k["ps"][:, banks + d, :]))


def mamba(nc, a, consts, kept, const):
    sems = []
    with ExitStack() as ctx:
        def sb(name, shape):
            return ctx.enter_context(nc.sbuf_tensor(name, shape, F32))

        def sem(name):
            sems.append(nc.alloc_semaphore(name))
            return sems[-1]

        X, ps = kept["X"], kept["ps"]
        w_in = sb("w_in", [P, KD, 2 * DI])
        w_x = sb("w_x", [P, KI, XD])
        w_out = sb("w_out", [P, KI, D])
        conv_w = sb("conv_w", [P, KI, TAPS])
        conv_b = sb("conv_b", [P, KI])
        d_skip = sb("d_skip", [P, KI])
        a_col = sb("a_col", [P, 1])
        a_neg = sb("a_neg", [P, 1])
        a_row = sb("a_row", [P, NS])
        xpad = sb("xpad", [P, KI, TAPS - 1 + TW])
        acc = sb("acc", [P, KI, TW])
        xcT = sb("xcT", [P, 2, KI, TW])
        zs = sb("zs", [P, 2, KI, TW])
        xd = sb("xd", [XD, TW])
        soft = sb("soft", [P, TW])
        delta = sb("delta", [P, TW])
        run = sb("run", [P, TW])
        bd = sb("bd", [P, TW])
        refs8 = sb("refs8", [P, TILE, NB])
        ref = sb("ref", [P, TILE])
        a2 = sb("a2", [P, TW])
        a1 = sb("a1", [P, TW])
        f2 = sb("f2", [P, TW])
        f1p = sb("f1p", [P, TW])
        f1 = sb("f1", [P, TW])
        TOKC = TILE * (XD + 32 + 32)
        tok = sb("tok", [P, TOKC])
        tok_x = tok[:, 0:TILE * XD].rearrange("p (c k) -> p c k", c=TILE)
        tok_d = tok[:, TILE * XD:TILE * (XD + 32)].rearrange("p (c k) -> p c k", c=TILE)
        tok_b = tok[:, TILE * (XD + 32):TOKC].rearrange("p (c k) -> p c k", c=TILE)
        cm = sb("cm", [P, TILE, Q * NS + Q])
        a3 = sb("a3", [P, TILE, Q])
        big = sb("big", [P, TILE, Q * NS])
        md = sb("md", [P, TILE, Q])
        mdx = sb("mdx", [P, TILE, P])
        mt = sb("mt", [P, TILE, P])
        wd = sb("wd", [P, TILE])
        w2a = sb("w2a", [P, TILE, NS])
        w2 = sb("w2", [P, TILE, NS])
        xtok = sb("xtok", [P, TILE, DI])
        h = sb("h", [NS, HALVES, TILE, DI])
        y = sb("y", [P, KI, TW])

        x_first, x_in = sem("x_tile0_in"), sem("x_in")
        const_loaded, w_in_loaded, w_loaded = sem("const_loaded"), sem("w_in_loaded"), sem("w_loaded")
        W_LOADS = 16 * (6 + NB)
        a_abs, a_ready, cleared = sem("a_abs"), sem("a_ready"), sem("cleared")
        nrm = Norm("m", sem, kept, const)
        S = {}
        for name, per in dict(xz=2 * KI, xpad=KI, zs=KI, conv=TAPS * KI, hist=1, xc=KI, xdT=1,
                              xd=1, rep=3, soft=3, delta=1, run=1, bd=1, refs8=1, ref=1, a2=TILE,
                              a1=TILE, e2=1, e1=1, f2=1, f1p=1, f1=1, tokp=1, tok=1, cm=2, crep=1,
                              a3=TILE, ah=1, eh=1, g1=1, g2=1, md=1, mdx=1, off=1, mt0=1, mt=1, wd=1,
                              w2a=1, w2e=1, w2=1, xtp=TILE, xt=TILE, y=TILE, hc=1, h=TILE,
                              ys=KI, yg=1, o=2, res=2).items():
            S[name] = Signal(sem(f"m_{name}"), per)

        def done(eng, name, i, n=None):
            s = S[name]
            eng.wait_ge(s.sem, s.at(i, s.per if n is None else n))

        with nc.Block() as block:

            @block.sync
            def _(sp):
                xin = a["L0_attn_x"].rearrange("b (c p) d -> p (b c) d", p=P)
                x_tile = lambda t: (X[:, TILE * t:TILE * (t + 1)], xin[:, TILE * t:TILE * (t + 1)])
                sp.dma_start(*x_tile(0)).then_inc(x_first, 16)
                for k in range(KD):
                    sp.dma_start(w_in[:, k, :], a["L0_attn_W_in"].rearrange("(k p) n -> k p n", p=P)[k]).then_inc(w_in_loaded, 16)
                prime(sp, S, nrm)
                sp.dma_start(w_x[:, :, :], a["L0_attn_W_x"].rearrange("(k p) n -> p k n", p=P)).then_inc(w_loaded, 16)
                sp.dma_start(*x_tile(1)).then_inc(x_in, 16)
                sp.dma_start(w_out[:, :, :], a["L0_attn_W_out"].rearrange("(k p) n -> p k n", p=P)).then_inc(w_loaded, 16)
                for t in range(2, TILES):
                    sp.dma_start(*x_tile(t)).then_inc(x_in, 16)

            def steps(eng, front_first, step, end=None):
                front_first()
                step(0, 0, front=True, far=True, before=False)
                with eng.Fori(0, B - 2) as b:
                    step(b * HALVES + 1, 1, front=True, far=True, before=True)
                    step(b * HALVES + 2, 0, front=True, far=True, before=True)
                step(TILES - 3, 1, front=True, far=True, before=True)
                step(TILES - 2, 0, front=True, far=False, before=True)
                step(TILES - 1, 1, front=False, far=False, before=True)
                if end:
                    end(TILES - 1, 1)

            @block.gpsimd
            def _(pool):
                pool.wait_ge(const_loaded, 16)

                def first():
                    nrm.gpsimd_rstd(pool, 0)
                    nrm.gpsimd_rstd(pool, 1)

                def step(i, half, front, far, before):
                    done(pool, "tok", i)
                    done(pool, "crep", i, 0)
                    S["cm"].inc(pool.tensor_tensor(
                        cm[:, :, 0:Q * NS].rearrange("p c (t n) -> p c t n", n=NS),
                        tok_x[:, :, 1 + NS:XD].unsqueeze(2).to_broadcast([P, TILE, Q, NS]),
                        const("place_n").rearrange("p (t n) -> p t n", n=NS).unsqueeze(1).to_broadcast([P, TILE, Q, NS]),
                        ALU.mult))
                    S["cm"].inc(pool.tensor_tensor(
                        cm[:, :, Q * NS:], tok_d[:, :, 0:1].to_broadcast([P, TILE, Q]),
                        const("place").unsqueeze(1).to_broadcast([P, TILE, Q]), ALU.mult))
                    if far:
                        nrm.gpsimd_rstd(pool, i + 2)

                steps(pool, first, step)

            @block.scalar
            def _(act):
                act.dma_start(kept["C"][:, :], consts).then_inc(const_loaded, 16)
                for dst, src in (
                    (a_row[:, :], a["L0_attn_A_log"].rearrange("(o n) -> o n", o=1).to_broadcast([P, NS])),
                    (conv_w[:, :, :], a["L0_attn_conv_w"].rearrange("(k p) n -> p k n", p=P)),
                    (conv_b[:, :], a["conv_b_cols"]),
                    (d_skip[:, :], a["d_cols"]),
                ):
                    act.dma_start(dst, src).then_inc(w_loaded, 16)
                for b in range(NB):
                    act.dma_start(a_col[b * NS:(b + 1) * NS, :],
                                  a["L0_attn_A_log"].rearrange("(n o) -> n o", o=1)).then_inc(w_loaded, 16)

                def copy_x(j, ms):
                    for m in ms:
                        done(act, "xz", j, m + 1)
                        if m == 0:
                            done(act, "hist", j, 0)
                        S["xpad"].inc(act.copy(xpad[:, m, TAPS - 1:], ps[:, m % 2, :]))

                def silu_z(j, par):
                    for m in range(KI):
                        done(act, "xz", j, KI + m + 1)
                        if m == 0:
                            done(act, "yg", j - 1, 0)
                        S["zs"].inc(act.activation(zs[:, par, m, :], ps[:, m % 2, :], ACT.Silu))

                def silu_x(j, par):
                    done(act, "ys", j - 1, 0)
                    for m in range(KI):
                        done(act, "conv", j, KI * (TAPS - 1) + m + 1)
                        S["xc"].inc(act.activation(xcT[:, par, m, :], acc[:, m, :], ACT.Silu))

                def first():
                    nrm.scalar_copy(act, 0, 0)
                    copy_x(0, range(KI))
                    silu_z(0, 0)
                    nrm.scalar_copy(act, 1, 0)
                    act.wait_ge(w_loaded, W_LOADS)
                    act.activation(a_col[:, :], a_col[:, :], ACT.Exp).then_inc(a_abs, 1)
                    act.activation(a_row[:, :], a_row[:, :], ACT.Exp).then_inc(a_abs, 1)
                    act.wait_ge(a_abs, 2)
                    act.mul(a_neg[:, :], a_col[:, :], -1.0).then_inc(a_ready, 1)
                    act.mul(a_row[:, :], a_row[:, :], -1.0).then_inc(a_ready, 1)
                    act.wait_ge(a_ready, 2)

                def step(i, half, front, far, before):
                    silu_x(i, half)
                    done(act, "xdT", i)
                    done(act, "tokp", i, 0)
                    S["xd"].inc(act.copy(xd[:, :], ps[0:XD, 2, :]))
                    done(act, "rep", i, 1)
                    done(act, "delta", i, 0)
                    S["soft"].inc(act.activation(soft[:, :], ps[:, 3, :], ACT.Abs))
                    done(act, "soft", i, 1)
                    S["soft"].inc(act.activation(soft[:, :], soft[:, :], ACT.Exp, scale=-1.0))
                    done(act, "soft", i, 2)
                    S["soft"].inc(act.activation(soft[:, :], soft[:, :], ACT.Ln, bias=1.0))
                    if front:
                        copy_x(i + 1, (0, 1))
                    done(act, "a2", i)
                    S["e2"].inc(act.activation(a2[:, :], a2[:, :], ACT.Exp, scale=a_col[:, :]))
                    done(act, "a1", i)
                    S["e1"].inc(act.activation(a1[:, :], a1[:, :], ACT.Exp, scale=a_neg[:, :]))
                    done(act, "tokp", i)
                    done(act, "w2", i, 0)
                    done(act, "cm", i, 0)
                    done(act, "g2", i, 0)
                    S["tok"].inc(act.copy(tok[:, :], ps[:, 2, 0:TOKC]))
                    if front:
                        copy_x(i + 1, (2, 3))
                    done(act, "w2a", i)
                    S["w2e"].inc(act.activation(w2a[:, :, :], w2a[:, :, :], ACT.Exp))
                    done(act, "ah", i)
                    S["eh"].inc(act.activation(big[:, :, :], big[:, :, :], ACT.Exp))
                    if front:
                        silu_z(i + 1, 1 - half)
                    if far:
                        nrm.scalar_copy(act, i + 2, 0)

                steps(act, first, step)

            @block.vector
            def _(dve):
                hist = xpad[:, :, 0:TAPS - 1]
                chunks = lambda t: t[:, :].rearrange("p (c t) -> p c t", c=TILE)
                dve.memset(hist, 0.0).then_inc(cleared, 1)

                def x_copies(i):
                    done(dve, "y", i, 0)
                    for c in range(TILE):
                        done(dve, "xtp", i, c + 1)
                        S["xt"].inc(dve.tensor_copy(xtok[:, c, :], ps[:, 6 + c % 2, :]))

                def convolve(j, taps):
                    for k in taps:
                        for m in range(KI):
                            if k == 0:
                                done(dve, "xpad", j, m + 1)
                                if m == 0:
                                    done(dve, "xc", j, 0)
                                    done(dve, "hist", j, 0)
                                ins = dve.tensor_scalar(acc[:, m, :], xpad[:, m, TAPS - 1:], conv_w[:, m, TAPS - 1:],
                                                        conv_b[:, m:m + 1], ALU.mult, ALU.add)
                            else:
                                done(dve, "conv", j, KI * (k - 1) + m + 1)
                                ins = dve.scalar_tensor_tensor(acc[:, m, :], xpad[:, m, k - 1:k - 1 + TW],
                                                               conv_w[:, m, k - 1:k], acc[:, m, :],
                                                               ALU.mult, ALU.add)
                            S["conv"].inc(ins)

                def history(j, half):
                    done(dve, "conv", j)
                    if half < HALVES - 1:
                        S["hist"].inc(dve.tensor_copy(hist, xpad[:, :, TW:]))
                    else:
                        S["hist"].inc(dve.memset(hist, 0.0))

                def running_delta(i):
                    done(dve, "soft", i)
                    done(dve, "run", i, 0)
                    done(dve, "bd", i, 0)
                    S["delta"].inc(dve.scalar_tensor_tensor(delta[:, :], ps[:, 3, :], 0.0, soft[:, :],
                                                            ALU.max, ALU.add))
                    done(dve, "delta", i)
                    done(dve, "wd", i, 0)
                    done(dve, "tokp", i, 0)
                    S["run"].inc(dve.tensor_tensor_scan(run[:, :], const("scan_keep"), delta[:, :], 0.0,
                                                        ALU.mult, ALU.add))
                    done(dve, "rep", i, 2)
                    S["bd"].inc(dve.tensor_tensor(bd[:, :], delta[:, :], ps[:, 4, :], ALU.mult))
                    done(dve, "run", i)
                    S["refs8"].inc(dve.tensor_tensor(
                        refs8[:, :, :], run[:, :].rearrange("p (c b q) -> p c b q", c=TILE, q=Q)[:, :, :, Q - 1],
                        const("ref_of").unsqueeze(1).to_broadcast([P, TILE, NB]), ALU.mult))
                    done(dve, "refs8", i)
                    S["ref"].inc(dve.tensor_reduce(ref[:, :], refs8[:, :, :], AX.X, ALU.add))
                    done(dve, "ref", i)
                    for c in range(TILE):
                        S["a2"].inc(dve.tensor_scalar(a2[:, c * P:(c + 1) * P], run[:, c * P:(c + 1) * P],
                                                      ref[:, c:c + 1], 0.0, ALU.subtract, ALU.min))
                    done(dve, "h", i, 0)
                    for c in range(TILE):
                        S["a1"].inc(dve.tensor_scalar(a1[:, c * P:(c + 1) * P], run[:, c * P:(c + 1) * P],
                                                      ref[:, c:c + 1], 0.0, ALU.subtract, ALU.max))

                def factors(i):
                    done(dve, "e2", i)
                    done(dve, "bd", i)
                    done(dve, "off", i, 0)
                    S["f2"].inc(dve.tensor_tensor(f2[:, :], a2[:, :], bd[:, :], ALU.mult))
                    done(dve, "e1", i)
                    done(dve, "rep", i, 3)
                    done(dve, "y", i, 0)
                    S["f1p"].inc(dve.tensor_tensor(f1p[:, :], a1[:, :], ps[:, 5, :], ALU.mult))
                    done(dve, "f1p", i)
                    S["f1"].inc(dve.tensor_tensor(chunks(f1), chunks(f1p),
                                                  const("block_of_state").unsqueeze(1).to_broadcast([P, TILE, P]), ALU.mult))
                    done(dve, "tok", i)
                    S["wd"].inc(dve.tensor_tensor(wd[:, :], chunks(run)[:, :, P - 1], tok_d[:, :, 0], ALU.subtract))
                    done(dve, "wd", i)
                    S["w2a"].inc(dve.tensor_tensor(
                        w2a[:, :, :], wd[:, :].unsqueeze(2).to_broadcast([P, TILE, NS]),
                        a_row[:, :].unsqueeze(1).to_broadcast([P, TILE, NS]), ALU.mult))

                def block_exponents(i):
                    done(dve, "crep", i)
                    for c in range(TILE):
                        S["a3"].inc(dve.tensor_scalar(a3[:, c, :], ps[:, 2, TOKC + c * Q:TOKC + (c + 1) * Q],
                                                      tok_d[:, c, 0:1], 0.0, ALU.subtract, ALU.max))
                    done(dve, "a3", i)
                    S["ah"].inc(dve.tensor_tensor(
                        big[:, :, :].rearrange("p c (t n) -> p (c t) n", n=NS),
                        a3[:, :, :].rearrange("p c t -> p (c t)").unsqueeze(2).to_broadcast([P, TILE * Q, NS]),
                        a_row[:, :].unsqueeze(1).to_broadcast([P, TILE * Q, NS]), ALU.mult))

                def matrix(i):
                    done(dve, "w2e", i)
                    done(dve, "hc", i, 0)
                    S["w2"].inc(dve.tensor_tensor(w2[:, :, :], w2a[:, :, :], tok_b[:, :, 0:NS], ALU.mult))
                    done(dve, "off", i)
                    done(dve, "y", i, 0)
                    S["mt0"].inc(dve.tensor_tensor(
                        mt[:, :, :], ps[:, 3, :].rearrange("p (c t) -> p c t", c=TILE),
                        const("earlier_block").unsqueeze(1).to_broadcast([P, TILE, P]), ALU.mult))
                    done(dve, "eh", i)
                    S["g1"].inc(dve.tensor_tensor(big[:, :, :], big[:, :, :],
                                                  ps[:, 6:8, :].rearrange("p u (v n) -> p (u v) n", v=2), ALU.mult))
                    done(dve, "g1", i)
                    wide = big[:, :, :].rearrange("p c (t n) -> p c t n", n=NS)
                    S["g2"].inc(dve.tensor_tensor(wide, wide, tok_b[:, :, 0:NS].unsqueeze(2).to_broadcast([P, TILE, Q, NS]),
                                                  ALU.mult))
                    done(dve, "g2", i)
                    S["md"].inc(dve.tensor_reduce(md[:, :, :], wide, AX.X, ALU.add))
                    done(dve, "md", i)
                    S["mdx"].inc(dve.tensor_tensor(
                        mdx[:, :, :].rearrange("p c (b t) -> p c b t", t=Q),
                        md[:, :, :].unsqueeze(2).to_broadcast([P, TILE, NB, Q]),
                        const("own_block_causal").rearrange("p (b t) -> p b t", t=Q).unsqueeze(1).to_broadcast([P, TILE, NB, Q]),
                        ALU.mult))
                    done(dve, "mt0", i)
                    done(dve, "mdx", i)
                    S["mt"].inc(dve.tensor_tensor(mt[:, :, :], mt[:, :, :], mdx[:, :, :], ALU.add))

                def states(i, half):
                    done(dve, "hc", i)
                    for c in range(TILE):
                        to = h[:, half, c + 1, :] if c + 1 < TILE else h[:, 1 - half, 0, :]
                        own = ps[32 * c:32 * c + NS, 3, :]
                        if c or half:
                            done(dve, "h", i, c)
                            S["h"].inc(dve.scalar_tensor_tensor(
                                to, h[:, half, c, :], a1[0:NS, (c + 1) * P - 1:(c + 1) * P], own, ALU.mult, ALU.add))
                        else:
                            S["h"].inc(dve.tensor_copy(to, own))

                def gate(i, half):
                    done(dve, "y", i)
                    done(dve, "o", i, 0)
                    for m in range(KI):
                        S["ys"].inc(dve.scalar_tensor_tensor(
                            chunks(y[:, m, :]), chunks(xcT[:, half, m, :]), d_skip[:, m:m + 1],
                            ps[:, 4:4 + TILE, m * P:(m + 1) * P], ALU.mult, ALU.add))
                    done(dve, "ys", i)
                    S["yg"].inc(dve.tensor_tensor(y[:, :, :], y[:, :, :], zs[:, half, :, :], ALU.mult))

                def residual(i):
                    for j in range(2):
                        done(dve, "o", i, j + 1)
                        xs = X[:, ds(i * TILE + 2 * j, 2), :]
                        S["res"].inc(dve.tensor_tensor(xs, xs, ps[:, 2 + j, :].rearrange("p (c d) -> p c d", c=2), ALU.add))

                def first():
                    dve.wait_ge(x_first, 16)
                    nrm.vector_stats(dve, 0)
                    nrm.vector_apply(dve, 0)
                    dve.wait_ge(x_in, 16 * (TILES - 1))
                    dve.wait_ge(w_loaded, W_LOADS)
                    dve.wait_ge(cleared, 1)
                    nrm.vector_stats(dve, 1)
                    convolve(0, (0, 1))
                    nrm.vector_apply(dve, 1)
                    dve.wait_ge(a_ready, 2)

                def end(i, half):
                    gate(i, half)
                    residual(i)

                def step(i, half, front, far, before):
                    if before:
                        gate(i - 1, 1 - half)
                    convolve(i, (2, 3))
                    history(i, half)
                    if before:
                        residual(i - 1)
                    x_copies(i)
                    running_delta(i)
                    factors(i)
                    if front:
                        convolve(i + 1, (0, 1))
                    if far:
                        nrm.vector_stats(dve, i + 2)
                    block_exponents(i)
                    if far:
                        nrm.vector_apply(dve, i + 2)
                    matrix(i)
                    states(i, half)

                steps(dve, first, step, end)
                done(dve, "res", TILES - 1)

            @block.tensor
            def _(pe):
                def project(j, ms):
                    for m in ms:
                        if m == 0:
                            pe.wait_ge(nrm.xnT.sem, nrm.xnT.at(j, KD))
                        elif m >= 2:
                            done(pe, "xpad", j, min(m - 1, KI))
                            if m - 1 > KI:
                                done(pe, "zs", j, m - 1 - KI)
                        for k in range(KD):
                            t = pe.matmul(ps[:, m % 2, :], w_in[:, k, m * P:(m + 1) * P],
                                          kept["xnT"][:, k, :], start=(k == 0), stop=(k == KD - 1))
                        S["xz"].inc(t)

                def turn(j):
                    done(pe, "zs", j, 0)
                    nrm.tensor_turn(pe, j, 0)

                def first():
                    pe.wait_ge(const_loaded, 16)
                    turn(0)
                    pe.wait_ge(w_in_loaded, 16 * KD)
                    project(0, range(2 * KI))
                    turn(1)
                    pe.wait_ge(w_loaded, W_LOADS)

                def end(i, half):
                    done(pe, "yg", i)
                    done(pe, "h", i)
                    for c in range(TILE):
                        for m in range(KI):
                            t = pe.matmul(ps[:, 2 + c // 2, (c % 2) * D:(c % 2 + 1) * D], y[:, m, c * P:(c + 1) * P],
                                          w_out[:, m, :], start=(m == 0), stop=(m == KI - 1))
                        if c % 2:
                            S["o"].inc(t)

                def turn_x(i, half, c):
                    if c >= 2:
                        done(pe, "xt", i, c - 1)
                    for m in range(KI):
                        t = pe.transpose(ps[:, 6 + c % 2, m * P:(m + 1) * P], xcT[:, half, m, c * P:(c + 1) * P], const("ident"))
                    S["xtp"].inc(t)

                def step(i, half, front, far, before):
                    if front:
                        project(i + 1, (0, 1))
                    if before:
                        end(i - 1, 1 - half)
                    done(pe, "xc", i)
                    done(pe, "res", i, 0)
                    for m in range(KI):
                        t = pe.matmul(ps[0:XD, 2, :], w_x[:, m, :], xcT[:, half, m, :], start=(m == 0), stop=(m == KI - 1))
                    S["xdT"].inc(t)
                    done(pe, "ys", i, 0)
                    turn_x(i, half, 0)
                    turn_x(i, half, 1)
                    done(pe, "xd", i)
                    for j, name in enumerate(("sel_delta", "sel_b", "sel_c")):
                        S["rep"].inc(pe.matmul(ps[:, 3 + j, :], const(name, XD), xd[:, :], start=True, stop=True))
                    turn_x(i, half, 2)
                    turn_x(i, half, 3)
                    for c in range(TILE):
                        pe.transpose(ps[:, 2, c * XD:(c + 1) * XD], xd[:, c * P:(c + 1) * P], const("ident", XD)[:, 0:XD])
                    if front:
                        project(i + 1, (2,))
                    done(pe, "run", i)
                    done(pe, "bd", i)
                    for j, src in enumerate((run, bd)):
                        for c in range(TILE):
                            o = TILE * (XD + 32 * j) + 32 * c
                            t = pe.matmul(ps[:, 2, o:o + 32], src[:, c * P:(c + 1) * P], const("ident")[:, 0:32],
                                          start=True, stop=True)
                    S["tokp"].inc(t)
                    if front:
                        project(i + 1, (3,))
                    done(pe, "f1", i)
                    for c in range(TILE):
                        t = pe.matmul(ps[:, 3, c * P:(c + 1) * P], f2[:, c * P:(c + 1) * P],
                                      f1[:, c * P:(c + 1) * P], start=True, stop=True)
                    S["off"].inc(t)
                    done(pe, "cm", i)
                    done(pe, "xt", i)
                    for c in range(TILE):
                        pe.matmul(ps[:, 6 + c // 2, (c % 2) * Q * NS:(c % 2 + 1) * Q * NS], const("same_block"),
                                  cm[:, c, 0:Q * NS], start=True, stop=True)
                        t = pe.matmul(ps[:, 2, TOKC + c * Q:TOKC + (c + 1) * Q], const("same_block"),
                                      cm[:, c, Q * NS:], start=True, stop=True)
                    S["crep"].inc(t)
                    if front:
                        project(i + 1, range(KI, 2 * KI - 1))
                    done(pe, "xt", i)
                    done(pe, "w2", i)
                    done(pe, "mt0", i)
                    for c in range(TILE):
                        t = pe.matmul(ps[32 * c:32 * c + NS, 3, :], w2[:, c, :], xtok[:, c, :], start=True, stop=True)
                    S["hc"].inc(t)
                    if front:
                        project(i + 1, (2 * KI - 1,))
                    done(pe, "mt", i)
                    for c in range(TILE):
                        has_state = c or half
                        if c:
                            done(pe, "h", i, c)
                        for m in range(KI):
                            t = pe.matmul(ps[:, 4 + c, m * P:(m + 1) * P], xtok[:, c, m * P:(m + 1) * P],
                                          mt[:, c, :], start=True, stop=not has_state)
                            if has_state:
                                t = pe.matmul(ps[:, 4 + c, m * P:(m + 1) * P], h[:, half, c, m * P:(m + 1) * P],
                                              f1p[0:NS, c * P:(c + 1) * P], start=False, stop=True)
                        S["y"].inc(t)
                        if c == 0 and far:
                            turn(i + 2)

                steps(pe, first, step, end)

    nc.clear_and_free_semaphores(sems)
    nc.all_engine_barrier()


def sparse_ffn(nc, a, kept, const, scratch):
    X, ps = kept["X"], kept["ps"]
    with ExitStack() as ctx:
        def sb(name, shape, dt=F32):
            return ctx.enter_context(nc.sbuf_tensor(name, shape, dt))

        def sem(name):
            return ctx.enter_context(nc.semaphore(name))

        picks = sb("picks", [P, TOKENS], mybir.dt.bfloat16)
        with ExitStack() as sel_ctx:
            selT = sel_ctx.enter_context(nc.sbuf_tensor("selT", [P, KD, ES, GROUPS], F32))
            pick_tokens(nc, a, kept, const, picks, selT)
            apply_experts(nc, a, kept, const, selT, scratch)
        scatter_tokens(nc, a, kept, picks, scratch)


def signals(sem, prefix, **per):
    return {name: Signal(sem(f"{prefix}_{name}"), n) for name, n in per.items()}


def waiter(S):
    def done(eng, name, i, n=None):
        s = S[name]
        eng.wait_ge(s.sem, s.at(i, s.per if n is None else n))
    return done


def pick_tokens(nc, a, kept, const, picks, selT):
    X, ps = kept["X"], kept["ps"]
    with ExitStack() as ctx:
        def sb(name, shape, dt=F32):
            return ctx.enter_context(nc.sbuf_tensor(name, shape, dt))

        def sem(name):
            return ctx.enter_context(nc.semaphore(name))

        ctrl = sb("ctrl", [P, KD, 2 * ES])
        lg = sb("logits", [P, TW])
        gmax = sb("gmax", [P, TW // GRP])
        one = sb("one_hot", [P, TW])
        spread = sb("spread", [P, TILE, GC, ES])
        loaded = sem("p_loaded")
        nrm = Norm("p", sem, kept, const)
        S = signals(sem, "p", lgp=1, lg=1, gmax=1, one=1, picks=1, turned=1, spread=1, gath=KD * TILE, sel=KD * TILE)
        done = waiter(S)
        with nc.Block() as block:

            @block.sync
            def _(sp):
                sp.dma_start(ctrl[:, :, :], a["ctrl_twice"].rearrange("(k p) n -> p k n", p=P)).then_inc(loaded, 16)
                prime(sp, S, nrm)

            @block.gpsimd
            def _(pool):
                with pool.Fori(0, TILES) as i:
                    nrm.gpsimd_rstd(pool, i)

            @block.scalar
            def _(act):
                with act.Fori(0, TILES) as i:
                    nrm.scalar_copy(act, i, 0)
                    for c in range(TILE):
                        for k in range(KD):
                            n = KD * c + k
                            done(act, "gath", i, n + 1)
                            S["sel"].inc(act.copy(
                                selT[:, k, :, ds((i * TILE + c) * GC, GC)].rearrange("p e g -> p g e"),
                                ps[:, 4 + n % 4, :].rearrange("p (g e) -> p g e", g=GC)))

            @block.vector
            def _(dve):
                with dve.Fori(0, TILES) as i:
                    nrm.vector_stats(dve, i)
                    done(dve, "gath", i, 0)
                    nrm.vector_apply(dve, i)
                    done(dve, "lgp", i)
                    groups = lambda t: t.rearrange("p (g t) -> p g t", t=GRP)
                    S["lg"].inc(dve.tensor_tensor(groups(lg[:, :]), groups(ps[:, 2, :]),
                                                  const("tie").unsqueeze(1).to_broadcast([P, TW // GRP, GRP]), ALU.add))
                    done(dve, "lg", i)
                    S["gmax"].inc(dve.tensor_reduce(gmax[:, :], groups(lg[:, :]), AX.X, ALU.max))
                    done(dve, "gmax", i)
                    S["one"].inc(dve.tensor_tensor(groups(one[:, :]), groups(lg[:, :]),
                                                   gmax[:, :].unsqueeze(2).to_broadcast([P, TW // GRP, GRP]), ALU.is_equal))
                    done(dve, "one", i)
                    S["picks"].inc(dve.tensor_tensor(
                        picks[:, ds(i * TW, TW)].rearrange("p (c t) -> p c t", c=TILE),
                        one[:, :].rearrange("p (c t) -> p c t", c=TILE),
                        const("parity").unsqueeze(1).to_broadcast([P, TILE, P]), ALU.mult))
                    done(dve, "turned", i)
                    S["spread"].inc(dve.tensor_tensor(
                        spread[:, :, :, :],
                        ps[:, 3, :].rearrange("p (c e) -> p c e", c=TILE)[:, :, 0:ES].unsqueeze(2).to_broadcast([P, TILE, GC, ES]),
                        const("group_of").unsqueeze(1).unsqueeze(3).to_broadcast([P, TILE, GC, ES]), ALU.mult))

            @block.tensor
            def _(pe):
                pe.wait_ge(loaded, 16)
                with pe.Fori(0, TILES) as i:
                    nrm.tensor_turn(pe, i, 0)
                    pe.wait_ge(nrm.xnT.sem, nrm.xnT.at(i, KD))
                    done(pe, "lg", i, 0)
                    for k in range(KD):
                        t = pe.matmul(ps[:, 2, :], ctrl[:, k, :], kept["xnT"][:, k, :], start=(k == 0), stop=(k == KD - 1))
                    S["lgp"].inc(t)
                    done(pe, "one", i)
                    done(pe, "spread", i, 0)
                    for c in range(TILE):
                        t = pe.transpose(ps[:, 3, c * P:(c + 1) * P], one[:, c * P:(c + 1) * P], const("ident"))
                    S["turned"].inc(t)
                    done(pe, "spread", i)
                    for c in range(TILE):
                        for k in range(KD):
                            n = KD * c + k
                            if n < 4:
                                done(pe, "sel", i, 0)
                            else:
                                done(pe, "sel", i, n - 3)
                            S["gath"].inc(pe.matmul(ps[:, 4 + n % 4, :], kept["xn"][:, c, k * P:(k + 1) * P],
                                                    spread[:, c, :, :].rearrange("p g e -> p (g e)"), start=True, stop=True))


def apply_experts(nc, a, kept, const, selT, scratch):
    ps, xn, xnT = kept["ps"], kept["xn"], kept["xnT"]
    SLOTS = 4
    with ExitStack() as ctx:
        def sb(name, shape, dt=F32):
            return ctx.enter_context(nc.sbuf_tensor(name, shape, dt))

        def sem(name):
            return ctx.enter_context(nc.semaphore(name))

        f1 = sb("f1w", [P, KD, SLOTS, 2 * FF])
        f2 = sb("f2w", [P, SLOTS, D])
        bias = sb("ffn_bias", [P, PAIRS])
        inter = sb("inter_sb", [P, 2, 2, 2, D])
        loaded = sem("e_loaded")
        f1_in = [sem(f"e_f1_in{u}") for u in range(SLOTS)]
        f2_in = [sem(f"e_f2_in{u}") for u in range(SLOTS)]
        stored = [sem(f"e_stored{u}") for u in range(2)]
        S = signals(sem, "e", innp=SLOTS, inner=2 * SLOTS, outp=SLOTS, low=SLOTS, high=SLOTS)
        done = waiter(S)
        f1_d = a["L0_ffn_f1"].rearrange("(k p) e s f -> p k (e s f)", p=P)
        f2_d = a["L0_ffn_f2"].rearrange("e s f d -> (e s f) d")
        out_d = scratch.rearrange("(h g) e d -> g h (e d)", g=P)

        def stored_before(eng, i, v):
            eng.wait_ge(stored[v % 2], PRIME + 16 * (2 * i + v // 2))

        with nc.Block() as block:

            @block.gpsimd
            def _(pool):
                pool.dma_start(bias[:, :], a["ffn_bias_cols"]).then_inc(loaded, 16)
                with pool.Fori(0, PAIRS // SLOTS) as i:
                    for u in range(SLOTS):
                        pair = i * SLOTS + u
                        done(pool, "innp", i, u + 1 - SLOTS)
                        pool.dma_start(f1[:, :, u, :], f1_d[:, :, ds(pair * P, P)]).then_inc(f1_in[u], 16)
                        done(pool, "outp", i, u + 1 - SLOTS)
                        pool.dma_start(f2[:, u, :], f2_d[ds(pair * P, P), :]).then_inc(f2_in[u], 16)

            @block.tensor
            def _(pe):
                def second(i, u, n):
                    done(pe, "inner", i, 2 * n + 2)
                    done(pe, "low", i, n - 1)
                    done(pe, "high", i, n - 1)
                    pe.wait_ge(f2_in[u], 16 * (i + 1) if n >= 0 else 16 * i)
                    for g in range(2):
                        for e in range(2):
                            t = pe.matmul(ps[:, 2 + 2 * (u % 2) + e, g * D:(g + 1) * D],
                                          xn[e * FF:(e + 1) * FF, u, g * P:(g + 1) * P],
                                          f2[e * FF:(e + 1) * FF, u, :], start=True, stop=True)
                    S["outp"].inc(t)

                with pe.Fori(0, PAIRS // SLOTS) as i:
                    for u in range(SLOTS):
                        pe.wait_ge(f1_in[u], 16 * (i + 1))
                        done(pe, "inner", i, 2 * (u - 1))
                        for e in range(2):
                            for k in range(KD):
                                t = pe.matmul(ps[:, u % 2, e * GROUPS:(e + 1) * GROUPS], f1[:, k, u, :],
                                              selT[:, k, ds((i * SLOTS + u) * 2 + e, 1), :].rearrange("p o g -> p (o g)"),
                                              start=(k == 0), stop=(k == KD - 1))
                        S["innp"].inc(t)
                        if u:
                            second(i, u - 1, u - 1)
                    second(i, SLOTS - 1, SLOTS - 1)

            @block.scalar
            def _(act):
                act.wait_ge(loaded, 16)
                with act.Fori(0, PAIRS // SLOTS) as i:
                    for u in range(SLOTS + 1):
                        if u < SLOTS:
                            done(act, "innp", i, u + 1)
                            done(act, "outp", i, u + 1 - SLOTS)
                            for e in range(2):
                                r = slice(e * FF, (e + 1) * FF)
                                S["inner"].inc(act.activation(xn[r, u, :], ps[r, u % 2, e * GROUPS:(e + 1) * GROUPS],
                                                              ACT.Relu, bias=bias[r, ds(i * SLOTS + u, 1)]))
                        if u:
                            v = u - 1
                            done(act, "outp", i, v + 1)
                            stored_before(act, i, v)
                            S["high"].inc(act.copy(inter[:, v % 2, :, 1, :],
                                                   ps[:, 3 + 2 * (v % 2), :].rearrange("p (g d) -> p g d", g=2)))

            @block.vector
            def _(dve):
                with dve.Fori(0, PAIRS // SLOTS) as i:
                    for v in range(SLOTS):
                        done(dve, "outp", i, v + 1)
                        stored_before(dve, i, v)
                        S["low"].inc(dve.tensor_copy(inter[:, v % 2, :, 0, :],
                                                     ps[:, 2 + 2 * (v % 2), :].rearrange("p (g d) -> p g d", g=2)))

            @block.sync
            def _(sp):
                prime(sp, S)
                for s in stored:
                    sp.sem_inc(s, PRIME)
                with sp.Fori(0, PAIRS // SLOTS) as i:
                    for v in range(SLOTS):
                        done(sp, "low", i, v + 1)
                        done(sp, "high", i, v + 1)
                        sp.dma_start(out_d[:, :, ds((i * SLOTS + v) * 2 * D, 2 * D)],
                                     inter[:, v % 2, :, :, :].rearrange("p g e d -> p g (e d)")).then_inc(stored[v % 2], 16)
                for s in stored:
                    sp.wait_ge(s, PRIME + 16 * PAIRS // 2)


def scatter_tokens(nc, a, kept, picks, scratch):
    X, ps = kept["X"], kept["ps"]
    GP = GC // 2
    with ExitStack() as ctx:
        def sb(name, shape, dt=F32):
            return ctx.enter_context(nc.sbuf_tensor(name, shape, dt))

        def sem(name):
            return ctx.enter_context(nc.semaphore(name))

        inter = sb("inter_in", [P, 2, TILE, GP, D])
        hot = sb("hot", [P, 2, TW])
        read = [sem(f"s_read{u}") for u in range(2 * TILE)]
        S = signals(sem, "s", hot=2, added=2 * TILE, res=2 * TILE)
        done = waiter(S)
        src = scratch.rearrange("(c q r) e d -> c (r e) q d", q=GP, r=2)
        with nc.Block() as block:

            @block.sync
            def _(sp):
                prime(sp, S)
                with sp.Fori(0, TILES // 2) as i:
                    for u in range(2 * TILE):
                        done(sp, "added", i, u + 1 - 2 * TILE)
                        sp.dma_start(inter[:, u // TILE, u % TILE, :, :],
                                     src[ds(i * 2 * TILE + u, 1)].rearrange("o p q d -> p (o q) d")).then_inc(read[u], 16)

            @block.scalar
            def _(act):
                with act.Fori(0, TILES // 2) as i:
                    for t in range(2):
                        done(act, "added", i, TILE * (t - 1))
                        S["hot"].inc(act.copy(hot[:, t, :], picks[:, ds((2 * i + t) * TW, TW)]))

            @block.tensor
            def _(pe):
                with pe.Fori(0, TILES // 2) as i:
                    for u in range(2 * TILE):
                        t, c = u // TILE, u % TILE
                        done(pe, "hot", i, t + 1)
                        done(pe, "res", i, u - 7)
                        pe.wait_ge(read[u], 16 * (i + 1))
                        for q in range(GP):
                            m = pe.matmul(ps[32 * q:32 * (q + 1), u, 0:D], hot[:, t, c * P + 32 * q:c * P + 32 * (q + 1)],
                                          inter[:, t, c, q, :], start=True, stop=True)
                        S["added"].inc(m)

            @block.vector
            def _(dve):
                with dve.Fori(0, TILES // 2) as i:
                    for u in range(2 * TILE):
                        done(dve, "added", i, u + 1)
                        xs = X[:, ds(i * 2 * TILE + u, 1), :]
                        S["res"].inc(dve.tensor_tensor(xs, xs, ps[:, u, 0:D].unsqueeze(1), ALU.add))
                    done(dve, "res", i)

def attention(nc, a, kept, const, nxt):
    X, ps, xnT = kept["X"], kept["ps"], kept["xnT"]
    NJ = len(HEADS_OF)
    rows = [NORM_ROW[j] + len(HEADS_OF[j]) for j in range(NJ)]
    with ExitStack() as ctx:
        def sb(name, shape, dt=F32):
            return ctx.enter_context(nc.sbuf_tensor(name, shape, dt))

        def sem(name):
            return ctx.enter_context(nc.semaphore(name))

        wqkv = sb("wqkv", [P, KD, 3 * D])
        wo = sb("wo", [P, KD, D])
        rfb = sb("rfb", [P, NJ * 6 * NF])
        b_out = sb("b_out", [P, D])
        kT = sb("kT", [P, NJ, TW])
        qT = sb("qT", [P, NJ, HALVES, TW])
        sq = sb("sq", [P, 2 * NJ, TW])
        v = sb("v", [P, TILE, D])
        ones = sb("ones", [P, 2 * HD])
        kp = sb("kp", [P, TILE, HEADS * NF])
        kvT = sb("kvT", [P, 2 * D])
        kv = sb("kv", [P, 2, HP, 2 * HD])
        qp = sb("qp", [P, HP, TW])
        den = sb("den", [P, TW])
        rec = sb("rec", [P, TW])
        oT = sb("oT", [P, KD, TW])
        ew = sb("ew", [P, KD, 2, D])
        loaded, cleared = sem("a_loaded"), sem("a_cleared")
        ew_read, next_loaded = sem("a_ew_read"), sem("a_next_loaded")
        nrm = Norm("a", sem, kept, const)
        S = signals(sem, "a", qk=2 * NJ, sq=2 * NJ, copy=2 * NJ, nsq=2 * NJ, norm=2 * NJ,
                    vp=2, v=2, kpp=TILE, kp=TILE, kvp=TILE,
                    qpp=HP, qp=HP, nd=KD, den=KD, rec=KD, oT=KD, yp=2, res=2, bias=1)
        S2 = signals(sem, "a", kvT=1, kvp2=1, kv=2, ew_hi=1, ew_lo=1)
        done = waiter({**S, **S2})

        proj_bank = lambda n: 2 + n if n < 5 else 1
        feature_bank = lambda half, p: 2 + (half * HP + p) % 3

        def rows_of(eng, first, batch):
            first()
            with eng.Fori(0, B - 1) as b:
                batch(b, True)
            batch(B - 1, False)

        with nc.Block() as block:

            @block.sync
            def _(sp):
                for dst, src in ((wqkv[:, :, :], a["w_qkv_T"].rearrange("(k p) n -> p k n", p=P)),
                                 (rfb[:, :], a["rf_blocks"]),
                                 (wo[:, :, :], a["w_out_T"].rearrange("(k p) n -> p k n", p=P)),
                                 (b_out[:, :], a["L1_attn_b_out"].rearrange("(o n) -> o n", o=1).to_broadcast([P, D]))):
                    sp.dma_start(dst, src).then_inc(loaded, 16)
                prime(sp, {**S, **S2}, nrm)
                for dst, src in ((nxt["rw"][:, :, :], a["L1_ffn_router_w"].rearrange("(k p) e -> p k e", p=P)),
                                 (nxt["rb"][:, :], a["L1_ffn_router_b"].rearrange("(o n) -> o n", o=1).to_broadcast([P, NE])),
                                 (nxt["eb"][:, :], a["L1_ffn_expert_b"])):
                    sp.dma_start(dst, src).then_inc(next_loaded, 16)
                e_w = a["L1_ffn_expert_w"].rearrange("e (k p) d -> p k e d", p=P)
                with sp.Fori(0, B) as b:
                    done(sp, "ew_lo", b, 0)
                    for k in range(KD):
                        sp.dma_start(ew[:, k, :, :], e_w[:, k, ds(2 * b, 2), :]).then_inc(ew_read, 16)
                sp.wait_ge(next_loaded, 48)

            @block.gpsimd
            def _(pool):
                pool.memset(kv[:, :, :, :], 0.0).then_inc(cleared, 1)
                pool.memset(ones[:, :], 1.0).then_inc(cleared, 1)

                def batch(b, more):
                    nrm.gpsimd_rstd(pool, b * HALVES + 1)
                    if more:
                        nrm.gpsimd_rstd(pool, b * HALVES + HALVES)
                    hi, lo = (nxt[n][:, :, ds(2 * b, 2), :] for n in ("w_hi", "w_lo"))
                    pool.wait_ge(ew_read, 16 * KD * (b + 1))
                    S2["ew_hi"].inc(pool.tensor_copy(hi, ew[:, :, :, :]))
                    done(pool, "ew_hi", b)
                    S2["ew_lo"].inc(pool.tensor_tensor(lo, ew[:, :, :, :], hi.bitcast(F32), ALU.subtract))
                    for half in range(HALVES):
                        i = b * HALVES + half
                        done(pool, "res", i)
                        xs = X[:, ds(i * TILE, TILE), :]
                        S["bias"].inc(pool.tensor_tensor(xs, xs, b_out[:, :].unsqueeze(1).to_broadcast([P, TILE, D]), ALU.add))

                nrm.gpsimd_rstd(pool, 0)
                pool.wait_ge(loaded, 64)
                rows_of(pool, lambda: None, batch)

            @block.scalar
            def _(act):
                def squares(i, some):
                    for n in some:
                        j = n % NJ
                        done(act, "qk", i, n + 1)
                        if n == 0:
                            done(act, "nsq", i, 0)
                        S["sq"].inc(act.activation(sq[0:NORM_ROW[j], n, :], ps[0:NORM_ROW[j], proj_bank(n), :], ACT.Square))

                def roots(i, half):
                    for n in range(2 * NJ):
                        j = n % NJ
                        r = slice(NORM_ROW[j], rows[j])
                        done(act, "nsq", i, n + 1)
                        if n == 0:
                            done(act, "kpp", i, 0)
                        if n == NJ and half == 0:
                            done(act, "qpp", i, 0)
                        dst = kT[r, j, :] if n < NJ else qT[r, j, half, :]
                        S["norm"].inc(act.activation(dst, ps[r, proj_bank(n), :], ACT.Sqrt))

                def front(j):
                    done(act, "vp", j, 0)
                    nrm.scalar_copy(act, j, 0)
                    squares(j, range(NJ))

                def batch(b, more):
                    for half in range(HALVES):
                        i = b * HALVES + half
                        squares(i, range(NJ, 2 * NJ))
                        roots(i, half)
                        for c in range(TILE):
                            done(act, "kpp", i, c + 1)
                            done(act, "kvp", i, c + 1 - TILE)
                            S["kp"].inc(act.activation(kp[:, c, :].rearrange("p (u n) -> p u n", u=2),
                                                       ps[:, 2 + 2 * (c % 2):4 + 2 * (c % 2), :], ACT.Exp, scale=NF ** -0.5))
                        if half == 0:
                            front(i + 1)
                    for half in range(HALVES):
                        i = b * HALVES + half
                        for p in range(HP):
                            done(act, "qpp", i, p + 1)
                            done(act, "nd", i, p // 4 - 1)
                            S["qp"].inc(act.activation(qp[:, p, :], ps[:, feature_bank(half, p), :], ACT.Exp, scale=NF ** -0.5))
                    if more:
                        front(b * HALVES + HALVES)

                rows_of(act, lambda: front(0), batch)

            @block.vector
            def _(dve):
                def copies(i, half, some):
                    for n in some:
                        j = n % NJ
                        done(dve, "sq", i, n + 1)
                        if n == 0:
                            done(dve, "kpp", i, 0)
                        if n == NJ and half == 0:
                            done(dve, "qpp", i, 0)
                        dst = kT[0:NORM_ROW[j], j, :] if n < NJ else qT[0:NORM_ROW[j], j, half, :]
                        S["copy"].inc(dve.tensor_copy(dst, ps[0:NORM_ROW[j], proj_bank(n), :]))

                def values(i, u):
                    done(dve, "vp", i, u + 1)
                    if u == 0:
                        done(dve, "kvp", i, 0)
                    S["v"].inc(dve.tensor_copy(v[:, 2 * u:2 * u + 2, :], ps[:, 0, :].rearrange("p (c d) -> p c d", c=2)))

                def norm(j):
                    nrm.vector_stats(dve, j)
                    nrm.vector_apply(dve, j)

                def quotients(i, k):
                    done(dve, "nd", i, k + 1)
                    done(dve, "rec", i, k)
                    S["den"].inc(dve.tensor_scalar(den[:, :], ps[:, 6, :], 1e-6, None, ALU.add))
                    done(dve, "den", i, k + 1)
                    done(dve, "oT", i, k)
                    S["rec"].inc(dve.reciprocal(rec[:, :], den[:, :]))
                    done(dve, "rec", i, k + 1)
                    done(dve, "yp", i, 0)
                    S["oT"].inc(dve.tensor_tensor(oT[:, k, :], ps[:, 5, :], rec[:, :], ALU.mult))

                def residual(i):
                    for u in range(2):
                        done(dve, "yp", i, u + 1)
                        xs = X[:, ds(i * TILE + 2 * u, 2), :]
                        S["res"].inc(dve.tensor_tensor(xs, xs, ps[:, 7 - u, :].rearrange("p (c d) -> p c d", c=2), ALU.add))

                def batch(b, more):
                    for half in range(HALVES):
                        i = b * HALVES + half
                        copies(i, half, range(NJ, 2 * NJ))
                        values(i, 0)
                        values(i, 1)
                        if half == 0 or more:
                            norm(i + 1)
                        if half == 0:
                            copies(i + 1, 1, range(NJ))
                    done(dve, "kvp", b * HALVES + 1)
                    S2["kvT"].inc(dve.tensor_copy(kvT[:, :], ps[:, 7, :]))
                    done(dve, "kvp2", b)
                    done(dve, "nd", b * HALVES, 0)
                    for e in range(2):
                        r, w = slice(e * NF, (e + 1) * NF), slice(e * HD, (e + 1) * HD)
                        S2["kv"].inc(dve.tensor_copy(kv[r, :, :, w].rearrange("p a b w -> p (a b) w"),
                                                     ps[r, 0, :].rearrange("p (a w) -> p a w", w=2 * HD)[:, :, w]))
                    i = b * HALVES
                    quotients(i, 0)
                    quotients(i, 1)
                    residual(i)
                    quotients(i + 1, 0)
                    quotients(i + 1, 1)
                    if more:
                        copies(i + 2, 0, range(NJ))
                    residual(i + 1)

                def first():
                    dve.wait_ge(cleared, 2)
                    norm(0)
                    copies(0, 0, range(NJ))

                rows_of(dve, first, batch)

            @block.tensor
            def _(pe):
                def project(i, some):
                    for n in some:
                        j = n % NJ
                        w = (D if n < NJ else 0) + HEADS_OF[j][0] * HD
                        for k in range(KD):
                            t = pe.matmul(ps[0:NORM_ROW[j], proj_bank(n), :], wqkv[:, k, w:w + NORM_ROW[j]],
                                          xnT[:, k, :], start=(k == 0), stop=(k == KD - 1))
                        S["qk"].inc(t)

                def turn(j):
                    done(pe, "v", j, 0)
                    done(pe, "norm", j, 0)
                    nrm.tensor_turn(pe, j, 0)

                def keys(j, half):
                    pe.wait_ge(nrm.xnT.sem, nrm.xnT.at(j, KD))
                    done(pe, "kp", j, 0)
                    done(pe, "qp", j - half, 0)
                    project(j, range(NJ))

                def values(i, u):
                    done(pe, "v", i, u)
                    for c in range(2):
                        for k in range(KD):
                            t = pe.matmul(ps[:, 0, c * D:(c + 1) * D], xnT[:, k, (2 * u + c) * P:(2 * u + c + 1) * P],
                                          wqkv[:, k, 2 * D:3 * D], start=(k == 0), stop=(k == KD - 1))
                    S["vp"].inc(t)

                def square_sums(i, some):
                    for n in some:
                        j = n % NJ
                        if j == 0:
                            done(pe, "sq", i, n + NJ)
                        S["nsq"].inc(pe.matmul(ps[NORM_ROW[j]:rows[j], proj_bank(n), :],
                                               const("head_of")[0:NORM_ROW[j], 0:len(HEADS_OF[j])],
                                               sq[0:NORM_ROW[j], n, :], start=True, stop=True))

                def key_features(i, c):
                    for name in ("norm", "copy"):
                        done(pe, name, i, 3 if c == 0 else 4)
                    if c >= 2:
                        done(pe, "kp", i, c - 1)
                    at = 0
                    for j in range(NJ):
                        left, src = len(HEADS_OF[j]) * NF, j * 6 * NF
                        while left:
                            n = min(left, 512 - at % 512)
                            t = pe.matmul(ps[:, 2 + 2 * (c % 2) + at // 512, at % 512:at % 512 + n],
                                          kT[0:rows[j], j, c * P:(c + 1) * P], rfb[0:rows[j], src:src + n],
                                          start=True, stop=True)
                            at, src, left = at + n, src + n, left - n
                    S["kpp"].inc(t)

                def keys_by_values(i, half, c):
                    done(pe, "kp", i, c + 1)
                    if c == 0:
                        done(pe, "v", i)
                        done(pe, "res", i - half, 0)
                    for kind in range(2):
                        for r in range(2):
                            for q in range(4):
                                p, col = 4 * r + q, (2 * kind + r) * P
                                t = pe.matmul(ps[32 * q:32 * (q + 1), 7, col:col + P],
                                              v[:, c, p * 32:(p + 1) * 32] if kind == 0 else ones[:, :],
                                              kp[:, c, p * P:(p + 1) * P],
                                              start=half == 0 and c == 0 and kind == 0 and r == 0,
                                              stop=half == HALVES - 1 and c == TILE - 1,
                                              skip_group_check=True)
                    S["kvp"].inc(t)

                def query_features(i, half, some):
                    for p in some:
                        if p == 0:
                            done(pe, "copy", i)
                            done(pe, "norm", i)
                            if half == 0:
                                done(pe, "kp", i + 1)
                        done(pe, "qp", i, p - 2)
                        j, src = p // 3, (p // 3) * 6 * NF + (p % 3) * P
                        S["qpp"].inc(pe.matmul(ps[:, feature_bank(half, p), :], rfb[0:rows[j], src:src + P],
                                               qT[0:rows[j], j, half, :], start=True, stop=True))

                def turn_kv(b):
                    done(pe, "kvT", b)
                    done(pe, "v", b * HALVES + 1)
                    for r in range(4):
                        t = pe.transpose(ps[:, 0, r * P:(r + 1) * P], kvT[:, r * P:(r + 1) * P], const("ident"))
                    S2["kvp2"].inc(t)

                def outputs(i, r):
                    done(pe, "qp", i, 4 * r + 4)
                    done(pe, "oT", i, r)
                    done(pe, "res", i, 0)
                    for kind in range(2):
                        for q in range(4):
                            t = pe.matmul(ps[32 * q:32 * (q + 1), 5 + kind, :], kv[:, kind, 4 * r + q, :],
                                          qp[:, 4 * r + q, :], start=True, stop=True)
                    S["nd"].inc(t)

                def project_out(i):
                    done(pe, "oT", i)
                    done(pe, "res", i, 0)
                    for u in range(2):
                        for c in range(2):
                            for k in range(KD):
                                t = pe.matmul(ps[:, 7 - u, c * D:(c + 1) * D], oT[:, k, (2 * u + c) * P:(2 * u + c + 1) * P],
                                              wo[:, k, :], start=(k == 0), stop=(k == KD - 1))
                        S["yp"].inc(t)

                def batch(b, more):
                    i = b * HALVES
                    for half in range(HALVES):
                        t = i + half
                        done(pe, "res", i, 0)
                        project(t, range(NJ, 2 * NJ))
                        values(t, 0)
                        square_sums(t, range(NJ))
                        values(t, 1)
                        square_sums(t, range(NJ, 2 * NJ))
                        key_features(t, 0)
                        key_features(t, 1)
                        keys_by_values(t, half, 0)
                        key_features(t, 2)
                        keys_by_values(t, half, 1)
                        key_features(t, 3)
                        keys_by_values(t, half, 2)
                        if half == 0:
                            turn(t + 1)
                            keys_by_values(t, half, 3)
                            keys(t + 1, 1)
                    query_features(i, 0, (0,))
                    keys_by_values(i + 1, 1, 3)
                    query_features(i, 0, (1, 2, 3))
                    turn_kv(b)
                    query_features(i, 0, (4,))
                    done(pe, "kv", b)
                    outputs(i, 0)
                    query_features(i, 0, (5, 6, 7))
                    query_features(i + 1, 1, (0,))
                    outputs(i, 1)
                    query_features(i + 1, 1, (1, 2, 3))
                    project_out(i)
                    query_features(i + 1, 1, (4,))
                    outputs(i + 1, 0)
                    query_features(i + 1, 1, (5, 6, 7))
                    if more:
                        turn(i + 2)
                    outputs(i + 1, 1)
                    if more:
                        keys(i + 2, 0)
                    project_out(i + 1)

                def first():
                    pe.wait_ge(loaded, 64)
                    turn(0)
                    keys(0, 0)

                rows_of(pe, first, batch)


def experts(nc, a, kept, const, nxt, out):
    X, ps, xnT = kept["X"], kept["ps"], kept["xnT"]
    w_hi, w_lo, rw, rb, eb = (nxt[n] for n in ("w_hi", "w_lo", "rw", "rb", "eb"))
    with ExitStack() as ctx:
        def sb(name, shape, dt=F32):
            return ctx.enter_context(nc.sbuf_tensor(name, shape, dt))

        def sem(name):
            return ctx.enter_context(nc.semaphore(name))

        x_hi = sb("x_hi", [P, 2, KD, TW], F32R)
        x_lo = sb("x_lo", [P, 2, KD, TW], F32R)
        lg = sb("router_logits", [P, TILE, NE])
        z = sb("z", [P, TILE, NE])
        top = sb("top", [P, TILE])
        total = sb("total", [P, TILE])
        gate = sb("gate", [P, TILE])
        one = sb("one", [P, TILE, NE])
        best = sb("best", [P, TILE])
        g = sb("g", [P, 2, TILE, NE])
        gT = sb("gT", [NE, 2, TW])
        stored = sem("stored")
        nrm = Norm("x", sem, kept, const)
        S = signals(sem, "x", hi=KD, lo=KD, lgp=1, lg=1, top=1, z=1, ez=1, total=1, gate=1, one=1, ranked=1,
                    best=1, first=1, g=1, gTp=1, gT=1, biasp=TILE, bias=TILE, yp=TILE * NE // 2, acc=TILE * NE)
        done = waiter(S)

        def steps(eng, front_first, step):
            front_first()
            with eng.Fori(0, TILES // 2 - 1) as k:
                step(2 * k, 0, True)
                step(2 * k + 1, 1, True)
            step(TILES - 2, 0, True)
            step(TILES - 1, 1, False)

        with nc.Block() as block:

            @block.sync
            def _(sp):
                prime(sp, S, nrm)
                o = out.rearrange("b (c p) d -> p (b c) d", p=P)
                with sp.Fori(0, TILES) as i:
                    done(sp, "bias", i)
                    sp.dma_start(o[:, ds(i * TILE, TILE)], X[:, ds(i * TILE, TILE)]).then_inc(stored, 16)
                sp.wait_ge(stored, 16 * TILES)

            @block.gpsimd
            def _(pool):
                def step(i, slot, front):
                    if front:
                        nrm.gpsimd_rstd(pool, i + 1)

                steps(pool, lambda: nrm.gpsimd_rstd(pool, 0), step)

            @block.scalar
            def _(act):
                def front(j, slot, after=True):
                    if after:
                        done(act, "lo", j, 0)
                        done(act, "lgp", j, 0)
                    nrm.scalar_copy(act, j, 0)
                    for d in range(KD):
                        act.wait_ge(nrm.xnT.sem, nrm.xnT.at(j, d + 1))
                        S["hi"].inc(act.copy(x_hi[:, slot, d, :], xnT[:, d, :]))
                    done(act, "z", j)
                    S["ez"].inc(act.activation(z[:, :, :], z[:, :, :], ACT.Exp))
                    done(act, "gTp", j)
                    if after:
                        done(act, "biasp", j - 1, 0)
                    S["gT"].inc(act.copy(gT[:, slot, :], ps[0:NE, 3, :]))

                def step(i, slot, with_front):
                    if with_front:
                        front(i + 1, 1 - slot)

                steps(act, lambda: front(0, 0, False), step)

            @block.vector
            def _(dve):
                wide = lambda t: t[:, :].unsqueeze(2).to_broadcast([P, TILE, NE])

                def split(j, slot):
                    for d in range(KD):
                        done(dve, "hi", j, d + 1)
                        S["lo"].inc(dve.tensor_tensor(x_lo[:, slot, d, :], xnT[:, d, :],
                                                      x_hi[:, slot, d, :].bitcast(F32), ALU.subtract))

                def route(j, slot):
                    done(dve, "lgp", j)
                    S["lg"].inc(dve.tensor_tensor(lg[:, :, :], ps[:, 2, 0:TILE * NE].rearrange("p (c e) -> p c e", e=NE),
                                                  rb[:, :].unsqueeze(1).to_broadcast([P, TILE, NE]), ALU.add))
                    done(dve, "lg", j)
                    S["top"].inc(dve.tensor_reduce(top[:, :], lg[:, :, :], AX.X, ALU.max))
                    done(dve, "top", j)
                    S["z"].inc(dve.tensor_tensor(z[:, :, :], lg[:, :, :], wide(top), ALU.subtract))
                    S["one"].inc(dve.tensor_tensor(one[:, :, :], lg[:, :, :], wide(top), ALU.is_equal))
                    done(dve, "one", j)
                    S["ranked"].inc(dve.tensor_tensor(one[:, :, :], one[:, :, :],
                                                      const("rank").unsqueeze(1).to_broadcast([P, TILE, NE]), ALU.mult))
                    done(dve, "ranked", j)
                    S["best"].inc(dve.tensor_reduce(best[:, :], one[:, :, :], AX.X, ALU.max))
                    done(dve, "best", j)
                    S["first"].inc(dve.tensor_tensor(one[:, :, :], one[:, :, :], wide(best), ALU.is_equal))
                    done(dve, "ez", j)
                    S["total"].inc(dve.tensor_reduce(total[:, :], z[:, :, :], AX.X, ALU.add))
                    done(dve, "total", j)
                    S["gate"].inc(dve.reciprocal(gate[:, :], total[:, :]))
                    done(dve, "gate", j)
                    done(dve, "first", j)
                    S["g"].inc(dve.tensor_tensor(g[:, slot, :, :], one[:, :, :], wide(gate), ALU.mult))

                def add(i, slot, c):
                    xs = X[:, ds(i * TILE + c, 1), :]
                    done(dve, "g", i)
                    for e in range(NE):
                        if e % 2 == 0:
                            done(dve, "yp", i, (c * NE + e) // 2 + 1)
                        if e:
                            done(dve, "acc", i, c * NE + e)
                        S["acc"].inc(dve.scalar_tensor_tensor(
                            xs, ps[:, 4 + e // 2, (e % 2) * D:(e % 2 + 1) * D].unsqueeze(1), g[:, slot, c, e:e + 1], xs,
                            ALU.mult, ALU.add))
                    done(dve, "biasp", i, c + 1)
                    done(dve, "acc", i, (c + 1) * NE)
                    S["bias"].inc(dve.tensor_tensor(xs, xs, ps[:, 2, D:2 * D].unsqueeze(1), ALU.add))

                def first():
                    nrm.vector_stats(dve, 0)
                    nrm.vector_apply(dve, 0)
                    split(0, 0)
                    route(0, 0)

                def step(i, slot, front):
                    if front:
                        nrm.vector_stats(dve, i + 1)
                    add(i, slot, 0)
                    if front:
                        nrm.vector_apply(dve, i + 1)
                    add(i, slot, 1)
                    if front:
                        split(i + 1, 1 - slot)
                    add(i, slot, 2)
                    if front:
                        route(i + 1, 1 - slot)
                    add(i, slot, 3)

                steps(dve, first, step)

            @block.tensor
            def _(pe):
                def turn(j):
                    if not (isinstance(j, int) and j == 0):
                        done(pe, "lo", j, 0)
                    nrm.tensor_turn(pe, j, 0)

                def router(j):
                    for d in range(KD):
                        pe.wait_ge(nrm.xnT.sem, nrm.xnT.at(j, d + 1))
                    done(pe, "lg", j, 0)
                    for c in range(TILE):
                        for k in range(KD):
                            t = pe.matmul(ps[:, 2, c * NE:(c + 1) * NE], xnT[:, k, c * P:(c + 1) * P], rw[:, k, :],
                                          start=(k == 0), stop=(k == KD - 1))
                    S["lgp"].inc(t)

                def turn_gates(j, slot):
                    done(pe, "g", j)
                    done(pe, "gT", j, 0)
                    for c in range(TILE):
                        t = pe.transpose(ps[0:NE, 3, c * P:(c + 1) * P], g[:, slot, c, :], const("ident"))
                    S["gTp"].inc(t)

                def products(i, slot, c):
                    if c == 0:
                        done(pe, "lo", i)
                    for q in range(NE // 2):
                        done(pe, "acc", i, (c - 1) * NE + 2 * q + 2)
                        n = 0
                        for x, w in ((x_hi, w_hi), (x_hi, w_lo), (x_lo, w_hi)):
                            for k in range(KD):
                                t = pe.matmul(ps[:, 4 + q, :], x[:, slot, k, c * P:(c + 1) * P],
                                              w[:, k, 2 * q:2 * q + 2, :].rearrange("p e d -> p (e d)"),
                                              start=(n == 0), stop=(n == 3 * KD - 1))
                                n += 1
                        S["yp"].inc(t)
                    done(pe, "gT", i)
                    done(pe, "bias", i, c)
                    S["biasp"].inc(pe.matmul(ps[:, 2, D:2 * D], gT[:, slot, c * P:(c + 1) * P], eb[:, :], start=True, stop=True))

                def step(i, slot, front):
                    products(i, slot, 0)
                    products(i, slot, 1)
                    if front:
                        turn(i + 1)
                    products(i, slot, 2)
                    if front:
                        done(pe, "bias", i, 3)
                        router(i + 1)
                        done(pe, "lg", i + 1)
                    products(i, slot, 3)
                    if front:
                        turn_gates(i + 1, 1 - slot)

                def first():
                    turn(0)
                    router(0)
                    turn_gates(0, 0)

                steps(pe, first, step)


PHASES = 4
_INS = ['L0_attn_x', 'L0_attn_W_in', 'L0_attn_conv_w', 'L0_attn_W_x', 'L0_attn_A_log', 'L0_attn_W_out',
        'L0_ffn_f1', 'L0_ffn_f2', 'L1_attn_b_out', 'L1_ffn_router_w', 'L1_ffn_router_b', 'L1_ffn_expert_w',
        'L1_ffn_expert_b']


def laid_out(inputs):
    w_qkv = np.asarray(inputs["L1_attn_w_qkv"])
    rf = np.asarray(inputs["L1_attn_random_features"])
    rfb = np.zeros((P, 3 * 6 * NF), np.float32)
    for j, heads in enumerate(HEADS_OF):
        for n, _ in enumerate(heads):
            c = (j * 6 + n) * NF
            rfb[n * HD:(n + 1) * HD, c:c + NF] = rf.T
            rfb[NORM_ROW[j] + n, c:c + NF] = -float(NF) ** 0.5
    ctrl = np.asarray(inputs["L0_ffn_controller"]).reshape(D, ES)
    return {
        "conv_b_cols": np.asarray(inputs["L0_attn_conv_b"]).reshape(KI, P).T,
        "d_cols": np.asarray(inputs["L0_attn_D_param"]).reshape(KI, P).T,
        "ctrl_twice": np.concatenate([ctrl, ctrl], 1),
        "ffn_bias_cols": np.asarray(inputs["L0_ffn_bias"]).reshape(PAIRS, P).T,
        "w_qkv_T": w_qkv.T,
        "w_out_T": np.asarray(inputs["L1_attn_w_out"]).T,
        "rf_blocks": rfb,
    }


def kernel(**inputs):
    import numpy as _np
    import concourse.bacc as _bacc
    from concourse import mybir as _mybir
    from concourse.bass_utils import run_bass_kernel_spmd as _run

    nc = _bacc.Bacc("TRN2", target_bir_lowering=False, num_devices=1)
    arrays, a = {}, {}
    consts, at = shape_constants()
    given = {n: inputs[n] for n in _INS}
    for name, v in {**given, **laid_out(inputs), "consts": consts}.items():
        v = _np.ascontiguousarray(v)
        arrays[f"in_{name}"] = v
        a[name] = nc.dram_tensor(f"in_{name}", v.shape, _mybir.dt.from_np(v.dtype), kind="ExternalInput").ap()
    out = nc.dram_tensor("out", (B, L, D), F32, kind="ExternalOutput").ap()
    scratch = nc.dram_tensor("inter", (GROUPS, ES, D), F32, kind="Internal").ap()
    build(nc, a, out, a["consts"], at, scratch, PHASES)
    r = _run(nc, [arrays], core_ids=[0])
    return r.results[0]["out"]
```

```python
from contextlib import ExitStack

import concourse.bass as bass
import numpy as np
from concourse import mybir

ALU = mybir.AluOpType
ACT = mybir.ActivationFunctionType
AX = mybir.AxisListType
F32 = mybir.dt.float32
F32R = mybir.dt.float32r
ds = bass.ds

P = 128
B, L, D = 4, 1024, 256
TOKENS = B * L
CHUNKS = TOKENS // P
TILE = 4
TW = TILE * P
TILES = CHUNKS // TILE
KD = D // P
HALVES = L // TW
EPS = 1e-5
DI, NS, TAPS = 512, 16, 4
KI = DI // P
Q = 16
NB = P // Q
XD = 1 + 2 * NS
GRP = 16
ES, FF = 64, 64
GC = P // GRP
GROUPS = TOKENS // GRP
PAIRS = ES // 2
HEADS, HD, NF = 16, 16, 64
HP = HEADS // 2
HEADS_OF = [range(0, 6), range(6, 12), range(12, 16)]
NORM_ROW = [96, 96, 64]
NE = 8


def shape_constants():
    p = np.arange(P)
    parts = {
        "ident": np.eye(P),
        "sel_delta": np.repeat((p == 0)[:, None], P, 1),
        "sel_b": (p[:, None] == 1 + p[None, :] % NS),
        "sel_c": (p[:, None] == 1 + NS + p[None, :] % NS),
        "place_n": np.repeat((p[:, None] % Q) == np.arange(Q)[None, :], NS, 1),
        "place": (p[:, None] % Q) == np.arange(Q)[None, :],
        "same_block": (p[:, None] // Q) == (p[None, :] // Q),
        "earlier_block": (p[:, None] // Q) < (p[None, :] // Q),
        "own_block_causal": ((p[:, None] // Q) == (p[None, :] // Q)) & (p[None, :] >= p[:, None]),
        "ref_of": (p[:, None] // NS - 1) == np.arange(NB)[None, :],
        "block_of_state": (p[:, None] // NS) == (p[None, :] // Q),
        "scan_keep": np.repeat((np.arange(TW) % P != 0)[None, :], P, 0),
        "tie": np.repeat(np.linspace(0.0, 1e-6, GRP, dtype=np.float32)[None, :], P, 0),
        "group_of": (p[:, None] // GRP) == np.arange(GC)[None, :],
        "parity": (p[:, None] // ES) == ((p[None, :] // GRP) % 2),
        "eps": np.full((P, 1), EPS),
        "head_of": (p[:, None] // HD) == np.arange(6)[None, :],
        "minus_half": np.full((P, 1), -0.5),
        "rank": np.repeat(np.arange(NE, 0, -1)[None, :], P, 0),
    }
    at, n = {}, 0
    for k, v in parts.items():
        at[k] = (n, n + v.shape[1])
        n += v.shape[1]
    return np.concatenate([v.astype(np.float32) for v in parts.values()], 1), at


PRIME = 16


class Signal:

    def __init__(self, sem, per):
        self.sem, self.per = sem, per

    def inc(self, instruction):
        instruction.then_inc(self.sem, 1)

    def at(self, i, n):
        return i * self.per + n + PRIME


def build(nc, a, out, consts, at, scratch):
    with ExitStack() as ctx:
        kept = dict(
            X=ctx.enter_context(nc.sbuf_tensor("X", [P, CHUNKS, D], F32)),
            C=ctx.enter_context(nc.sbuf_tensor("consts", [P, consts.shape[1]], F32)),
            ps=ctx.enter_context(nc.psum_tensor("ps", [P, 8, 512], F32)),
            mv=ctx.enter_context(nc.sbuf_tensor("mean_var", [P, TILE, 2], F32)),
            st=ctx.enter_context(nc.sbuf_tensor("stats", [P, TILE, 6], F32)),
            carrier=ctx.enter_context(nc.sbuf_tensor("carrier", [P, 1], F32)),
            ve=ctx.enter_context(nc.sbuf_tensor("var_eps", [P, TILE], F32)),
            rstd=ctx.enter_context(nc.sbuf_tensor("rstd", [P, TILE], F32)),
            xn=ctx.enter_context(nc.sbuf_tensor("xn", [P, TILE, D], F32)),
            xnT=ctx.enter_context(nc.sbuf_tensor("xnT", [P, KD, TW], F32)),
        )

        def const(name, rows=P):
            lo, hi = at[name]
            return kept["C"][0:rows, lo:hi]

        mamba(nc, a, consts, kept, const)
        sparse_ffn(nc, a, kept, const, scratch)
        nxt = dict(
            w_hi=ctx.enter_context(nc.sbuf_tensor("ew_hi", [P, KD, NE, D], F32R)),
            w_lo=ctx.enter_context(nc.sbuf_tensor("ew_lo", [P, KD, NE, D], F32R)),
            rw=ctx.enter_context(nc.sbuf_tensor("rw", [P, KD, NE], F32)),
            rb=ctx.enter_context(nc.sbuf_tensor("rb", [P, NE], F32)),
            eb=ctx.enter_context(nc.sbuf_tensor("eb", [NE, D], F32)),
        )
        attention(nc, a, kept, const, nxt)
        experts(nc, a, kept, const, nxt, out)


def prime(eng, S, *norms):
    for s in [*S.values(), *(x for n in norms for x in (n.stats, n.mv, n.ve, n.rstd, n.xn, n.turned, n.xnT))]:
        eng.sem_inc(s.sem, PRIME)


class Norm:

    def __init__(self, name, sem, kept, const):
        self.k, self.const = kept, const
        self.stats = Signal(sem(f"{name}_stats"), TILE)
        self.mv = Signal(sem(f"{name}_mean_var"), TILE)
        self.ve = Signal(sem(f"{name}_var_eps"), 1)
        self.rstd = Signal(sem(f"{name}_rstd"), 1)
        self.xn = Signal(sem(f"{name}_xn"), TILE)
        self.turned = Signal(sem(f"{name}_xn_turned"), KD)
        self.xnT = Signal(sem(f"{name}_xnT"), KD)

    def vector_stats(self, dve, i):
        k = self.k
        for c in range(TILE):
            self.stats.inc(dve.bn_stats(k["st"][:, c:c + 1, :], k["X"][:, ds(i * TILE + c, 1), :]))
        dve.wait_ge(self.stats.sem, self.stats.at(i, TILE))
        dve.wait_ge(self.ve.sem, self.ve.at(i, 0))
        dve.wait_ge(self.xn.sem, self.xn.at(i, 0))
        dve.tensor_copy(k["carrier"][:, :], k["st"][:, 0, 0:1])
        for c in range(TILE):
            self.mv.inc(dve.bn_aggr(k["mv"][:, c, :], k["st"][:, c, :]))

    def gpsimd_rstd(self, pool, i):
        k = self.k
        pool.wait_ge(self.mv.sem, self.mv.at(i, TILE))
        pool.wait_ge(self.xn.sem, self.xn.at(i, 0))
        self.ve.inc(pool.tensor_tensor(k["ve"][:, :], k["mv"][:, :, 1],
                                       self.const("eps").to_broadcast([P, TILE]), ALU.add))
        pool.wait_ge(self.ve.sem, self.ve.at(i, 1))
        self.rstd.inc(pool.tensor_tensor(k["rstd"][:, :], k["ve"][:, :],
                                         self.const("minus_half").to_broadcast([P, TILE]), ALU.pow))

    def vector_apply(self, dve, i, xn=None):
        k = self.k
        xn = k["xn"] if xn is None else xn
        dve.wait_ge(self.rstd.sem, self.rstd.at(i, 1))
        dve.wait_ge(self.turned.sem, self.turned.at(i, 0))
        for c in range(TILE):
            self.xn.inc(dve.tensor_scalar(xn[:, c:c + 1, :], k["X"][:, ds(i * TILE + c, 1), :],
                                          k["mv"][:, c, 0:1], k["rstd"][:, c:c + 1],
                                          ALU.subtract, ALU.mult))

    def tensor_turn(self, pe, i, banks, xn=None):
        k = self.k
        xn = k["xn"] if xn is None else xn
        pe.wait_ge(self.xn.sem, self.xn.at(i, TILE))
        pe.wait_ge(self.xnT.sem, self.xnT.at(i, 0))
        for d in range(KD):
            for c in range(TILE):
                t = pe.transpose(k["ps"][:, banks + d, c * P:(c + 1) * P],
                                 xn[:, c, d * P:(d + 1) * P], self.const("ident"))
            self.turned.inc(t)

    def scalar_copy(self, act, i, banks, xnT=None):
        k = self.k
        xnT = k["xnT"] if xnT is None else xnT
        for d in range(KD):
            act.wait_ge(self.turned.sem, self.turned.at(i, d + 1))
            self.xnT.inc(act.copy(xnT[:, d, :], k["ps"][:, banks + d, :]))


def mamba(nc, a, consts, kept, const):
    sems = []
    with ExitStack() as ctx:
        def sb(name, shape):
            return ctx.enter_context(nc.sbuf_tensor(name, shape, F32))

        def sem(name):
            sems.append(nc.alloc_semaphore(name))
            return sems[-1]

        X, ps = kept["X"], kept["ps"]
        w_in = sb("w_in", [P, KD, 2 * DI])
        w_x = sb("w_x", [P, KI, XD])
        w_out = sb("w_out", [P, KI, D])
        conv_w = sb("conv_w", [P, KI, TAPS])
        conv_b = sb("conv_b", [P, KI])
        d_skip = sb("d_skip", [P, KI])
        a_col = sb("a_col", [P, 1])
        a_neg = sb("a_neg", [P, 1])
        a_row = sb("a_row", [P, NS])
        xpad = sb("xpad", [P, KI, TAPS - 1 + TW])
        acc = sb("acc", [P, KI, TW])
        xcT = sb("xcT", [P, 2, KI, TW])
        zs = sb("zs", [P, 2, KI, TW])
        xd = sb("xd", [XD, TW])
        soft = sb("soft", [P, TW])
        delta = sb("delta", [P, TW])
        run = sb("run", [P, TW])
        bd = sb("bd", [P, TW])
        refs8 = sb("refs8", [P, TILE, NB])
        ref = sb("ref", [P, TILE])
        a2 = sb("a2", [P, TW])
        a1 = sb("a1", [P, TW])
        f2 = sb("f2", [P, TW])
        f1p = sb("f1p", [P, TW])
        f1 = sb("f1", [P, TW])
        TOKC = TILE * (XD + 32 + 32)
        tok = sb("tok", [P, TOKC])
        tok_x = tok[:, 0:TILE * XD].rearrange("p (c k) -> p c k", c=TILE)
        tok_d = tok[:, TILE * XD:TILE * (XD + 32)].rearrange("p (c k) -> p c k", c=TILE)
        tok_b = tok[:, TILE * (XD + 32):TOKC].rearrange("p (c k) -> p c k", c=TILE)
        cm = sb("cm", [P, TILE, Q * NS + Q])
        a3 = sb("a3", [P, TILE, Q])
        big = sb("big", [P, TILE, Q * NS])
        md = sb("md", [P, TILE, Q])
        mdx = sb("mdx", [P, TILE, P])
        mt = sb("mt", [P, TILE, P])
        wd = sb("wd", [P, TILE])
        w2a = sb("w2a", [P, TILE, NS])
        w2 = sb("w2", [P, TILE, NS])
        xtok = sb("xtok", [P, TILE, DI])
        h = sb("h", [NS, HALVES, TILE, DI])
        y = sb("y", [P, KI, TW])

        x_first, x_in = sem("x_tile0_in"), sem("x_in")
        const_loaded, w_in_loaded, w_loaded = sem("const_loaded"), sem("w_in_loaded"), sem("w_loaded")
        W_LOADS = 16 * (6 + NB)
        a_abs, a_ready, cleared = sem("a_abs"), sem("a_ready"), sem("cleared")
        xnT_of = [kept["xnT"], sb("xnT_odd", [P, KD, TW])]
        CONV = [(0, 0), (0, 1), (1, 0), (1, 1), (0, 2), (0, 3), (1, 2), (1, 3)] + [(k, m) for k in (2, 3) for m in range(KI)]
        convolved = lambda k, m: CONV.index((k, m)) + 1
        nrm = Norm("m", sem, kept, const)
        S = {}
        for name, per in dict(xz=2 * KI, xpad=KI, zc=KI, zs=1, conv=TAPS * KI, hist=1, xc=KI, xdT=1,
                              xd=1, rep=3, soft=3, delta=1, run=1, bd=1, refs8=1, ref=1, a2=TILE,
                              a1=TILE, e2=1, e1=1, f2=1, f1p=1, f1=1, tokp=1, tok=1, cm=2, crep=1,
                              a3=TILE, ah=1, eh=1, g1=1, g2=1, md=1, mdx=1, off=1, mt0=1, mt=1, wd=1,
                              w2a=1, w2e=1, w2=1, xtp=TILE, xt=TILE, y=TILE, hc=1, h=TILE,
                              ys=TILE * KI, yg=TILE, o=2, res=2).items():
            S[name] = Signal(sem(f"m_{name}"), per)

        def done(eng, name, i, n=None):
            s = S[name]
            eng.wait_ge(s.sem, s.at(i, s.per if n is None else n))

        with nc.Block() as block:

            @block.sync
            def _(sp):
                xin = a["L0_attn_x"].rearrange("b (c p) d -> p (b c) d", p=P)
                x_tile = lambda t: (X[:, TILE * t:TILE * (t + 1)], xin[:, TILE * t:TILE * (t + 1)])
                sp.dma_start(*x_tile(0)).then_inc(x_first, 16)
                for k in range(KD):
                    sp.dma_start(w_in[:, k, :], a["L0_attn_W_in"].rearrange("(k p) n -> k p n", p=P)[k]).then_inc(w_in_loaded, 16)
                prime(sp, S, nrm)
                sp.dma_start(w_x[:, :, :], a["L0_attn_W_x"].rearrange("(k p) n -> p k n", p=P)).then_inc(w_loaded, 16)
                sp.dma_start(*x_tile(1)).then_inc(x_in, 16)
                sp.dma_start(w_out[:, :, :], a["L0_attn_W_out"].rearrange("(k p) n -> p k n", p=P)).then_inc(w_loaded, 16)
                for t in range(2, TILES):
                    sp.dma_start(*x_tile(t)).then_inc(x_in, 16)

            def steps(eng, front_first, step, end=None):
                front_first()
                step(0, 0, front=True, far=True, before=False)
                with eng.Fori(0, B - 2) as b:
                    step(b * HALVES + 1, 1, front=True, far=True, before=True)
                    step(b * HALVES + 2, 0, front=True, far=True, before=True)
                step(TILES - 3, 1, front=True, far=True, before=True)
                step(TILES - 2, 0, front=True, far=False, before=True)
                step(TILES - 1, 1, front=False, far=False, before=True)
                if end:
                    end(TILES - 1, 1)

            @block.gpsimd
            def _(pool):
                pool.wait_ge(const_loaded, 16)

                def first():
                    nrm.gpsimd_rstd(pool, 0)
                    nrm.gpsimd_rstd(pool, 1)

                def gate(i, half):
                    done(pool, "zs", i)
                    for c in range(TILE):
                        w = slice(c * P, (c + 1) * P)
                        done(pool, "ys", i, (c + 1) * KI)
                        S["yg"].inc(pool.tensor_tensor(y[:, :, w], y[:, :, w], zs[:, half, :, w], ALU.mult))

                def step(i, half, front, far, before):
                    if before:
                        gate(i - 1, 1 - half)
                    done(pool, "tok", i)
                    done(pool, "crep", i, 0)
                    S["cm"].inc(pool.tensor_tensor(
                        cm[:, :, 0:Q * NS].rearrange("p c (t n) -> p c t n", n=NS),
                        tok_x[:, :, 1 + NS:XD].unsqueeze(2).to_broadcast([P, TILE, Q, NS]),
                        const("place_n").rearrange("p (t n) -> p t n", n=NS).unsqueeze(1).to_broadcast([P, TILE, Q, NS]),
                        ALU.mult))
                    S["cm"].inc(pool.tensor_tensor(
                        cm[:, :, Q * NS:], tok_d[:, :, 0:1].to_broadcast([P, TILE, Q]),
                        const("place").unsqueeze(1).to_broadcast([P, TILE, Q]), ALU.mult))
                    if far:
                        nrm.gpsimd_rstd(pool, i + 2)

                steps(pool, first, step, gate)

            @block.scalar
            def _(act):
                act.dma_start(kept["C"][:, :], consts).then_inc(const_loaded, 16)
                for dst, src in (
                    (a_row[:, :], a["L0_attn_A_log"].rearrange("(o n) -> o n", o=1).to_broadcast([P, NS])),
                    (conv_w[:, :, :], a["L0_attn_conv_w"].rearrange("(k p) n -> p k n", p=P)),
                    (conv_b[:, :], a["conv_b_cols"]),
                    (d_skip[:, :], a["d_cols"]),
                ):
                    act.dma_start(dst, src).then_inc(w_loaded, 16)
                for b in range(NB):
                    act.dma_start(a_col[b * NS:(b + 1) * NS, :],
                                  a["L0_attn_A_log"].rearrange("(n o) -> n o", o=1)).then_inc(w_loaded, 16)

                def copy_x(j, ms):
                    for m in ms:
                        done(act, "xz", j, m + 1)
                        if m == 0:
                            done(act, "hist", j, 0)
                        S["xpad"].inc(act.copy(xpad[:, m, TAPS - 1:], ps[:, m % 2, :]))

                def copy_z(j, par, ms):
                    for m in ms:
                        done(act, "xz", j, KI + m + 1)
                        if m == 0:
                            done(act, "yg", j - 1, 0)
                        S["zc"].inc(act.copy(zs[:, par, m, :], ps[:, m % 2, :]))

                def silu_z(j, par):
                    done(act, "zc", j)
                    S["zs"].inc(act.activation(zs[:, par, :, :], zs[:, par, :, :], ACT.Silu))

                def silu_x(j, par):
                    done(act, "ys", j - 1, 0)
                    for m in range(KI):
                        done(act, "conv", j, convolved(TAPS - 1, m))
                        S["xc"].inc(act.activation(xcT[:, par, m, :], acc[:, m, :], ACT.Silu))

                def first():
                    nrm.scalar_copy(act, 0, 0, xnT_of[0])
                    copy_x(0, range(KI))
                    copy_z(0, 0, range(KI))
                    nrm.scalar_copy(act, 1, 4, xnT_of[1])
                    act.wait_ge(w_loaded, W_LOADS)
                    act.activation(a_col[:, :], a_col[:, :], ACT.Exp).then_inc(a_abs, 1)
                    act.activation(a_row[:, :], a_row[:, :], ACT.Exp).then_inc(a_abs, 1)
                    act.wait_ge(a_abs, 2)
                    act.mul(a_neg[:, :], a_col[:, :], -1.0).then_inc(a_ready, 1)
                    act.mul(a_row[:, :], a_row[:, :], -1.0).then_inc(a_ready, 1)
                    act.wait_ge(a_ready, 2)

                def step(i, half, front, far, before):
                    silu_x(i, half)
                    silu_z(i, half)
                    if front:
                        copy_x(i + 1, (0, 1))
                    done(act, "xdT", i)
                    done(act, "tokp", i, 0)
                    S["xd"].inc(act.copy(xd[:, :], ps[0:XD, 2, :]))
                    done(act, "rep", i, 1)
                    done(act, "delta", i, 0)
                    S["soft"].inc(act.activation(soft[:, :], ps[:, 3, :], ACT.Abs))
                    done(act, "soft", i, 1)
                    S["soft"].inc(act.activation(soft[:, :], soft[:, :], ACT.Exp, scale=-1.0))
                    done(act, "soft", i, 2)
                    S["soft"].inc(act.activation(soft[:, :], soft[:, :], ACT.Ln, bias=1.0))
                    if front:
                        copy_x(i + 1, (2, 3))
                    done(act, "a2", i)
                    S["e2"].inc(act.activation(a2[:, :], a2[:, :], ACT.Exp, scale=a_col[:, :]))
                    done(act, "a1", i)
                    S["e1"].inc(act.activation(a1[:, :], a1[:, :], ACT.Exp, scale=a_neg[:, :]))
                    done(act, "tokp", i)
                    done(act, "w2", i, 0)
                    done(act, "cm", i, 0)
                    done(act, "g2", i, 0)
                    S["tok"].inc(act.copy(tok[:, :], ps[:, 2, 0:TOKC]))
                    if front:
                        copy_z(i + 1, 1 - half, (0,))
                    done(act, "w2a", i)
                    S["w2e"].inc(act.activation(w2a[:, :, :], w2a[:, :, :], ACT.Exp))
                    if front:
                        copy_z(i + 1, 1 - half, (1,))
                    done(act, "ah", i)
                    S["eh"].inc(act.activation(big[:, :, :], big[:, :, :], ACT.Exp))
                    if front:
                        copy_z(i + 1, 1 - half, (2, 3))
                    if far:
                        nrm.scalar_copy(act, i + 2, 4, xnT_of[half])

                steps(act, first, step)

            @block.vector
            def _(dve):
                hist = xpad[:, :, 0:TAPS - 1]
                chunks = lambda t: t[:, :].rearrange("p (c t) -> p c t", c=TILE)
                dve.memset(hist, 0.0).then_inc(cleared, 1)

                def x_copies(i):
                    done(dve, "y", i, 0)
                    for c in range(TILE):
                        done(dve, "xtp", i, c + 1)
                        S["xt"].inc(dve.tensor_copy(xtok[:, c, :], ps[:, 6 + c % 2, :]))

                def convolve(j, some):
                    for k, m in some:
                        if k == 0:
                            done(dve, "xpad", j, m + 1)
                            if m == 0:
                                done(dve, "xc", j, 0)
                                done(dve, "hist", j, 0)
                            ins = dve.tensor_scalar(acc[:, m, :], xpad[:, m, TAPS - 1:], conv_w[:, m, TAPS - 1:],
                                                    conv_b[:, m:m + 1], ALU.mult, ALU.add)
                        else:
                            done(dve, "conv", j, convolved(k - 1, m))
                            ins = dve.scalar_tensor_tensor(acc[:, m, :], xpad[:, m, k - 1:k - 1 + TW],
                                                           conv_w[:, m, k - 1:k], acc[:, m, :],
                                                           ALU.mult, ALU.add)
                        S["conv"].inc(ins)

                def history(j, half):
                    done(dve, "conv", j)
                    if half < HALVES - 1:
                        S["hist"].inc(dve.tensor_copy(hist, xpad[:, :, TW:]))
                    else:
                        S["hist"].inc(dve.memset(hist, 0.0))

                def running_delta(i):
                    done(dve, "soft", i)
                    done(dve, "run", i, 0)
                    done(dve, "bd", i, 0)
                    S["delta"].inc(dve.scalar_tensor_tensor(delta[:, :], ps[:, 3, :], 0.0, soft[:, :],
                                                            ALU.max, ALU.add))
                    done(dve, "delta", i)
                    done(dve, "wd", i, 0)
                    done(dve, "tokp", i, 0)
                    S["run"].inc(dve.tensor_tensor_scan(run[:, :], const("scan_keep"), delta[:, :], 0.0,
                                                        ALU.mult, ALU.add))
                    done(dve, "rep", i, 2)
                    S["bd"].inc(dve.tensor_tensor(bd[:, :], delta[:, :], ps[:, 4, :], ALU.mult))
                    done(dve, "run", i)
                    S["refs8"].inc(dve.tensor_tensor(
                        refs8[:, :, :], run[:, :].rearrange("p (c b q) -> p c b q", c=TILE, q=Q)[:, :, :, Q - 1],
                        const("ref_of").unsqueeze(1).to_broadcast([P, TILE, NB]), ALU.mult))
                    done(dve, "refs8", i)
                    S["ref"].inc(dve.tensor_reduce(ref[:, :], refs8[:, :, :], AX.X, ALU.add))
                    done(dve, "ref", i)
                    for c in range(TILE):
                        S["a2"].inc(dve.tensor_scalar(a2[:, c * P:(c + 1) * P], run[:, c * P:(c + 1) * P],
                                                      ref[:, c:c + 1], 0.0, ALU.subtract, ALU.min))
                    done(dve, "h", i, 0)
                    for c in range(TILE):
                        S["a1"].inc(dve.tensor_scalar(a1[:, c * P:(c + 1) * P], run[:, c * P:(c + 1) * P],
                                                      ref[:, c:c + 1], 0.0, ALU.subtract, ALU.max))

                def factors(i):
                    done(dve, "e2", i)
                    done(dve, "bd", i)
                    done(dve, "off", i, 0)
                    S["f2"].inc(dve.tensor_tensor(f2[:, :], a2[:, :], bd[:, :], ALU.mult))
                    done(dve, "e1", i)
                    done(dve, "rep", i, 3)
                    done(dve, "y", i, 0)
                    S["f1p"].inc(dve.tensor_tensor(f1p[:, :], a1[:, :], ps[:, 5, :], ALU.mult))
                    done(dve, "f1p", i)
                    S["f1"].inc(dve.tensor_tensor(chunks(f1), chunks(f1p),
                                                  const("block_of_state").unsqueeze(1).to_broadcast([P, TILE, P]), ALU.mult))
                    done(dve, "tok", i)
                    S["wd"].inc(dve.tensor_tensor(wd[:, :], chunks(run)[:, :, P - 1], tok_d[:, :, 0], ALU.subtract))
                    done(dve, "wd", i)
                    S["w2a"].inc(dve.tensor_tensor(
                        w2a[:, :, :], wd[:, :].unsqueeze(2).to_broadcast([P, TILE, NS]),
                        a_row[:, :].unsqueeze(1).to_broadcast([P, TILE, NS]), ALU.mult))

                def block_exponents(i):
                    done(dve, "crep", i)
                    for c in range(TILE):
                        S["a3"].inc(dve.tensor_scalar(a3[:, c, :], ps[:, 2, TOKC + c * Q:TOKC + (c + 1) * Q],
                                                      tok_d[:, c, 0:1], 0.0, ALU.subtract, ALU.max))
                    done(dve, "a3", i)
                    S["ah"].inc(dve.tensor_tensor(
                        big[:, :, :].rearrange("p c (t n) -> p (c t) n", n=NS),
                        a3[:, :, :].rearrange("p c t -> p (c t)").unsqueeze(2).to_broadcast([P, TILE * Q, NS]),
                        a_row[:, :].unsqueeze(1).to_broadcast([P, TILE * Q, NS]), ALU.mult))

                def matrix(i):
                    done(dve, "w2e", i)
                    done(dve, "hc", i, 0)
                    S["w2"].inc(dve.tensor_tensor(w2[:, :, :], w2a[:, :, :], tok_b[:, :, 0:NS], ALU.mult))
                    done(dve, "off", i)
                    done(dve, "y", i, 0)
                    S["mt0"].inc(dve.tensor_tensor(
                        mt[:, :, :], ps[:, 3, :].rearrange("p (c t) -> p c t", c=TILE),
                        const("earlier_block").unsqueeze(1).to_broadcast([P, TILE, P]), ALU.mult))
                    done(dve, "eh", i)
                    S["g1"].inc(dve.tensor_tensor(big[:, :, :], big[:, :, :],
                                                  ps[:, 6:8, :].rearrange("p u (v n) -> p (u v) n", v=2), ALU.mult))
                    done(dve, "g1", i)
                    wide = big[:, :, :].rearrange("p c (t n) -> p c t n", n=NS)
                    S["g2"].inc(dve.tensor_tensor(wide, wide, tok_b[:, :, 0:NS].unsqueeze(2).to_broadcast([P, TILE, Q, NS]),
                                                  ALU.mult))
                    done(dve, "g2", i)
                    S["md"].inc(dve.tensor_reduce(md[:, :, :], wide, AX.X, ALU.add))
                    done(dve, "md", i)
                    S["mdx"].inc(dve.tensor_tensor(
                        mdx[:, :, :].rearrange("p c (b t) -> p c b t", t=Q),
                        md[:, :, :].unsqueeze(2).to_broadcast([P, TILE, NB, Q]),
                        const("own_block_causal").rearrange("p (b t) -> p b t", t=Q).unsqueeze(1).to_broadcast([P, TILE, NB, Q]),
                        ALU.mult))
                    done(dve, "mt0", i)
                    done(dve, "mdx", i)
                    S["mt"].inc(dve.tensor_tensor(mt[:, :, :], mt[:, :, :], mdx[:, :, :], ALU.add))

                def states(i, half):
                    done(dve, "hc", i)
                    for c in range(TILE):
                        to = h[:, half, c + 1, :] if c + 1 < TILE else h[:, 1 - half, 0, :]
                        own = ps[32 * c:32 * c + NS, 3, :]
                        if c or half:
                            done(dve, "h", i, c)
                            S["h"].inc(dve.scalar_tensor_tensor(
                                to, h[:, half, c, :], a1[0:NS, (c + 1) * P - 1:(c + 1) * P], own, ALU.mult, ALU.add))
                        else:
                            S["h"].inc(dve.tensor_copy(to, own))

                def skip(i, half):
                    done(dve, "o", i, 0)
                    for c in range(TILE):
                        done(dve, "y", i, c + 1)
                        w = slice(c * P, (c + 1) * P)
                        for m in range(KI):
                            S["ys"].inc(dve.scalar_tensor_tensor(
                                y[:, m, w], xcT[:, half, m, w], d_skip[:, m:m + 1],
                                ps[:, 4 + c, m * P:(m + 1) * P], ALU.mult, ALU.add))

                def residual(i, js):
                    for j in js:
                        done(dve, "o", i, j + 1)
                        xs = X[:, ds(i * TILE + 2 * j, 2), :]
                        S["res"].inc(dve.tensor_tensor(xs, xs, ps[:, 2 + j, :].rearrange("p (c d) -> p c d", c=2), ALU.add))

                def first():
                    dve.wait_ge(x_first, 16)
                    nrm.vector_stats(dve, 0)
                    nrm.vector_apply(dve, 0)
                    dve.wait_ge(x_in, 16 * (TILES - 1))
                    dve.wait_ge(w_loaded, W_LOADS)
                    dve.wait_ge(cleared, 1)
                    nrm.vector_stats(dve, 1)
                    convolve(0, CONV[:8])
                    nrm.vector_apply(dve, 1)
                    dve.wait_ge(a_ready, 2)

                def end(i, half):
                    skip(i, half)
                    residual(i, range(2))

                def step(i, half, front, far, before):
                    if before:
                        skip(i - 1, 1 - half)
                    convolve(i, CONV[8:12])
                    if before:
                        residual(i - 1, (0,))
                    convolve(i, CONV[12:])
                    history(i, half)
                    if before:
                        residual(i - 1, (1,))
                    x_copies(i)
                    if front:
                        convolve(i + 1, CONV[:4])
                    running_delta(i)
                    factors(i)
                    if far:
                        nrm.vector_stats(dve, i + 2)
                    if front:
                        convolve(i + 1, CONV[4:8])
                    block_exponents(i)
                    if far:
                        nrm.vector_apply(dve, i + 2)
                    matrix(i)
                    states(i, half)

                steps(dve, first, step, end)
                done(dve, "res", TILES - 1)

            @block.tensor
            def _(pe):
                def project(j, slot, ms):
                    for m in ms:
                        if m == 0:
                            pe.wait_ge(nrm.xnT.sem, nrm.xnT.at(j, KD))
                            done(pe, "zc", j, 0)
                        if m >= 2:
                            done(pe, "xpad", j, min(m - 1, KI))
                            if m - 1 > KI:
                                done(pe, "zc", j, m - 1 - KI)
                        for k in range(KD):
                            t = pe.matmul(ps[:, m % 2, :], w_in[:, k, m * P:(m + 1) * P],
                                          xnT_of[slot][:, k, :], start=(k == 0), stop=(k == KD - 1))
                        S["xz"].inc(t)

                def first():
                    pe.wait_ge(const_loaded, 16)
                    nrm.tensor_turn(pe, 0, 0)
                    pe.wait_ge(w_in_loaded, 16 * KD)
                    project(0, 0, range(2 * KI))
                    nrm.tensor_turn(pe, 1, 4)
                    project(1, 1, (0, 1))
                    pe.wait_ge(w_loaded, W_LOADS)

                def end(i, half):
                    done(pe, "h", i)
                    for c in range(TILE):
                        done(pe, "yg", i, c + 1)
                        for m in range(KI):
                            t = pe.matmul(ps[:, 2 + c // 2, (c % 2) * D:(c % 2 + 1) * D], y[:, m, c * P:(c + 1) * P],
                                          w_out[:, m, :], start=(m == 0), stop=(m == KI - 1))
                        if c % 2:
                            S["o"].inc(t)

                def turn_x(i, half, c):
                    if c >= 2:
                        done(pe, "xt", i, c - 1)
                    for m in range(KI):
                        t = pe.transpose(ps[:, 6 + c % 2, m * P:(m + 1) * P], xcT[:, half, m, c * P:(c + 1) * P], const("ident"))
                    S["xtp"].inc(t)

                def step(i, half, front, far, before):
                    if before:
                        end(i - 1, 1 - half)
                    done(pe, "res", i - 1, 1)
                    for m in range(KI):
                        done(pe, "xc", i, m + 1)
                        t = pe.matmul(ps[0:XD, 2, :], w_x[:, m, :], xcT[:, half, m, :], start=(m == 0), stop=(m == KI - 1))
                    S["xdT"].inc(t)
                    done(pe, "ys", i, 0)
                    turn_x(i, half, 0)
                    turn_x(i, half, 1)
                    done(pe, "xd", i)
                    done(pe, "res", i, 0)
                    for j, name in enumerate(("sel_delta", "sel_b", "sel_c")):
                        S["rep"].inc(pe.matmul(ps[:, 3 + j, :], const(name, XD), xd[:, :], start=True, stop=True))
                    turn_x(i, half, 2)
                    turn_x(i, half, 3)
                    for c in range(TILE):
                        pe.transpose(ps[:, 2, c * XD:(c + 1) * XD], xd[:, c * P:(c + 1) * P], const("ident", XD)[:, 0:XD])
                    if front:
                        project(i + 1, 1 - half, (2, 3))
                    done(pe, "run", i)
                    done(pe, "bd", i)
                    for j, src in enumerate((run, bd)):
                        for c in range(TILE):
                            o = TILE * (XD + 32 * j) + 32 * c
                            t = pe.matmul(ps[:, 2, o:o + 32], src[:, c * P:(c + 1) * P], const("ident")[:, 0:32],
                                          start=True, stop=True)
                    S["tokp"].inc(t)
                    if front:
                        project(i + 1, 1 - half, (4,))
                    done(pe, "f1", i)
                    for c in range(TILE):
                        t = pe.matmul(ps[:, 3, c * P:(c + 1) * P], f2[:, c * P:(c + 1) * P],
                                      f1[:, c * P:(c + 1) * P], start=True, stop=True)
                    S["off"].inc(t)
                    if front:
                        project(i + 1, 1 - half, (5,))
                    done(pe, "cm", i)
                    done(pe, "xt", i)
                    for c in range(TILE):
                        pe.matmul(ps[:, 6 + c // 2, (c % 2) * Q * NS:(c % 2 + 1) * Q * NS], const("same_block"),
                                  cm[:, c, 0:Q * NS], start=True, stop=True)
                        t = pe.matmul(ps[:, 2, TOKC + c * Q:TOKC + (c + 1) * Q], const("same_block"),
                                      cm[:, c, Q * NS:], start=True, stop=True)
                    S["crep"].inc(t)
                    if front:
                        project(i + 1, 1 - half, (6, 7))
                    if far:
                        nrm.tensor_turn(pe, i + 2, 4)
                    done(pe, "xt", i)
                    done(pe, "w2", i)
                    done(pe, "mt0", i)
                    for c in range(TILE):
                        t = pe.matmul(ps[32 * c:32 * c + NS, 3, :], w2[:, c, :], xtok[:, c, :], start=True, stop=True)
                    S["hc"].inc(t)
                    if far:
                        project(i + 2, half, (0, 1))
                    done(pe, "mt", i)
                    for c in range(TILE):
                        has_state = c or half
                        if c:
                            done(pe, "h", i, c)
                        for m in range(KI):
                            t = pe.matmul(ps[:, 4 + c, m * P:(m + 1) * P], xtok[:, c, m * P:(m + 1) * P],
                                          mt[:, c, :], start=True, stop=not has_state)
                            if has_state:
                                t = pe.matmul(ps[:, 4 + c, m * P:(m + 1) * P], h[:, half, c, m * P:(m + 1) * P],
                                              f1p[0:NS, c * P:(c + 1) * P], start=False, stop=True)
                        S["y"].inc(t)
                steps(pe, first, step, end)

    nc.clear_and_free_semaphores(sems)
    nc.all_engine_barrier()


def sparse_ffn(nc, a, kept, const, scratch):
    X, ps = kept["X"], kept["ps"]
    with ExitStack() as ctx:
        def sb(name, shape, dt=F32):
            return ctx.enter_context(nc.sbuf_tensor(name, shape, dt))

        def sem(name):
            return ctx.enter_context(nc.semaphore(name))

        picks = sb("picks", [P, TOKENS], mybir.dt.bfloat16)
        with ExitStack() as sel_ctx:
            selT = sel_ctx.enter_context(nc.sbuf_tensor("selT", [P, KD, ES, GROUPS], F32))
            pick_tokens(nc, a, kept, const, picks, selT)
            apply_experts(nc, a, kept, const, selT, scratch)
        scatter_tokens(nc, a, kept, picks, scratch)


def signals(sem, prefix, **per):
    return {name: Signal(sem(f"{prefix}_{name}"), n) for name, n in per.items()}


def waiter(S):
    def done(eng, name, i, n=None):
        s = S[name]
        eng.wait_ge(s.sem, s.at(i, s.per if n is None else n))
    return done


def pick_tokens(nc, a, kept, const, picks, selT):
    X, ps = kept["X"], kept["ps"]
    with ExitStack() as ctx:
        def sb(name, shape, dt=F32):
            return ctx.enter_context(nc.sbuf_tensor(name, shape, dt))

        def sem(name):
            return ctx.enter_context(nc.semaphore(name))

        ctrl = sb("ctrl", [P, KD, 2 * ES])
        lg = sb("logits", [P, TW])
        gmax = sb("gmax", [P, TW // GRP])
        spread = sb("spread", [P, TILE, GC, ES], F32R)
        x_hi = sb("p_x_hi", [P, TILE, D], F32R)
        x_lo = sb("p_x_lo", [P, TILE, D], F32R)
        xn_of = [kept["xn"], sb("xn_odd", [P, TILE, D])]
        loaded = sem("p_loaded")
        nrm = Norm("p", sem, kept, const)
        S = signals(sem, "p", hi=TILE, lo=TILE, lgp=1, lg=1, gmax=1, one=1, picks=1, turned=1, spread=TILE, gath=KD * TILE, sel=KD * TILE)
        done = waiter(S)

        def steps(eng, front_first, step):
            front_first()
            with eng.Fori(0, TILES // 2 - 1) as k:
                step(2 * k, 0, True)
                step(2 * k + 1, 1, True)
            step(TILES - 2, 0, True)
            step(TILES - 1, 1, False)

        with nc.Block() as block:

            @block.sync
            def _(sp):
                sp.dma_start(ctrl[:, :, :], a["ctrl_twice"].rearrange("(k p) n -> p k n", p=P)).then_inc(loaded, 16)
                prime(sp, S, nrm)

            @block.gpsimd
            def _(pool):
                def low(j, slot):
                    for c in range(TILE):
                        done(pool, "hi", j, c + 1)
                        S["lo"].inc(pool.tensor_tensor(x_lo[:, c, :], xn_of[slot][:, c, :],
                                                       x_hi[:, c, :].bitcast(F32), ALU.subtract))

                def first():
                    nrm.gpsimd_rstd(pool, 0)
                    nrm.gpsimd_rstd(pool, 1)
                    low(0, 0)

                first()
                with pool.Fori(0, TILES // 2 - 1) as k:
                    for slot in range(2):
                        nrm.gpsimd_rstd(pool, 2 * k + slot + 2)
                        low(2 * k + slot + 1, 1 - slot)
                low(TILES - 1, 1)

            @block.scalar
            def _(act):
                def gathered(i, ns):
                    for n in ns:
                        c, k = n // KD, n % KD
                        done(act, "gath", i, n + 1)
                        S["sel"].inc(act.copy(
                            selT[:, k, :, ds((i * TILE + c) * GC, GC)].rearrange("p e g -> p g e"),
                            ps[:, 4 + n % 4, :].rearrange("p (g e) -> p g e", g=GC)))

                def high(j, slot, cs):
                    act.wait_ge(nrm.xn.sem, nrm.xn.at(j, TILE))
                    for c in cs:
                        done(act, "gath", j - 1, KD * (c + 1))
                        S["hi"].inc(act.copy(x_hi[:, c, :], xn_of[slot][:, c, :]))

                def first():
                    nrm.scalar_copy(act, 0, 0)
                    high(0, 0, range(TILE))

                def step(i, slot, front):
                    if front:
                        nrm.scalar_copy(act, i + 1, 0)
                    for c in range(TILE):
                        gathered(i, range(KD * c, KD * (c + 1)))
                        if front:
                            high(i + 1, 1 - slot, (c,))

                steps(act, first, step)

            @block.vector
            def _(dve):
                groups = lambda t: t.rearrange("p (g t) -> p g t", t=GRP)

                def norm(j, slot):
                    nrm.vector_stats(dve, j)
                    nrm.vector_apply(dve, j, xn_of[slot])

                def pick(j):
                    done(dve, "lgp", j)
                    done(dve, "turned", j, 0)
                    done(dve, "picks", j, 0)
                    S["lg"].inc(dve.tensor_tensor(groups(lg[:, :]), groups(ps[:, 2, :]),
                                                  const("tie").unsqueeze(1).to_broadcast([P, TW // GRP, GRP]), ALU.add))
                    done(dve, "lg", j)
                    S["gmax"].inc(dve.tensor_reduce(gmax[:, :], groups(lg[:, :]), AX.X, ALU.max))
                    done(dve, "gmax", j)
                    S["one"].inc(dve.tensor_tensor(groups(lg[:, :]), groups(lg[:, :]),
                                                   gmax[:, :].unsqueeze(2).to_broadcast([P, TW // GRP, GRP]), ALU.is_equal))

                def keep_picks(j):
                    done(dve, "one", j)
                    S["picks"].inc(dve.tensor_tensor(
                        picks[:, ds(j * TW, TW)].rearrange("p (c t) -> p c t", c=TILE),
                        lg[:, :].rearrange("p (c t) -> p c t", c=TILE),
                        const("parity").unsqueeze(1).to_broadcast([P, TILE, P]), ALU.mult))

                def spread_out(j, gathering):
                    done(dve, "turned", j)
                    for c in range(TILE):
                        if gathering:
                            done(dve, "gath", j - 1, KD * (c + 1))
                        S["spread"].inc(dve.tensor_tensor(
                            spread[:, c, :, :], ps[:, 3, c * P:c * P + ES].unsqueeze(1).to_broadcast([P, GC, ES]),
                            const("group_of").unsqueeze(2).to_broadcast([P, GC, ES]), ALU.mult))

                def first():
                    norm(0, 0)
                    pick(0)
                    norm(1, 1)
                    spread_out(0, False)
                    keep_picks(0)

                def step(i, slot, front):
                    if front:
                        nrm.vector_stats(dve, i + 2)
                        done(dve, "lo", i)
                        nrm.vector_apply(dve, i + 2, xn_of[slot])
                        pick(i + 1)
                        spread_out(i + 1, True)
                        keep_picks(i + 1)

                def last_step(i):
                    pick(i + 1)
                    spread_out(i + 1, True)
                    keep_picks(i + 1)

                first()
                with dve.Fori(0, TILES // 2 - 1) as k:
                    step(2 * k, 0, True)
                    step(2 * k + 1, 1, True)
                last_step(TILES - 2)

            @block.tensor
            def _(pe):
                def logits(j):
                    pe.wait_ge(nrm.xnT.sem, nrm.xnT.at(j, KD))
                    done(pe, "lg", j, 0)
                    for k in range(KD):
                        t = pe.matmul(ps[:, 2, :], ctrl[:, k, :], kept["xnT"][:, k, :], start=(k == 0), stop=(k == KD - 1))
                    S["lgp"].inc(t)

                def turn_picks(j):
                    done(pe, "one", j)
                    done(pe, "spread", j, 0)
                    for c in range(TILE):
                        t = pe.transpose(ps[:, 3, c * P:(c + 1) * P], lg[:, c * P:(c + 1) * P], const("ident"))
                    S["turned"].inc(t)

                def gather(i, slot, c):
                    done(pe, "spread", i, c + 1)
                    done(pe, "lo", i, c + 1)
                    for k in range(KD):
                        n = KD * c + k
                        done(pe, "sel", i, n - 3)
                        for n2, part in enumerate((x_hi, x_lo)):
                            t = pe.matmul(ps[:, 4 + n % 4, :], part[:, c, k * P:(k + 1) * P],
                                          spread[:, c, :, :].rearrange("p g e -> p (g e)"),
                                          start=n2 == 0, stop=n2 == 1)
                        S["gath"].inc(t)

                def first():
                    pe.wait_ge(loaded, 16)
                    nrm.tensor_turn(pe, 0, 0, xn_of[0])
                    logits(0)
                    turn_picks(0)

                def step(i, slot, front):
                    gather(i, slot, 0)
                    if front:
                        nrm.tensor_turn(pe, i + 1, 0, xn_of[1 - slot])
                    gather(i, slot, 1)
                    if front:
                        logits(i + 1)
                    gather(i, slot, 2)
                    gather(i, slot, 3)
                    if front:
                        turn_picks(i + 1)

                steps(pe, first, step)


def apply_experts(nc, a, kept, const, selT, scratch):
    ps, xn, xnT = kept["ps"], kept["xn"], kept["xnT"]
    SLOTS = 4
    with ExitStack() as ctx:
        def sb(name, shape, dt=F32):
            return ctx.enter_context(nc.sbuf_tensor(name, shape, dt))

        def sem(name):
            return ctx.enter_context(nc.semaphore(name))

        f1 = sb("f1w", [P, KD, SLOTS, 2 * FF])
        f2 = sb("f2w", [P, SLOTS, D])
        bias = sb("ffn_bias", [P, PAIRS])
        inter = sb("inter_sb", [P, 2, 2, 2, D])
        loaded = sem("e_loaded")
        f1_in = [sem(f"e_f1_in{u}") for u in range(SLOTS)]
        f2_in = [sem(f"e_f2_in{u}") for u in range(SLOTS)]
        stored = [sem(f"e_stored{u}") for u in range(2)]
        S = signals(sem, "e", innp=SLOTS, inner=2 * SLOTS, outp=SLOTS, low=SLOTS, high=SLOTS)
        done = waiter(S)
        f1_d = a["L0_ffn_f1"].rearrange("(k p) e s f -> p k (e s f)", p=P)
        f2_d = a["L0_ffn_f2"].rearrange("e s f d -> (e s f) d")
        out_d = scratch.rearrange("(h g) e d -> g h (e d)", g=P)

        def stored_before(eng, i, v):
            eng.wait_ge(stored[v % 2], PRIME + 16 * (2 * i + v // 2))

        with nc.Block() as block:

            @block.gpsimd
            def _(pool):
                with pool.Fori(0, PAIRS // SLOTS) as i:
                    for u in range(SLOTS):
                        pair = i * SLOTS + u
                        done(pool, "innp", i, u + 1 - SLOTS)
                        pool.dma_start(f1[:, :, u, :], f1_d[:, :, ds(pair * P, P)]).then_inc(f1_in[u], 16)
                        done(pool, "outp", i, u + 1 - SLOTS)
                        pool.dma_start(f2[:, u, :], f2_d[ds(pair * P, P), :]).then_inc(f2_in[u], 16)

            @block.tensor
            def _(pe):
                def second(i, u, n):
                    done(pe, "inner", i, 2 * n + 2)
                    done(pe, "low", i, n - 1)
                    done(pe, "high", i, n - 1)
                    pe.wait_ge(f2_in[u], 16 * (i + 1) if n >= 0 else 16 * i)
                    for g in range(2):
                        for e in range(2):
                            t = pe.matmul(ps[:, 2 + 2 * (u % 2) + e, g * D:(g + 1) * D],
                                          xn[e * FF:(e + 1) * FF, u, g * P:(g + 1) * P],
                                          f2[e * FF:(e + 1) * FF, u, :], start=True, stop=True)
                    S["outp"].inc(t)

                with pe.Fori(0, PAIRS // SLOTS) as i:
                    for u in range(SLOTS):
                        pe.wait_ge(f1_in[u], 16 * (i + 1))
                        done(pe, "inner", i, 2 * (u - 1))
                        for e in range(2):
                            for k in range(KD):
                                t = pe.matmul(ps[:, u % 2, e * GROUPS:(e + 1) * GROUPS], f1[:, k, u, :],
                                              selT[:, k, ds((i * SLOTS + u) * 2 + e, 1), :].rearrange("p o g -> p (o g)"),
                                              start=(k == 0), stop=(k == KD - 1))
                        S["innp"].inc(t)
                        if u:
                            second(i, u - 1, u - 1)
                    second(i, SLOTS - 1, SLOTS - 1)

            @block.scalar
            def _(act):
                act.wait_ge(loaded, 16)
                with act.Fori(0, PAIRS // SLOTS) as i:
                    for u in range(SLOTS + 1):
                        if u < SLOTS:
                            done(act, "innp", i, u + 1)
                            done(act, "outp", i, u + 1 - SLOTS)
                            for e in range(2):
                                r = slice(e * FF, (e + 1) * FF)
                                S["inner"].inc(act.activation(xn[r, u, :], ps[r, u % 2, e * GROUPS:(e + 1) * GROUPS],
                                                              ACT.Relu, bias=bias[r, ds(i * SLOTS + u, 1)]))
                        if u:
                            v = u - 1
                            done(act, "outp", i, v + 1)
                            stored_before(act, i, v)
                            S["high"].inc(act.copy(inter[:, v % 2, :, 1, :],
                                                   ps[:, 3 + 2 * (v % 2), :].rearrange("p (g d) -> p g d", g=2)))

            @block.vector
            def _(dve):
                with dve.Fori(0, PAIRS // SLOTS) as i:
                    for v in range(SLOTS):
                        done(dve, "outp", i, v + 1)
                        stored_before(dve, i, v)
                        S["low"].inc(dve.tensor_copy(inter[:, v % 2, :, 0, :],
                                                     ps[:, 2 + 2 * (v % 2), :].rearrange("p (g d) -> p g d", g=2)))

            @block.sync
            def _(sp):
                sp.dma_start(bias[:, :], a["ffn_bias_cols"]).then_inc(loaded, 16)
                prime(sp, S)
                for s in stored:
                    sp.sem_inc(s, PRIME)
                with sp.Fori(0, PAIRS // SLOTS) as i:
                    for v in range(SLOTS):
                        done(sp, "low", i, v + 1)
                        done(sp, "high", i, v + 1)
                        sp.dma_start(out_d[:, :, ds((i * SLOTS + v) * 2 * D, 2 * D)],
                                     inter[:, v % 2, :, :, :].rearrange("p g e d -> p g (e d)")).then_inc(stored[v % 2], 16)
                for s in stored:
                    sp.wait_ge(s, PRIME + 16 * PAIRS // 2)


def scatter_tokens(nc, a, kept, picks, scratch):
    X, ps = kept["X"], kept["ps"]
    GP = GC // 2
    with ExitStack() as ctx:
        def sb(name, shape, dt=F32):
            return ctx.enter_context(nc.sbuf_tensor(name, shape, dt))

        def sem(name):
            return ctx.enter_context(nc.semaphore(name))

        inter = sb("inter_in", [P, 2, TILE, GP, D])
        hot = sb("hot", [P, 2, TW])
        read = [sem(f"s_read{u}") for u in range(2 * TILE)]
        S = signals(sem, "s", hot=2, added=2 * TILE, res=2 * TILE)
        done = waiter(S)
        src = scratch.rearrange("(c q r) e d -> c (r e) q d", q=GP, r=2)
        with nc.Block() as block:

            @block.sync
            def _(sp):
                prime(sp, S)
                with sp.Fori(0, TILES // 2) as i:
                    for u in range(2 * TILE):
                        done(sp, "added", i, u + 1 - 2 * TILE)
                        sp.dma_start(inter[:, u // TILE, u % TILE, :, :],
                                     src[ds(i * 2 * TILE + u, 1)].rearrange("o p q d -> p (o q) d")).then_inc(read[u], 16)

            @block.scalar
            def _(act):
                with act.Fori(0, TILES // 2) as i:
                    for t in range(2):
                        done(act, "added", i, TILE * (t - 1))
                        S["hot"].inc(act.copy(hot[:, t, :], picks[:, ds((2 * i + t) * TW, TW)]))

            @block.tensor
            def _(pe):
                with pe.Fori(0, TILES // 2) as i:
                    for u in range(2 * TILE):
                        t, c = u // TILE, u % TILE
                        done(pe, "hot", i, t + 1)
                        done(pe, "res", i, u - 7)
                        pe.wait_ge(read[u], 16 * (i + 1))
                        for q in range(GP):
                            m = pe.matmul(ps[32 * q:32 * (q + 1), u, 0:D], hot[:, t, c * P + 32 * q:c * P + 32 * (q + 1)],
                                          inter[:, t, c, q, :], start=True, stop=True)
                        S["added"].inc(m)

            @block.vector
            def _(dve):
                with dve.Fori(0, TILES // 2) as i:
                    for u in range(2 * TILE):
                        done(dve, "added", i, u + 1)
                        xs = X[:, ds(i * 2 * TILE + u, 1), :]
                        S["res"].inc(dve.tensor_tensor(xs, xs, ps[:, u, 0:D].unsqueeze(1), ALU.add))
                    done(dve, "res", i)

def attention(nc, a, kept, const, nxt):
    X, ps = kept["X"], kept["ps"]
    NJ = len(HEADS_OF)
    rows = [NORM_ROW[j] + len(HEADS_OF[j]) for j in range(NJ)]
    with ExitStack() as ctx:
        def sb(name, shape, dt=F32):
            return ctx.enter_context(nc.sbuf_tensor(name, shape, dt))

        def sem(name):
            return ctx.enter_context(nc.semaphore(name))

        wqkv_hi = sb("wqkv_hi", [P, KD, 3 * D], F32R)
        wqkv_lo = sb("wqkv_lo", [P, KD, 3 * D], F32R)
        wo = sb("wo", [P, KD, D])
        x_hi = sb("a_x_hi", [P, KD, TW], F32R)
        x_lo = sb("a_x_lo", [P, KD, TW], F32R)
        rfb = sb("rfb", [P, NJ * 6 * NF])
        b_out = sb("b_out", [P, D])
        kT = sb("kT", [P, NJ, TW])
        qT = sb("qT", [P, NJ, HALVES, TW])
        sq = sb("sq", [P, 2 * NJ, TW])
        v = sb("v", [P, TILE, D])
        ones = sb("ones", [P, 2 * HD])
        kp = sb("kp", [P, TILE, HEADS * NF])
        kvT = sb("kvT", [P, 2 * D])
        kv = sb("kv", [P, 2, HP, 2 * HD])
        qp = sb("qp", [P, HP, TW])
        den = sb("den", [P, TW])
        rec = sb("rec", [P, TW])
        oT = sb("oT", [P, KD, TW])
        wqkv = kp[:, :, :].rearrange("p c n -> p (c n)")[:, 0:KD * 3 * D].rearrange("p (k n) -> p k n", k=KD)
        ew = sb("ew", [P, KD, 2, D])
        loaded, cleared = sem("a_loaded"), sem("a_cleared")
        w_high, w_split = sem("a_w_high"), sem("a_w_split")
        ew_read, next_loaded = sem("a_ew_read"), sem("a_next_loaded")
        nrm = Norm("a", sem, kept, const)
        S = signals(sem, "a", qk=2 * NJ, sq=2 * NJ, copy=2 * NJ, nsq=2 * NJ, norm=2 * NJ,
                    vp=2, v=2, kpp=TILE, kp=TILE, kvp=TILE,
                    qpp=HP, qp=HP, nd=KD, den=KD, rec=KD, oT=KD, xlo=KD, yp=2, res=2, bias=1)
        S2 = signals(sem, "a", kvT=1, kvp2=1, kv=2, ew_hi=1, ew_lo=1)
        done = waiter({**S, **S2})

        proj_bank = lambda n: (2, 3, 4, 5, 1, 6)[n]
        output_banks = lambda half, r: (0, 1) if half == 0 and r else (5, 6)
        feature_bank = lambda half, p: 2 + (half * HP + p) % 3

        def rows_of(eng, first, batch):
            first()
            with eng.Fori(0, B - 1) as b:
                batch(b, True)
            batch(B - 1, False)

        with nc.Block() as block:

            @block.sync
            def _(sp):
                for dst, src in ((wqkv, a["w_qkv_T"].rearrange("(k p) n -> p k n", p=P)),
                                 (rfb[:, :], a["rf_blocks"]),
                                 (wo[:, :, :], a["w_out_T"].rearrange("(k p) n -> p k n", p=P)),
                                 (b_out[:, :], a["L1_attn_b_out"].rearrange("(o n) -> o n", o=1).to_broadcast([P, D]))):
                    sp.dma_start(dst, src).then_inc(loaded, 16)
                prime(sp, {**S, **S2}, nrm)
                for dst, src in ((nxt["rw"][:, :, :], a["L1_ffn_router_w"].rearrange("(k p) e -> p k e", p=P)),
                                 (nxt["rb"][:, :], a["L1_ffn_router_b"].rearrange("(o n) -> o n", o=1).to_broadcast([P, NE])),
                                 (nxt["eb"][:, :], a["L1_ffn_expert_b"])):
                    sp.dma_start(dst, src).then_inc(next_loaded, 16)
                e_w = a["L1_ffn_expert_w"].rearrange("e (k p) d -> p k e d", p=P)
                with sp.Fori(0, B) as b:
                    done(sp, "ew_lo", b, 0)
                    for k in range(KD):
                        sp.dma_start(ew[:, k, :, :], e_w[:, k, ds(2 * b, 2), :]).then_inc(ew_read, 16)
                sp.wait_ge(next_loaded, 48)

            @block.gpsimd
            def _(pool):
                pool.memset(kv[:, :, :, :], 0.0).then_inc(cleared, 1)
                pool.memset(ones[:, :], 1.0).then_inc(cleared, 1)

                def batch(b, more):
                    nrm.gpsimd_rstd(pool, b * HALVES + 1)
                    if more:
                        nrm.gpsimd_rstd(pool, b * HALVES + HALVES)
                    hi, lo = (nxt[n][:, :, ds(2 * b, 2), :] for n in ("w_hi", "w_lo"))
                    pool.wait_ge(ew_read, 16 * KD * (b + 1))
                    S2["ew_hi"].inc(pool.tensor_copy(hi, ew[:, :, :, :]))
                    done(pool, "ew_hi", b)
                    S2["ew_lo"].inc(pool.tensor_tensor(lo, ew[:, :, :, :], hi.bitcast(F32), ALU.subtract))
                    for half in range(HALVES):
                        i = b * HALVES + half
                        done(pool, "res", i)
                        xs = X[:, ds(i * TILE, TILE), :]
                        S["bias"].inc(pool.tensor_tensor(xs, xs, b_out[:, :].unsqueeze(1).to_broadcast([P, TILE, D]), ALU.add))

                nrm.gpsimd_rstd(pool, 0)
                pool.wait_ge(loaded, 64)
                rows_of(pool, lambda: None, batch)

            @block.scalar
            def _(act):
                def squares(i, some):
                    for n in some:
                        j = n % NJ
                        done(act, "qk", i, n + 1)
                        if n == 0:
                            done(act, "nsq", i, 0)
                        S["sq"].inc(act.activation(sq[0:NORM_ROW[j], n, :], ps[0:NORM_ROW[j], proj_bank(n), :], ACT.Square))

                def roots(i, half):
                    for n in range(2 * NJ):
                        j = n % NJ
                        r = slice(NORM_ROW[j], rows[j])
                        done(act, "nsq", i, n + 1)
                        if n == 0:
                            done(act, "kpp", i, 0)
                        if n == NJ and half == 0:
                            done(act, "qpp", i, 0)
                        dst = kT[r, j, :] if n < NJ else qT[r, j, half, :]
                        S["norm"].inc(act.activation(dst, ps[r, proj_bank(n), :], ACT.Sqrt))

                def front(j):
                    done(act, "vp", j, 0)
                    nrm.scalar_copy(act, j, 0, x_hi)
                    squares(j, range(NJ))

                def batch(b, more):
                    for half in range(HALVES):
                        i = b * HALVES + half
                        squares(i, range(NJ, 2 * NJ))
                        roots(i, half)
                        for c in range(TILE):
                            if c == 0:
                                act.wait_ge(w_split, 1)
                            done(act, "kpp", i, c + 1)
                            done(act, "kvp", i, c + 1 - TILE)
                            S["kp"].inc(act.activation(kp[:, c, :].rearrange("p (u n) -> p u n", u=2),
                                                       ps[:, 2 + 2 * (c % 2):4 + 2 * (c % 2), :], ACT.Exp, scale=NF ** -0.5))
                        if half == 0:
                            front(i + 1)
                    for half in range(HALVES):
                        i = b * HALVES + half
                        for p in range(HP):
                            done(act, "qpp", i, p + 1)
                            done(act, "nd", i, p // 4 - 1)
                            S["qp"].inc(act.activation(qp[:, p, :], ps[:, feature_bank(half, p), :], ACT.Exp, scale=NF ** -0.5))
                    if more:
                        front(b * HALVES + HALVES)

                def first():
                    act.wait_ge(loaded, 64)
                    act.copy(wqkv_hi[:, :, :], wqkv).then_inc(w_high, 1)
                    front(0)

                rows_of(act, first, batch)

            @block.vector
            def _(dve):
                def split_x(j):
                    done(dve, "vp", j, 0)
                    for d in range(KD):
                        dve.wait_ge(nrm.xnT.sem, nrm.xnT.at(j, d + 1))
                        S["xlo"].inc(dve.tensor_tensor(x_lo[:, d, :], ps[:, d, :], x_hi[:, d, :].bitcast(F32), ALU.subtract))

                def copies(i, half, some):
                    for n in some:
                        j = n % NJ
                        done(dve, "sq", i, n + 1)
                        if n == 0:
                            done(dve, "kpp", i, 0)
                        if n == NJ and half == 0:
                            done(dve, "qpp", i, 0)
                        dst = kT[0:NORM_ROW[j], j, :] if n < NJ else qT[0:NORM_ROW[j], j, half, :]
                        S["copy"].inc(dve.tensor_copy(dst, ps[0:NORM_ROW[j], proj_bank(n), :]))

                def values(i, u):
                    done(dve, "vp", i, u + 1)
                    if u == 0:
                        done(dve, "kvp", i, 0)
                    S["v"].inc(dve.tensor_copy(v[:, 2 * u:2 * u + 2, :], ps[:, 0, :].rearrange("p (c d) -> p c d", c=2)))

                def norm(j):
                    nrm.vector_stats(dve, j)
                    nrm.vector_apply(dve, j)

                def quotients(i, half, k):
                    done(dve, "nd", i, k + 1)
                    num_bank, den_bank = output_banks(half, k)
                    done(dve, "oT", i, k)
                    S["den"].inc(dve.tensor_scalar(den[:, :], ps[:, den_bank, :], 1e-6, None, ALU.add))
                    done(dve, "den", i, k + 1)
                    S["rec"].inc(dve.reciprocal(rec[:, :], den[:, :]))
                    done(dve, "rec", i, k + 1)
                    done(dve, "yp", i, 0)
                    S["oT"].inc(dve.tensor_tensor(oT[:, k, :], ps[:, num_bank, :], rec[:, :], ALU.mult))

                def residual(i):
                    for u in range(2):
                        done(dve, "yp", i, u + 1)
                        xs = X[:, ds(i * TILE + 2 * u, 2), :]
                        S["res"].inc(dve.tensor_tensor(xs, xs, ps[:, 7 - u, :].rearrange("p (c d) -> p c d", c=2), ALU.add))

                def batch(b, more):
                    for half in range(HALVES):
                        i = b * HALVES + half
                        copies(i, half, range(NJ, 2 * NJ))
                        values(i, 0)
                        values(i, 1)
                        if half == 0 or more:
                            norm(i + 1)
                        if half == 0:
                            split_x(i + 1)
                            copies(i + 1, 1, range(NJ))
                    done(dve, "kvp", b * HALVES + 1)
                    S2["kvT"].inc(dve.tensor_copy(kvT[:, :], ps[:, 7, :]))
                    done(dve, "kvp2", b)
                    done(dve, "nd", b * HALVES, 0)
                    for e in range(2):
                        r, w = slice(e * NF, (e + 1) * NF), slice(e * HD, (e + 1) * HD)
                        S2["kv"].inc(dve.tensor_copy(kv[r, :, :, w].rearrange("p a b w -> p (a b) w"),
                                                     ps[r, 0, :].rearrange("p (a w) -> p a w", w=2 * HD)[:, :, w]))
                    i = b * HALVES
                    quotients(i, 0, 0)
                    quotients(i, 0, 1)
                    residual(i)
                    quotients(i + 1, 1, 0)
                    if more:
                        split_x(i + 2)
                    quotients(i + 1, 1, 1)
                    if more:
                        copies(i + 2, 0, range(NJ))
                    residual(i + 1)

                def first():
                    dve.wait_ge(cleared, 2)
                    norm(0)
                    dve.wait_ge(w_high, 1)
                    dve.tensor_tensor(wqkv_lo[:, :, :], wqkv, wqkv_hi[:, :, :].bitcast(F32), ALU.subtract).then_inc(w_split, 1)
                    split_x(0)
                    copies(0, 0, range(NJ))

                rows_of(dve, first, batch)

            @block.tensor
            def _(pe):
                def project(i, i_half, some):
                    for n in some:
                        j = n % NJ
                        w = (D if n < NJ else 0) + HEADS_OF[j][0] * HD
                        if n == 2 * NJ - 1:
                            done(pe, "res", i - i_half, 0)
                        for s, (wt, x) in enumerate(((wqkv_hi, x_hi), (wqkv_lo, x_hi), (wqkv_hi, x_lo))):
                            for k in range(KD):
                                t = pe.matmul(ps[0:NORM_ROW[j], proj_bank(n), :], wt[:, k, w:w + NORM_ROW[j]],
                                              x[:, k, :], start=(s == 0 and k == 0), stop=(s == 2 and k == KD - 1))
                        S["qk"].inc(t)

                def turn(j):
                    done(pe, "v", j, 0)
                    done(pe, "norm", j, 0)
                    nrm.tensor_turn(pe, j, 0)

                def keys(j, half):
                    done(pe, "xlo", j)
                    done(pe, "kp", j, 0)
                    done(pe, "qp", j - half, 0)
                    project(j, half, range(NJ))

                def values(i, u):
                    done(pe, "v", i, u)
                    for c in range(2):
                        for s, (x, wt) in enumerate(((x_hi, wqkv_hi), (x_hi, wqkv_lo), (x_lo, wqkv_hi))):
                            for k in range(KD):
                                t = pe.matmul(ps[:, 0, c * D:(c + 1) * D], x[:, k, (2 * u + c) * P:(2 * u + c + 1) * P],
                                              wt[:, k, 2 * D:3 * D], start=(s == 0 and k == 0), stop=(s == 2 and k == KD - 1))
                    S["vp"].inc(t)

                def square_sums(i, some):
                    for n in some:
                        j = n % NJ
                        if j == 0:
                            done(pe, "sq", i, n + NJ)
                        S["nsq"].inc(pe.matmul(ps[NORM_ROW[j]:rows[j], proj_bank(n), :],
                                               const("head_of")[0:NORM_ROW[j], 0:len(HEADS_OF[j])],
                                               sq[0:NORM_ROW[j], n, :], start=True, stop=True))

                def key_features(i, c):
                    for name in ("norm", "copy"):
                        done(pe, name, i, 3 if c == 0 else 4)
                    if c >= 2:
                        done(pe, "kp", i, c - 1)
                    at = 0
                    for j in range(NJ):
                        left, src = len(HEADS_OF[j]) * NF, j * 6 * NF
                        while left:
                            n = min(left, 512 - at % 512)
                            t = pe.matmul(ps[:, 2 + 2 * (c % 2) + at // 512, at % 512:at % 512 + n],
                                          kT[0:rows[j], j, c * P:(c + 1) * P], rfb[0:rows[j], src:src + n],
                                          start=True, stop=True)
                            at, src, left = at + n, src + n, left - n
                    S["kpp"].inc(t)

                def keys_by_values(i, half, c):
                    done(pe, "kp", i, c + 1)
                    if c == 0:
                        done(pe, "v", i)
                        done(pe, "res", i - half, 0)
                    for kind in range(2):
                        for r in range(2):
                            for q in range(4):
                                p, col = 4 * r + q, (2 * kind + r) * P
                                t = pe.matmul(ps[32 * q:32 * (q + 1), 7, col:col + P],
                                              v[:, c, p * 32:(p + 1) * 32] if kind == 0 else ones[:, :],
                                              kp[:, c, p * P:(p + 1) * P],
                                              start=half == 0 and c == 0 and kind == 0 and r == 0,
                                              stop=half == HALVES - 1 and c == TILE - 1,
                                              skip_group_check=True)
                    S["kvp"].inc(t)

                def query_features(i, half, some):
                    for p in some:
                        if p == 0:
                            done(pe, "copy", i)
                            done(pe, "norm", i)
                            if half == 0:
                                done(pe, "kp", i + 1)
                        done(pe, "qp", i, p - 2)
                        j, src = p // 3, (p // 3) * 6 * NF + (p % 3) * P
                        S["qpp"].inc(pe.matmul(ps[:, feature_bank(half, p), :], rfb[0:rows[j], src:src + P],
                                               qT[0:rows[j], j, half, :], start=True, stop=True))

                def turn_kv(b):
                    done(pe, "kvT", b)
                    done(pe, "v", b * HALVES + 1)
                    for r in range(4):
                        t = pe.transpose(ps[:, 0, r * P:(r + 1) * P], kvT[:, r * P:(r + 1) * P], const("ident"))
                    S2["kvp2"].inc(t)

                def outputs(i, half, r):
                    done(pe, "qp", i, 4 * r + 4)
                    done(pe, "oT", i, half * r)
                    done(pe, "res", i, 0)
                    banks = output_banks(half, r)
                    for kind in range(2):
                        for q in range(4):
                            t = pe.matmul(ps[32 * q:32 * (q + 1), banks[kind], :], kv[:, kind, 4 * r + q, :],
                                          qp[:, 4 * r + q, :], start=True, stop=True)
                    S["nd"].inc(t)

                def project_out(i):
                    done(pe, "oT", i)
                    done(pe, "res", i, 0)
                    for u in range(2):
                        for c in range(2):
                            for k in range(KD):
                                t = pe.matmul(ps[:, 7 - u, c * D:(c + 1) * D], oT[:, k, (2 * u + c) * P:(2 * u + c + 1) * P],
                                              wo[:, k, :], start=(k == 0), stop=(k == KD - 1))
                        S["yp"].inc(t)

                def batch(b, more):
                    i = b * HALVES
                    for half in range(HALVES):
                        t = i + half
                        project(t, half, range(NJ, 2 * NJ))
                        values(t, 0)
                        square_sums(t, range(NJ))
                        square_sums(t, range(NJ, 2 * NJ))
                        values(t, 1)
                        key_features(t, 0)
                        key_features(t, 1)
                        keys_by_values(t, half, 0)
                        key_features(t, 2)
                        keys_by_values(t, half, 1)
                        key_features(t, 3)
                        keys_by_values(t, half, 2)
                        if half == 0:
                            turn(t + 1)
                            keys_by_values(t, half, 3)
                            keys(t + 1, 1)
                    query_features(i, 0, (0,))
                    keys_by_values(i + 1, 1, 3)
                    query_features(i, 0, (1, 2, 3))
                    turn_kv(b)
                    query_features(i, 0, (4,))
                    done(pe, "kv", b)
                    outputs(i, 0, 0)
                    query_features(i, 0, (5, 6, 7))
                    query_features(i + 1, 1, (0,))
                    outputs(i, 0, 1)
                    query_features(i + 1, 1, (1, 2, 3, 4))
                    project_out(i)
                    outputs(i + 1, 1, 0)
                    query_features(i + 1, 1, (5, 6, 7))
                    done(pe, "oT", i + 1, 0)
                    if more:
                        turn(i + 2)
                    outputs(i + 1, 1, 1)
                    if more:
                        keys(i + 2, 0)
                    project_out(i + 1)

                def first():
                    turn(0)
                    pe.wait_ge(w_split, 1)
                    keys(0, 0)

                rows_of(pe, first, batch)


def experts(nc, a, kept, const, nxt, out):
    X, ps, xnT = kept["X"], kept["ps"], kept["xnT"]
    w_hi, w_lo, rw, rb, eb = (nxt[n] for n in ("w_hi", "w_lo", "rw", "rb", "eb"))
    with ExitStack() as ctx:
        def sb(name, shape, dt=F32):
            return ctx.enter_context(nc.sbuf_tensor(name, shape, dt))

        def sem(name):
            return ctx.enter_context(nc.semaphore(name))

        x_hi = sb("x_hi", [P, 2, KD, TW], F32R)
        x_lo = sb("x_lo", [P, 2, KD, TW], F32R)
        lg = sb("router_logits", [P, TILE, NE])
        z = sb("z", [P, TILE, NE])
        top = sb("top", [P, TILE])
        total = sb("total", [P, TILE])
        gate = sb("gate", [P, TILE])
        one = sb("one", [P, TILE, NE])
        best = sb("best", [P, TILE])
        g = sb("g", [P, 2, TILE, NE])
        gT = sb("gT", [NE, 2, TW])
        stored = sem("stored")
        nrm = Norm("x", sem, kept, const)
        S = signals(sem, "x", hi=KD, lo=KD, lgp=1, lg=1, top=1, z=1, ez=1, total=1, gate=1, one=1, ranked=1,
                    best=1, first=1, g=1, gTp=1, gT=1, biasp=TILE, bias=TILE, yp=TILE * NE // 2, acc=TILE * NE)
        done = waiter(S)

        def steps(eng, front_first, step):
            front_first()
            with eng.Fori(0, TILES // 2 - 1) as k:
                step(2 * k, 0, True)
                step(2 * k + 1, 1, True)
            step(TILES - 2, 0, True)
            step(TILES - 1, 1, False)

        with nc.Block() as block:

            @block.sync
            def _(sp):
                prime(sp, S, nrm)
                o = out.rearrange("b (c p) d -> p (b c) d", p=P)
                with sp.Fori(0, TILES) as i:
                    done(sp, "bias", i)
                    sp.dma_start(o[:, ds(i * TILE, TILE)], X[:, ds(i * TILE, TILE)]).then_inc(stored, 16)
                sp.wait_ge(stored, 16 * TILES)

            @block.gpsimd
            def _(pool):
                def step(i, slot, front):
                    if front:
                        nrm.gpsimd_rstd(pool, i + 1)

                steps(pool, lambda: nrm.gpsimd_rstd(pool, 0), step)

            @block.scalar
            def _(act):
                def front(j, slot, after=True):
                    if after:
                        done(act, "lo", j, 0)
                        done(act, "lgp", j, 0)
                    nrm.scalar_copy(act, j, 0)
                    for d in range(KD):
                        act.wait_ge(nrm.xnT.sem, nrm.xnT.at(j, d + 1))
                        S["hi"].inc(act.copy(x_hi[:, slot, d, :], xnT[:, d, :]))
                    done(act, "z", j)
                    S["ez"].inc(act.activation(z[:, :, :], z[:, :, :], ACT.Exp))
                    done(act, "gTp", j)
                    if after:
                        done(act, "biasp", j - 1, 0)
                    S["gT"].inc(act.copy(gT[:, slot, :], ps[0:NE, 1, :]))

                def step(i, slot, with_front):
                    if with_front:
                        front(i + 1, 1 - slot)

                steps(act, lambda: front(0, 0, False), step)

            @block.vector
            def _(dve):
                wide = lambda t: t[:, :].unsqueeze(2).to_broadcast([P, TILE, NE])

                def split(j, slot):
                    for d in range(KD):
                        done(dve, "hi", j, d + 1)
                        S["lo"].inc(dve.tensor_tensor(x_lo[:, slot, d, :], xnT[:, d, :],
                                                      x_hi[:, slot, d, :].bitcast(F32), ALU.subtract))

                def route(j, slot):
                    done(dve, "lgp", j)
                    S["lg"].inc(dve.tensor_tensor(lg[:, :, :], ps[:, 0, 0:TILE * NE].rearrange("p (c e) -> p c e", e=NE),
                                                  rb[:, :].unsqueeze(1).to_broadcast([P, TILE, NE]), ALU.add))
                    done(dve, "lg", j)
                    S["top"].inc(dve.tensor_reduce(top[:, :], lg[:, :, :], AX.X, ALU.max))
                    done(dve, "top", j)
                    S["z"].inc(dve.tensor_tensor(z[:, :, :], lg[:, :, :], wide(top), ALU.subtract))
                    S["one"].inc(dve.tensor_tensor(one[:, :, :], lg[:, :, :], wide(top), ALU.is_equal))
                    done(dve, "one", j)
                    S["ranked"].inc(dve.tensor_tensor(one[:, :, :], one[:, :, :],
                                                      const("rank").unsqueeze(1).to_broadcast([P, TILE, NE]), ALU.mult))
                    done(dve, "ranked", j)
                    S["best"].inc(dve.tensor_reduce(best[:, :], one[:, :, :], AX.X, ALU.max))
                    done(dve, "best", j)
                    S["first"].inc(dve.tensor_tensor(one[:, :, :], one[:, :, :], wide(best), ALU.is_equal))
                    done(dve, "ez", j)
                    S["total"].inc(dve.tensor_reduce(total[:, :], z[:, :, :], AX.X, ALU.add))
                    done(dve, "total", j)
                    S["gate"].inc(dve.reciprocal(gate[:, :], total[:, :]))
                    done(dve, "gate", j)
                    done(dve, "first", j)
                    S["g"].inc(dve.tensor_tensor(g[:, slot, :, :], one[:, :, :], wide(gate), ALU.mult))

                def add(i, slot, c):
                    xs = X[:, ds(i * TILE + c, 1), :]
                    done(dve, "g", i)
                    for e in range(NE):
                        if e % 2 == 0:
                            done(dve, "yp", i, (c * NE + e) // 2 + 1)
                        if e:
                            done(dve, "acc", i, c * NE + e)
                        S["acc"].inc(dve.scalar_tensor_tensor(
                            xs, ps[:, 4 + e // 2, (e % 2) * D:(e % 2 + 1) * D].unsqueeze(1), g[:, slot, c, e:e + 1], xs,
                            ALU.mult, ALU.add))
                    done(dve, "biasp", i, c + 1)
                    done(dve, "acc", i, (c + 1) * NE)
                    S["bias"].inc(dve.tensor_tensor(xs, xs, ps[:, 2 + c % 2, 0:D].unsqueeze(1), ALU.add))

                def first():
                    nrm.vector_stats(dve, 0)
                    nrm.vector_apply(dve, 0)
                    split(0, 0)
                    route(0, 0)

                def step(i, slot, front):
                    if front:
                        nrm.vector_stats(dve, i + 1)
                    add(i, slot, 0)
                    if front:
                        nrm.vector_apply(dve, i + 1)
                    add(i, slot, 1)
                    if front:
                        split(i + 1, 1 - slot)
                    add(i, slot, 2)
                    if front:
                        route(i + 1, 1 - slot)
                    add(i, slot, 3)

                steps(dve, first, step)

            @block.tensor
            def _(pe):
                def turn(j):
                    done(pe, "lg", j, 0)
                    done(pe, "gT", j, 0)
                    nrm.tensor_turn(pe, j, 0)

                def router(j):
                    for d in range(KD):
                        pe.wait_ge(nrm.xnT.sem, nrm.xnT.at(j, d + 1))
                    for c in range(TILE):
                        for k in range(KD):
                            t = pe.matmul(ps[:, 0, c * NE:(c + 1) * NE], xnT[:, k, c * P:(c + 1) * P], rw[:, k, :],
                                          start=(k == 0), stop=(k == KD - 1))
                    S["lgp"].inc(t)

                def turn_gates(j, slot):
                    done(pe, "g", j)
                    for c in range(TILE):
                        t = pe.transpose(ps[0:NE, 1, c * P:(c + 1) * P], g[:, slot, c, :], const("ident"))
                    S["gTp"].inc(t)

                def products(i, slot, c):
                    if c == 0:
                        done(pe, "lo", i)
                    for q in range(NE // 2):
                        done(pe, "acc", i, (c - 1) * NE + 2 * q + 2)
                        n = 0
                        for x, w in ((x_hi, w_hi), (x_hi, w_lo), (x_lo, w_hi)):
                            for k in range(KD):
                                t = pe.matmul(ps[:, 4 + q, :], x[:, slot, k, c * P:(c + 1) * P],
                                              w[:, k, 2 * q:2 * q + 2, :].rearrange("p e d -> p (e d)"),
                                              start=(n == 0), stop=(n == 3 * KD - 1))
                                n += 1
                        S["yp"].inc(t)
                    done(pe, "gT", i)
                    done(pe, "bias", i, c - 1)
                    S["biasp"].inc(pe.matmul(ps[:, 2 + c % 2, 0:D], gT[:, slot, c * P:(c + 1) * P], eb[:, :], start=True, stop=True))

                def step(i, slot, front):
                    products(i, slot, 0)
                    products(i, slot, 1)
                    if front:
                        turn(i + 1)
                    products(i, slot, 2)
                    if front:
                        router(i + 1)
                    products(i, slot, 3)
                    if front:
                        turn_gates(i + 1, 1 - slot)

                def first():
                    turn(0)
                    router(0)
                    turn_gates(0, 0)

                steps(pe, first, step)


_INS = ['L0_attn_x', 'L0_attn_W_in', 'L0_attn_conv_w', 'L0_attn_W_x', 'L0_attn_A_log', 'L0_attn_W_out',
        'L0_ffn_f1', 'L0_ffn_f2', 'L1_attn_b_out', 'L1_ffn_router_w', 'L1_ffn_router_b', 'L1_ffn_expert_w',
        'L1_ffn_expert_b']


def laid_out(inputs):
    w_qkv = np.asarray(inputs["L1_attn_w_qkv"])
    rf = np.asarray(inputs["L1_attn_random_features"])
    rfb = np.zeros((P, 3 * 6 * NF), np.float32)
    for j, heads in enumerate(HEADS_OF):
        for n, _ in enumerate(heads):
            c = (j * 6 + n) * NF
            rfb[n * HD:(n + 1) * HD, c:c + NF] = rf.T
            rfb[NORM_ROW[j] + n, c:c + NF] = -float(NF) ** 0.5
    ctrl = np.asarray(inputs["L0_ffn_controller"]).reshape(D, ES)
    return {
        "conv_b_cols": np.asarray(inputs["L0_attn_conv_b"]).reshape(KI, P).T,
        "d_cols": np.asarray(inputs["L0_attn_D_param"]).reshape(KI, P).T,
        "ctrl_twice": np.concatenate([ctrl, ctrl], 1),
        "ffn_bias_cols": np.asarray(inputs["L0_ffn_bias"]).reshape(PAIRS, P).T,
        "w_qkv_T": w_qkv.T,
        "w_out_T": np.asarray(inputs["L1_attn_w_out"]).T,
        "rf_blocks": rfb,
    }


def kernel(**inputs):
    import numpy as _np
    import concourse.bacc as _bacc
    from concourse import mybir as _mybir
    from concourse.bass_utils import run_bass_kernel_spmd as _run

    nc = _bacc.Bacc("TRN2", target_bir_lowering=False, num_devices=1)
    arrays, a = {}, {}
    consts, at = shape_constants()
    given = {n: inputs[n] for n in _INS}
    for name, v in {**given, **laid_out(inputs), "consts": consts}.items():
        v = _np.ascontiguousarray(v)
        arrays[f"in_{name}"] = v
        a[name] = nc.dram_tensor(f"in_{name}", v.shape, _mybir.dt.from_np(v.dtype), kind="ExternalInput").ap()
    out = nc.dram_tensor("out", (B, L, D), F32, kind="ExternalOutput").ap()
    scratch = nc.dram_tensor("inter", (GROUPS, ES, D), F32, kind="Internal").ap()
    build(nc, a, out, a["consts"], at, scratch)
    r = _run(nc, [arrays], core_ids=[0])
    return r.results[0]["out"]
```
